# Optimizing a Trainium2 kernel written in Bass

```python
import numpy as np
import jax
import jax.numpy as jnp

def _softmax(x, axis=-1):
    return jax.nn.softmax(x, axis=axis)

def _gelu(x):
    return jax.nn.gelu(x, approximate=True)

def _silu(x):
    return jax.nn.silu(x)

def _sigmoid(x):
    return jax.nn.sigmoid(x)

def _layernorm(x, axis=-1, eps=1e-05):
    m = jnp.mean(x, axis=axis, keepdims=True)
    v = jnp.var(x, axis=axis, keepdims=True)
    return (x - m) / jnp.sqrt(v + eps)

def _scatter_add(tgt, idx, src, axis=0):
    return tgt.at[idx].add(src)

def _segment_sum(src, seg, n):
    return jax.ops.segment_sum(src, seg, n)
kernel_name = 'mk_seq_preln_d2_jaxref_r8_84984c'

def setup_inputs(seed: int=0):
    np.random.seed(seed)
    _w = jnp.asarray

    def _L0_attn_setup():
        import jax, jax.numpy as jnp
        import numpy as np
        DIM = 256
        HID = 512
        STATE = 128
        HEADS = 64
        GROUPS = 1
        CONV = 4
        CHUNK = 32
        HEAD_DIM = HID // HEADS
        CONV_DIM = HID + 2 * GROUPS * STATE
        D_IN = 2 * HID + 2 * GROUPS * STATE + HEADS

        def _causal_conv1d_silu(xBC, w):
            b, s, c = xBC.shape
            k = w.shape[1]
            xp = jnp.pad(xBC, ((0, 0), (k - 1, 0), (0, 0)))
            out = xp[:, 0:s, :] * w[:, 0]
            for i in range(1, k):
                out = out + xp[:, i:i + s, :] * w[:, i]
            return jax.nn.silu(out)

        def _ssd_chunk_scan(x, dt, A, B, C, D, chunk):
            b, s, h, p = x.shape
            g, n = (B.shape[2], B.shape[3])
            c = s // chunk
            Bh = jnp.repeat(B, h // g, axis=2).reshape(b, c, chunk, h, n)
            Ch = jnp.repeat(C, h // g, axis=2).reshape(b, c, chunk, h, n)
            xr = x.reshape(b, c, chunk, h, p)
            dtr = dt.reshape(b, c, chunk, h)
            dA = dtr * A
            dAc = jnp.cumsum(dA, axis=2)
            seg = dAc[:, :, :, None, :] - dAc[:, :, None, :, :]
            mask = jnp.tril(jnp.ones((chunk, chunk), bool))
            Lmat = jnp.where(mask[None, None, :, :, None], jnp.exp(seg), 0.0)
            xdt = xr * dtr[..., None]
            y_diag = jnp.einsum('bclhn,bcshn,bclsh,bcshp->bclhp', Ch, Bh, Lmat, xdt)
            dA_last = dAc[:, :, -1:, :]
            decay_states = jnp.exp(dA_last - dAc)
            states = jnp.einsum('bclhn,bclh,bclhp->bchpn', Bh, decay_states, xdt)
            chunk_decay = jnp.exp(dA_last[:, :, 0, :])

            def step(carry, inp):
                dec, st = inp
                new = carry * dec[:, :, None, None] + st
                return (new, carry)
            init = jnp.zeros((b, h, p, n), x.dtype)
            _, prev = jax.lax.scan(step, init, (jnp.moveaxis(chunk_decay, 1, 0), jnp.moveaxis(states, 1, 0)))
            prev = jnp.moveaxis(prev, 0, 1)
            y_off = jnp.einsum('bclhn,bclh,bchpn->bclhp', Ch, jnp.exp(dAc), prev)
            y = (y_diag + y_off).reshape(b, s, h, p)
            return y + x * D[None, None, :, None]
        key = jax.random.key(seed)
        ks = jax.random.split(key, 8)
        x = jax.random.normal(ks[0], (1, 512, DIM), dtype=jnp.float32)
        in_proj_w = jax.random.normal(ks[1], (D_IN, DIM), jnp.float32) * DIM ** (-0.5)
        conv_w = jax.random.normal(ks[2], (CONV_DIM, CONV), jnp.float32) * CONV ** (-0.5)
        dt_bias = jnp.log(jnp.expm1(jax.random.uniform(ks[3], (HEADS,), jnp.float32, 0.001, 0.1)))
        A_log = jnp.log(jax.random.uniform(ks[4], (HEADS,), jnp.float32, 1.0, 16.0))
        D = jnp.ones((HEADS,), jnp.float32)
        norm_w = jnp.ones((HID,), jnp.float32)
        out_proj_w = jax.random.normal(ks[5], (DIM, HID), jnp.float32) * HID ** (-0.5)
        return dict(x=x, in_proj_w=in_proj_w, conv_w=conv_w, dt_bias=dt_bias, A_log=A_log, D=D, norm_w=norm_w, out_proj_w=out_proj_w)
    _L0_attn_in = _L0_attn_setup()

    def _L0_ffn_setup():
        import jax, jax.numpy as jnp
        import numpy as np
        H = 256
        I = 176
        E = 8
        TOP_K = 2
        N_SHARED = 2
        I_SH = I * N_SHARED
        NORM_TOPK = True

        def _moe_forward(hidden_states, gate_w, expert_gate, expert_up, expert_down, shared_gate, shared_up, shared_down):
            bsz, seq_len, hdim = hidden_states.shape
            x = hidden_states.reshape(-1, hdim)
            logits = x @ gate_w.T
            probs = jax.nn.softmax(logits, axis=-1)
            routing_weights, selected = jax.lax.top_k(probs, TOP_K)
            if NORM_TOPK:
                routing_weights = routing_weights / (routing_weights.sum(axis=-1, keepdims=True) + 1e-20)
            combine = jnp.sum(jax.nn.one_hot(selected, E, dtype=routing_weights.dtype) * routing_weights[..., None], axis=1)
            g_sh = x @ shared_gate.T
            u_sh = x @ shared_up.T
            out = jax.nn.silu(g_sh) * u_sh @ shared_down.T
            g = jnp.einsum('nh,eih->nei', x, expert_gate)
            u = jnp.einsum('nh,eih->nei', x, expert_up)
            y = jnp.einsum('nei,ehi->neh', jax.nn.silu(g) * u, expert_down)
            out = out + jnp.einsum('neh,ne->nh', y, combine)
            return out.reshape(bsz, seq_len, hdim)
        key = jax.random.key(seed)
        ks = jax.random.split(key, 8)
        s = 0.02
        return {'hidden_states': jax.random.normal(ks[0], (1, 128, H), dtype=jnp.float32), 'gate_w': jax.random.normal(ks[1], (E, H), dtype=jnp.float32) * s, 'expert_gate': jax.random.normal(ks[2], (E, I, H), dtype=jnp.float32) * s, 'expert_up': jax.random.normal(ks[3], (E, I, H), dtype=jnp.float32) * s, 'expert_down': jax.random.normal(ks[4], (E, H, I), dtype=jnp.float32) * s, 'shared_gate': jax.random.normal(ks[5], (I_SH, H), dtype=jnp.float32) * s, 'shared_up': jax.random.normal(ks[6], (I_SH, H), dtype=jnp.float32) * s, 'shared_down': jax.random.normal(ks[7], (H, I_SH), dtype=jnp.float32) * s}
    _L0_ffn_in = _L0_ffn_setup()

    def _L1_attn_setup():
        import jax, jax.numpy as jnp
        import numpy as np
        N_HEADS = 16
        key = jax.random.key(seed)
        ks = jax.random.split(key, 9)
        B, S, D = (2, 256, 256)
        s = 0.02
        return {'X': jax.random.normal(ks[0], (B, S, D), jnp.float32), 'Wq': jax.random.normal(ks[1], (D, D), jnp.float32) * s, 'bq': jax.random.normal(ks[2], (D,), jnp.float32) * s, 'Wk': jax.random.normal(ks[3], (D, D), jnp.float32) * s, 'bk': jax.random.normal(ks[4], (D,), jnp.float32) * s, 'Wv': jax.random.normal(ks[5], (D, D), jnp.float32) * s, 'bv': jax.random.normal(ks[6], (D,), jnp.float32) * s, 'Wo': jax.random.normal(ks[7], (D, D), jnp.float32) * s, 'bo': jax.random.normal(ks[8], (D,), jnp.float32) * s}
    _L1_attn_in = _L1_attn_setup()

    def _L1_ffn_setup():
        import jax, jax.numpy as jnp
        import numpy as np
        ALPHA = 1.702
        LIMIT = 7.0
        TOP_K = 4
        B, S, H = (1, 128, 256)
        E, D = (16, 256)
        key = jax.random.key(seed)
        ks = jax.random.split(key, 7)
        s = 0.02
        return {'hidden_states': jax.random.normal(ks[0], (B, S, H), dtype=jnp.float32), 'router_weight': jax.random.normal(ks[1], (E, H), dtype=jnp.float32) * s, 'router_bias': jax.random.normal(ks[2], (E,), dtype=jnp.float32) * s, 'gate_up_proj': jax.random.normal(ks[3], (E, H, 2 * D), dtype=jnp.float32) * s, 'gate_up_proj_bias': jax.random.normal(ks[4], (E, 2 * D), dtype=jnp.float32) * s, 'down_proj': jax.random.normal(ks[5], (E, D, H), dtype=jnp.float32) * s, 'down_proj_bias': jax.random.normal(ks[6], (E, H), dtype=jnp.float32) * s}
    _L1_ffn_in = _L1_ffn_setup()
    _d = {'L0_attn_x': _L0_attn_in['x'], 'L0_attn_in_proj_w': _L0_attn_in['in_proj_w'], 'L0_attn_conv_w': _L0_attn_in['conv_w'], 'L0_attn_dt_bias': _L0_attn_in['dt_bias'], 'L0_attn_A_log': _L0_attn_in['A_log'], 'L0_attn_D': _L0_attn_in['D'], 'L0_attn_norm_w': _L0_attn_in['norm_w'], 'L0_attn_out_proj_w': _L0_attn_in['out_proj_w'], 'L0_ffn_gate_w': _L0_ffn_in['gate_w'], 'L0_ffn_expert_gate': _L0_ffn_in['expert_gate'], 'L0_ffn_expert_up': _L0_ffn_in['expert_up'], 'L0_ffn_expert_down': _L0_ffn_in['expert_down'], 'L0_ffn_shared_gate': _L0_ffn_in['shared_gate'], 'L0_ffn_shared_up': _L0_ffn_in['shared_up'], 'L0_ffn_shared_down': _L0_ffn_in['shared_down'], 'L1_attn_Wq': _L1_attn_in['Wq'], 'L1_attn_bq': _L1_attn_in['bq'], 'L1_attn_Wk': _L1_attn_in['Wk'], 'L1_attn_bk': _L1_attn_in['bk'], 'L1_attn_Wv': _L1_attn_in['Wv'], 'L1_attn_bv': _L1_attn_in['bv'], 'L1_attn_Wo': _L1_attn_in['Wo'], 'L1_attn_bo': _L1_attn_in['bo'], 'L1_ffn_router_weight': _L1_ffn_in['router_weight'], 'L1_ffn_router_bias': _L1_ffn_in['router_bias'], 'L1_ffn_gate_up_proj': _L1_ffn_in['gate_up_proj'], 'L1_ffn_gate_up_proj_bias': _L1_ffn_in['gate_up_proj_bias'], 'L1_ffn_down_proj': _L1_ffn_in['down_proj'], 'L1_ffn_down_proj_bias': _L1_ffn_in['down_proj_bias']}
    _x0 = _d['L0_attn_x']
    _d['L0_attn_x'] = jax.random.normal(jax.random.fold_in(jax.random.key(seed), 1), (4, 256, 256), dtype=_x0.dtype)
    del _x0
    return _d

def reference(L0_attn_x, L0_attn_in_proj_w, L0_attn_conv_w, L0_attn_dt_bias, L0_attn_A_log, L0_attn_D, L0_attn_norm_w, L0_attn_out_proj_w, L0_ffn_gate_w, L0_ffn_expert_gate, L0_ffn_expert_up, L0_ffn_expert_down, L0_ffn_shared_gate, L0_ffn_shared_up, L0_ffn_shared_down, L1_attn_Wq, L1_attn_bq, L1_attn_Wk, L1_attn_bk, L1_attn_Wv, L1_attn_bv, L1_attn_Wo, L1_attn_bo, L1_ffn_router_weight, L1_ffn_router_bias, L1_ffn_gate_up_proj, L1_ffn_gate_up_proj_bias, L1_ffn_down_proj, L1_ffn_down_proj_bias):

    def _L0_attn_ref(x, in_proj_w, conv_w, dt_bias, A_log, D, norm_w, out_proj_w):
        import jax, jax.numpy as jnp
        import numpy as np
        DIM = 256
        HID = 512
        STATE = 128
        HEADS = 64
        GROUPS = 1
        CONV = 4
        CHUNK = 32
        HEAD_DIM = HID // HEADS
        CONV_DIM = HID + 2 * GROUPS * STATE
        D_IN = 2 * HID + 2 * GROUPS * STATE + HEADS

        def _causal_conv1d_silu(xBC, w):
            b, s, c = xBC.shape
            k = w.shape[1]
            xp = jnp.pad(xBC, ((0, 0), (k - 1, 0), (0, 0)))
            out = xp[:, 0:s, :] * w[:, 0]
            for i in range(1, k):
                out = out + xp[:, i:i + s, :] * w[:, i]
            return jax.nn.silu(out)

        def _ssd_chunk_scan(x, dt, A, B, C, D, chunk):
            b, s, h, p = x.shape
            g, n = (B.shape[2], B.shape[3])
            c = s // chunk
            Bh = jnp.repeat(B, h // g, axis=2).reshape(b, c, chunk, h, n)
            Ch = jnp.repeat(C, h // g, axis=2).reshape(b, c, chunk, h, n)
            xr = x.reshape(b, c, chunk, h, p)
            dtr = dt.reshape(b, c, chunk, h)
            dA = dtr * A
            dAc = jnp.cumsum(dA, axis=2)
            seg = dAc[:, :, :, None, :] - dAc[:, :, None, :, :]
            mask = jnp.tril(jnp.ones((chunk, chunk), bool))
            Lmat = jnp.where(mask[None, None, :, :, None], jnp.exp(seg), 0.0)
            xdt = xr * dtr[..., None]
            y_diag = jnp.einsum('bclhn,bcshn,bclsh,bcshp->bclhp', Ch, Bh, Lmat, xdt)
            dA_last = dAc[:, :, -1:, :]
            decay_states = jnp.exp(dA_last - dAc)
            states = jnp.einsum('bclhn,bclh,bclhp->bchpn', Bh, decay_states, xdt)
            chunk_decay = jnp.exp(dA_last[:, :, 0, :])

            def step(carry, inp):
                dec, st = inp
                new = carry * dec[:, :, None, None] + st
                return (new, carry)
            init = jnp.zeros((b, h, p, n), x.dtype)
            _, prev = jax.lax.scan(step, init, (jnp.moveaxis(chunk_decay, 1, 0), jnp.moveaxis(states, 1, 0)))
            prev = jnp.moveaxis(prev, 0, 1)
            y_off = jnp.einsum('bclhn,bclh,bchpn->bclhp', Ch, jnp.exp(dAc), prev)
            y = (y_diag + y_off).reshape(b, s, h, p)
            return y + x * D[None, None, :, None]
        b, s, _ = x.shape
        zxbcdt = x @ in_proj_w.T
        z = zxbcdt[..., :HID]
        xBC = zxbcdt[..., HID:HID + CONV_DIM]
        dt = zxbcdt[..., HID + CONV_DIM:]
        xBC = _causal_conv1d_silu(xBC, conv_w)
        xh = xBC[..., :HID].reshape(b, s, HEADS, HEAD_DIM)
        B = xBC[..., HID:HID + GROUPS * STATE].reshape(b, s, GROUPS, STATE)
        C = xBC[..., HID + GROUPS * STATE:].reshape(b, s, GROUPS, STATE)
        A = -jnp.exp(A_log)
        dt = jax.nn.softplus(dt + dt_bias)
        y = _ssd_chunk_scan(xh, dt, A, B, C, D, CHUNK)
        y = y.reshape(b, s, HID)
        y = y * jax.nn.silu(z)
        y = y * jax.lax.rsqrt(jnp.mean(y * y, axis=-1, keepdims=True) + 1e-05) * norm_w
        return y @ out_proj_w.T

    def _L0_ffn_ref(hidden_states, gate_w, expert_gate, expert_up, expert_down, shared_gate, shared_up, shared_down):
        import jax, jax.numpy as jnp
        import numpy as np
        H = 256
        I = 176
        E = 8
        TOP_K = 2
        N_SHARED = 2
        I_SH = I * N_SHARED
        NORM_TOPK = True

        def _moe_forward(hidden_states, gate_w, expert_gate, expert_up, expert_down, shared_gate, shared_up, shared_down):
            bsz, seq_len, hdim = hidden_states.shape
            x = hidden_states.reshape(-1, hdim)
            logits = x @ gate_w.T
            probs = jax.nn.softmax(logits, axis=-1)
            routing_weights, selected = jax.lax.top_k(probs, TOP_K)
            if NORM_TOPK:
                routing_weights = routing_weights / (routing_weights.sum(axis=-1, keepdims=True) + 1e-20)
            combine = jnp.sum(jax.nn.one_hot(selected, E, dtype=routing_weights.dtype) * routing_weights[..., None], axis=1)
            g_sh = x @ shared_gate.T
            u_sh = x @ shared_up.T
            out = jax.nn.silu(g_sh) * u_sh @ shared_down.T
            g = jnp.einsum('nh,eih->nei', x, expert_gate)
            u = jnp.einsum('nh,eih->nei', x, expert_up)
            y = jnp.einsum('nei,ehi->neh', jax.nn.silu(g) * u, expert_down)
            out = out + jnp.einsum('neh,ne->nh', y, combine)
            return out.reshape(bsz, seq_len, hdim)
        return _moe_forward(hidden_states, gate_w, expert_gate, expert_up, expert_down, shared_gate, shared_up, shared_down)

    def _L1_attn_ref(X, Wq, bq, Wk, bk, Wv, bv, Wo, bo):
        import jax, jax.numpy as jnp
        import numpy as np
        N_HEADS = 16
        B, S, D = X.shape
        H = N_HEADS
        d_head = D // H
        scale = jnp.asarray(1.0 / np.sqrt(np.sqrt(d_head)), X.dtype)
        Q = (X @ Wq.T + bq).reshape(B, S, H, d_head) * scale
        K = (X @ Wk.T + bk).reshape(B, S, H, d_head) * scale
        V = (X @ Wv.T + bv).reshape(B, S, H, d_head)
        scores = jnp.einsum('bqhd,bkhd->bhqk', Q, K)
        causal = jnp.tril(jnp.ones((S, S), bool))
        scores = jnp.where(causal[None, None], scores, -jnp.inf)
        attn = jax.nn.softmax(scores.astype(jnp.float32), axis=-1).astype(X.dtype)
        out = jnp.einsum('bhqk,bkhd->bqhd', attn, V).reshape(B, S, D)
        return out @ Wo.T + bo

    def _L1_ffn_ref(hidden_states, router_weight, router_bias, gate_up_proj, gate_up_proj_bias, down_proj, down_proj_bias):
        import jax, jax.numpy as jnp
        import numpy as np
        ALPHA = 1.702
        LIMIT = 7.0
        TOP_K = 4
        B, S, H = (1, 128, 256)
        E, D = (16, 256)
        batch, seq, hdim = hidden_states.shape
        x = hidden_states.reshape(-1, hdim)
        T = x.shape[0]
        logits = x @ router_weight.T + router_bias
        top_val, top_idx = jax.lax.top_k(logits, TOP_K)
        top_val = jax.nn.softmax(top_val, axis=-1)
        router_scores = jnp.zeros_like(logits).at[jnp.arange(T)[:, None], top_idx].set(top_val)
        gate_up = jnp.einsum('th,ehd->etd', x, gate_up_proj) + gate_up_proj_bias[:, None, :]
        gate = gate_up[..., ::2]
        up = gate_up[..., 1::2]
        gate = jnp.minimum(gate, LIMIT)
        up = jnp.clip(up, -LIMIT, LIMIT)
        glu = gate * jax.nn.sigmoid(gate * ALPHA)
        out = jnp.einsum('etd,edh->eth', (up + 1.0) * glu, down_proj) + down_proj_bias[:, None, :]
        out = out * router_scores.T[:, :, None]
        out = out.sum(axis=0)
        return out.reshape(batch, seq, hdim)
    x = L0_attn_x
    x = x + _L0_attn_ref(_layernorm(x, axis=-1), L0_attn_in_proj_w, L0_attn_conv_w, L0_attn_dt_bias, L0_attn_A_log, L0_attn_D, L0_attn_norm_w, L0_attn_out_proj_w)
    x = x + _L0_ffn_ref(_layernorm(x, axis=-1), L0_ffn_gate_w, L0_ffn_expert_gate, L0_ffn_expert_up, L0_ffn_expert_down, L0_ffn_shared_gate, L0_ffn_shared_up, L0_ffn_shared_down)
    x = x + _L1_attn_ref(_layernorm(x, axis=-1), L1_attn_Wq, L1_attn_bq, L1_attn_Wk, L1_attn_bk, L1_attn_Wv, L1_attn_bv, L1_attn_Wo, L1_attn_bo)
    x = x + _L1_ffn_ref(_layernorm(x, axis=-1), L1_ffn_router_weight, L1_ffn_router_bias, L1_ffn_gate_up_proj, L1_ffn_gate_up_proj_bias, L1_ffn_down_proj, L1_ffn_down_proj_bias)
    return x

_drawn_inputs = setup_inputs


def setup_inputs(seed=0):
    import zlib

    import numpy as np

    out = dict(_drawn_inputs(seed))
    spreads = {'L0_attn_D': (1.0, 0.2), 'L0_attn_norm_w': (1.0, 0.2)}
    factors = {'L0_ffn_gate_w': 8.0,
     'L0_ffn_expert_gate': 8.0,
     'L0_ffn_expert_up': 7.928,
     'L0_ffn_expert_down': 7.923,
     'L0_ffn_shared_gate': 4.08,
     'L0_ffn_shared_up': 3.996,
     'L0_ffn_shared_down': 4.025,
     'L1_attn_Wq': 8.0,
     'L1_attn_bq': 8.0,
     'L1_attn_Wk': 8.0,
     'L1_attn_bk': 64.0,
     'L1_attn_Wv': 4.098,
     'L1_attn_bv': 8.0,
     'L1_attn_Wo': 3.919,
     'L1_attn_bo': 22.85,
     'L1_ffn_router_weight': 2.986,
     'L1_ffn_router_bias': 37.536,
     'L1_ffn_gate_up_proj': 2.774,
     'L1_ffn_gate_up_proj_bias': 44.576,
     'L1_ffn_down_proj': 2.696,
     'L1_ffn_down_proj_bias': 41.242}
    for name, (base, spread) in spreads.items():
        noise = np.random.default_rng([zlib.crc32(name.encode()), seed]).standard_normal(out[name].shape)
        drawn = base * np.exp(spread * noise) if base else spread * noise
        out[name] = jnp.asarray(drawn.astype(out[name].dtype))
    for name, factor in factors.items():
        out[name] = (out[name] * factor).astype(out[name].dtype)
    return out
```

```python
from contextlib import ExitStack

import concourse.bass as bass
from concourse import mybir

F32 = mybir.dt.float32
F16 = mybir.dt.float16
ALU = mybir.AluOpType
ACT = mybir.ActivationFunctionType
AX = mybir.AxisListType

P = 128
TOKENS = 1024
DIM = 256
TILES = TOKENS // P
KT = DIM // P
HALF = 512
HALVES = TOKENS // HALF
EPS = 1e-5

HID = 512
HEADS = 64
HEAD_DIM = HID // HEADS
CONV_BLOCKS = 6
XB = HID // P
TAPS = 4
SEQ = 256
LEVELS = 7
Z0, X0, DT0 = 0, HID, HID + 768


class Kit:

    def __init__(self, nc, stack, taken):
        self.nc, self.stack, self.taken = nc, stack, taken

    def part(self, stack):
        return Kit(self.nc, stack, self.taken)

    def sb(self, name, shape, dtype=F32):
        return self.stack.enter_context(self.nc.sbuf_tensor(name, shape, dtype))

    def sem(self, name):
        self.taken.append(self.nc.alloc_semaphore(name))
        return self.taken[-1]

    def retire_semaphores(self):
        with self.nc.Block() as block:
            @block.sync
            def _(sp):
                for sem in self.taken:
                    sp.sem_clear(sem)
        for sem in self.taken:
            self.nc.release_semaphore(sem)
        self.taken.clear()


def bc(ap, axis, n):
    ap = ap.unsqueeze(axis)
    shape = list(ap.shape)
    shape[axis] = n
    return ap.broadcast_to(shape)


class LayerNorm:

    def __init__(self, nc, kit, name, x, bank, ident):
        self.nc, self.x, self.bank, self.ident = nc, x, bank, ident
        self.stats = kit.sb(name + "_stats", [P, TILES, 6])
        self.mv = kit.sb(name + "_mean_var", [P, TILES, 2])
        self.var = kit.sb(name + "_var", [P, TILES])
        self.half_power = kit.sb(name + "_minus_half", [P, TILES])
        self.rstd = kit.sb(name + "_rstd", [P, TILES])
        self.xn = kit.sb(name + "_xn", [P, TILES, DIM])
        self.s_stats = kit.sem(name + "_stats_done")
        self.s_mv = kit.sem(name + "_mean_var_done")
        self.s_rstd = kit.sem(name + "_rstd_done")
        self.s_pool = kit.sem(name + "_pool_step")
        self.s_xn = kit.sem(name + "_xn_done")
        self.s_turned = kit.sem(name + "_turned")
        self.s_hi = kit.sem(name + "_hi_done")
        self.s_lo = kit.sem(name + "_lo_done")

    def vector_stats(self, dve, arrived=None):
        for i in range(TILES):
            if arrived is not None:
                arrived(i)
            dve.bn_stats(self.stats[:, i, :], self.x[:, i, :]).then_inc(self.s_stats, 1)
        for i in range(TILES):
            dve.wait_ge(self.s_stats, i + 1)
            dve.bn_aggr(self.mv[:, i, :], self.stats[:, i, :]).then_inc(self.s_mv, 1)

    def pool(self, pool):
        pool.memset(self.half_power[:], -0.5).then_inc(self.s_pool, 1)
        pool.wait_ge(self.s_mv, TILES)
        pool.tensor_scalar(self.var[:], self.mv[:, :, 1], EPS, 1.0, ALU.add, ALU.mult).then_inc(self.s_pool, 1)
        pool.wait_ge(self.s_pool, 2)
        pool.tensor_tensor(self.rstd[:], self.var[:], self.half_power[:], ALU.pow).then_inc(self.s_rstd, 1)

    def vector_normalize(self, dve):
        dve.wait_ge(self.s_rstd, 1)
        for i in range(TILES):
            dve.tensor_scalar(self.xn[:, i, :], self.x[:, i, :], self.mv[:, i, 0:1], self.rstd[:, i:i + 1],
                              ALU.subtract, ALU.mult).then_inc(self.s_xn, 1)

    def tensor(self, pe):
        for h in range(HALVES):
            for i in range(4 * h, 4 * h + 4):
                pe.wait_ge(self.s_xn, i + 1)
                for k in range(KT):
                    m = pe.transpose(self.bank[2 * h + k][:, P * (i % 4):P * (i % 4) + P],
                                     self.xn[:, i, P * k:P * k + P], self.ident)
            m.then_inc(self.s_turned, 1)

    def scalar_hi(self, act, hi, banks=range(4)):
        for b in banks:
            act.wait_ge(self.s_turned, b // 2 + 1)
            act.activation(hi[:, b % 2, HALF * (b // 2):HALF * (b // 2) + HALF], self.bank[b][:],
                           ACT.Copy).then_inc(self.s_hi, 1)

    def vector_lo(self, dve, hi, lo, banks=range(4)):
        for b in banks:
            dve.wait_ge(self.s_hi, b + 1)
            sl = slice(HALF * (b // 2), HALF * (b // 2) + HALF)
            dve.tensor_tensor(lo[:, b % 2, sl], self.bank[b][:], hi[:, b % 2, sl],
                              ALU.subtract).then_inc(self.s_lo, 1)


def three_products(pe, out, w_hi, w_lo, x_hi, x_lo, start, stop, **kw):
    pe.matmul(out, w_hi, x_hi, start=start, stop=False, **kw)
    pe.matmul(out, w_hi, x_lo, start=False, stop=False, **kw)
    return pe.matmul(out, w_lo, x_hi, start=False, stop=stop, **kw)


def mamba(nc, G):
    x, bank, ident = G["x"], G["bank"], G["ident"]
    with ExitStack() as stack:
        kit = Kit(nc, stack, [])
        xbc = kit.sb("xbc", [P, CONV_BLOCKS, TOKENS])
        zs = kit.sb("silu_z", [P, TILES, HID])
        dt = kit.sb("dt", [P, TILES, HEADS])
        d_a = kit.sb("dt_times_A", [P, TILES, HEADS])
        d_skip = kit.sb("D_rows", [P, HEADS])
        norm_w = kit.sb("norm_w", [P, XB])
        w_out = kit.sb("w_out", [P, XB, DIM])
        cum_masks = kit.sb("cum_masks", [P, 2 * (LEVELS + 1), P])
        pair_masks = kit.sb("pair_masks", [P, LEVELS, P])
        s_ssd_consts = kit.sem("ssd_consts_loaded")
        with ExitStack() as inner:
            mamba_projections(nc, G, kit.part(inner), x, bank, ident, xbc, zs, dt, d_a, d_skip, norm_w, w_out,
                              cum_masks, pair_masks, s_ssd_consts)
        with ExitStack() as inner:
            mamba_scan(nc, G, kit.part(inner), x, bank, ident, xbc, zs, dt, d_a, d_skip, norm_w, w_out,
                       cum_masks, pair_masks, s_ssd_consts)
        kit.retire_semaphores()


def mamba_projections(nc, G, kit, x, bank, ident, xbc, zs, dt, d_a, d_skip, norm_w, w_out, cum_masks,
                      pair_masks, s_ssd_consts):
    D_IN = 2 * HID + 256 + HEADS
    w_raw = kit.sb("w_in_raw", [P, KT, D_IN])
    w_hi = kit.sb("w_in_hi", [P, KT, D_IN], F16)
    w_lo = kit.sb("w_in_lo", [P, KT, D_IN], F16)
    xt_hi = kit.sb("xt_hi", [P, KT, TOKENS], F16)
    xt_lo = kit.sb("xt_lo", [P, KT, TOKENS], F16)
    conv_w = kit.sb("conv_w", [P, CONV_BLOCKS, TAPS])
    dt_bias = kit.sb("dt_bias_rows", [P, HEADS])
    a_log = kit.sb("A_log_rows", [P, HEADS])
    a_exp = kit.sb("A_exp_rows", [P, HEADS])
    dt_v = kit.sb("dt_shifted", [P, TILES, HEADS])
    dt_e = kit.sb("dt_exp", [P, TILES, HEADS])
    dt_l = kit.sb("dt_log", [P, TILES, HEADS])
    ln = LayerNorm(nc, kit, "ln0", x, bank, ident)
    s_x = [kit.sem(f"x_tile{i}_loaded") for i in range(TILES)]
    s_w = kit.sem("w_in_loaded")
    s_small = kit.sem("small_loaded")
    s_w_hi = kit.sem("w_in_hi_done")
    s_w_lo = kit.sem("w_in_lo_done")
    s_mm = kit.sem("projected")
    s_dt_mm = kit.sem("dt_projected")
    s_tap0 = kit.sem("first_tap_done")
    s_taps = kit.sem("tap_done")
    s_silu = kit.sem("silu_x_done")
    s_z = kit.sem("silu_z_done")
    s_dt = kit.sem("dt_step")
    UNITS = CONV_BLOCKS * HALVES
    SMALL = 5

    def mm_bank(u):
        return bank[4 + u % 3]

    with nc.Block() as block:
        @block.sync
        def _(sp):
            for i in range(TILES):
                sp.dma_start(x[:, i, :], G["x_in"][P * i:P * i + P, :]).then_inc(s_x[i], 16)
            sp.dma_start(conv_w[:], G["conv_w"].rearrange("(j p) t -> p j t", p=P)).then_inc(s_small, 16)
            sp.dma_start(dt_bias[:], G["dt_bias"].partition_broadcast(P)).then_inc(s_small, 16)
            sp.dma_start(a_log[:], G["A_log"].partition_broadcast(P)).then_inc(s_small, 16)
            sp.dma_start(d_skip[:], G["D"].partition_broadcast(P)).then_inc(s_small, 16)
            sp.dma_start(norm_w[:], G["norm_w"]).then_inc(s_small, 16)
            sp.dma_start(cum_masks[:], G["cum_masks"]).then_inc(s_ssd_consts, 16)
            sp.dma_start(pair_masks[:], G["pair_masks"]).then_inc(s_ssd_consts, 16)
            sp.dma_start(w_out[:], G["w_out"].rearrange("(j p) n -> p j n", p=P)).then_inc(s_ssd_consts, 16)

        @block.gpsimd
        def _(pool):
            ln.pool(pool)

        @block.scalar
        def _(act):
            act.dma_start(ident, G["ident_in"]).then_inc(G["s_ident"], 16)
            act.dma_start(w_raw[:], G["w_in"].rearrange("(k p) n -> p k n", p=P)).then_inc(s_w, 16)
            act.wait_ge(s_w, 16)
            for k in range(KT):
                act.activation(w_hi[:, k, :], w_raw[:, k, :], ACT.Copy).then_inc(s_w_hi, 1)
            ln.scalar_hi(act, xt_hi)
            act.wait_ge(s_small, 16 * SMALL)

            def first_tap(u):
                fb, h = u % CONV_BLOCKS, u // CONV_BLOCKS
                act.wait_ge(s_mm, u + 1)
                act.activation(xbc[:, fb, HALF * h:HALF * h + HALF], mm_bank(u)[:], ACT.Copy,
                               scale=conv_w[:, fb, TAPS - 1:TAPS]).then_inc(s_tap0, 1)

            def silu_x(u):
                fb, h = u % CONV_BLOCKS, u // CONV_BLOCKS
                act.wait_ge(s_taps, 3 * (u + 1))
                act.activation(xbc[:, fb, HALF * h:HALF * h + HALF], xbc[:, fb, HALF * h:HALF * h + HALF],
                               ACT.Silu).then_inc(s_silu, 1)

            for u in range(UNITS):
                first_tap(u)
                if u >= 2:
                    silu_x(u - 2)
            silu_x(UNITS - 2)
            silu_x(UNITS - 1)
            for i in range(TILES):
                act.wait_ge(s_mm, UNITS + i + 1)
                act.activation(zs[:, i, :], mm_bank(UNITS + i)[:], ACT.Silu).then_inc(s_z, 1)
            act.activation(a_exp[:], a_log[:], ACT.Exp).then_inc(s_dt, 1)
            act.wait_ge(s_dt, 2)
            act.activation(dt_e[:], dt_v[:], ACT.Abs).then_inc(s_dt, 1)
            act.wait_ge(s_dt, 3)
            act.activation(dt_e[:], dt_e[:], ACT.Exp, scale=-1.0).then_inc(s_dt, 1)
            act.wait_ge(s_dt, 4)
            act.activation(dt_l[:], dt_e[:], ACT.Ln, bias=1.0).then_inc(s_dt, 1)

        @block.tensor
        def _(pe):
            pe.wait_ge(G["s_ident"], 16)
            ln.tensor(pe)
            pe.wait_ge(s_w_lo, KT)
            for u in range(UNITS):
                fb, h = u % CONV_BLOCKS, u // CONV_BLOCKS
                pe.wait_ge(ln.s_lo, 2 * (h + 1))
                if u >= 3:
                    pe.wait_ge(s_taps, 3 * (u - 2))
                for k in range(KT):
                    c = slice(X0 + P * fb, X0 + P * fb + P)
                    t = slice(HALF * h, HALF * h + HALF)
                    m = three_products(pe, mm_bank(u)[:], w_hi[:, k, c], w_lo[:, k, c], xt_hi[:, k, t],
                                       xt_lo[:, k, t], k == 0, k == KT - 1)
                m.then_inc(s_mm, 1)
            for i in range(TILES):
                u = UNITS + i
                if i < 3:
                    pe.wait_ge(s_taps, 3 * (u - 2))
                else:
                    pe.wait_ge(s_z, i - 2)
                t = slice(P * i, P * i + P)
                for k in range(KT):
                    m = three_products(pe, mm_bank(u)[:], xt_hi[:, k, t], xt_lo[:, k, t], w_hi[:, k, Z0:Z0 + HID],
                                       w_lo[:, k, Z0:Z0 + HID], k == 0, k == KT - 1)
                m.then_inc(s_mm, 1)
                for k in range(KT):
                    m = three_products(pe, bank[7][:, HEADS * i:HEADS * i + HEADS], xt_hi[:, k, t], xt_lo[:, k, t],
                                       w_hi[:, k, DT0:D_IN], w_lo[:, k, DT0:D_IN], k == 0, k == KT - 1)
            m.then_inc(s_dt_mm, 1)

        @block.vector
        def _(dve):
            ln.vector_stats(dve, lambda i: dve.wait_ge(s_x[i], 16))
            ln.vector_normalize(dve)
            for k in range(KT):
                dve.wait_ge(s_w_hi, k + 1)
                dve.tensor_tensor(w_lo[:, k, :], w_raw[:, k, :], w_hi[:, k, :], ALU.subtract).then_inc(s_w_lo, 1)
            ln.vector_lo(dve, xt_hi, xt_lo)
            for u in range(UNITS):
                fb, h = u % CONV_BLOCKS, u // CONV_BLOCKS
                dve.wait_ge(s_tap0, u + 1)
                src = mm_bank(u)[:].rearrange("p (b s) -> p b s", s=SEQ)
                acc = xbc[:, fb, HALF * h:HALF * h + HALF].rearrange("p (b s) -> p b s", s=SEQ)
                for tap in range(1, TAPS):
                    if tap > 1:
                        dve.wait_ge(s_taps, 3 * u + tap - 1)
                    dve.scalar_tensor_tensor(acc[:, :, tap:], src[:, :, :SEQ - tap],
                                             conv_w[:, fb, TAPS - 1 - tap:TAPS - tap], acc[:, :, tap:],
                                             ALU.mult, ALU.add).then_inc(s_taps, 1)
            dve.wait_ge(s_dt_mm, 1)
            dve.wait_ge(s_dt, 1)
            dve.tensor_tensor(dt_v[:], bank[7][:].rearrange("p (t h) -> p t h", h=HEADS),
                              bc(dt_bias[:], 1, TILES), ALU.add).then_inc(s_dt, 1)
            dve.wait_ge(s_dt, 5)
            dve.scalar_tensor_tensor(dt[:], dt_v[:], 0.0, dt_l[:], ALU.max, ALU.add).then_inc(s_dt, 1)
            dve.wait_ge(s_dt, 6)
            dve.scalar_tensor_tensor(d_a[:], dt[:], -1.0, bc(a_exp[:], 1, TILES), ALU.mult,
                                     ALU.mult).then_inc(s_dt, 1)
            dve.wait_ge(s_dt, 7)


def mamba_scan(nc, G, kit, x, bank, ident, xbc, zs, dt, d_a, d_skip, norm_w, w_out, cum_masks, pair_masks,
               s_ssd_consts):
    SIDES = LEVELS + 1
    fs = kit.sb("source_factors", [P, SIDES, TILES, HEADS])
    fl = kit.sb("target_factors", [P, SIDES, TILES, HEADS])
    x_tok = kit.sb("x_tok", [P, 2, HID])
    scaled = kit.sb("scaled_x", [P, 2, SIDES, HID])
    g_all = kit.sb("g_scores", [P, 2, SEQ])
    g_masked = kit.sb("g_masked", [P, 2, LEVELS, P])
    g_diag = kit.sb("g_diag", [P, TILES])
    junk = kit.sb("diag_products", [P, 2, P])
    coef = kit.sb("diag_coef", [P, 2, HEADS])
    terms = kit.sb("terms", [P, 4, HID])
    y = kit.sb("y", [P, TILES, HID])
    square = kit.sb("squares", [P, 2, HID])
    mean_sq = kit.sb("sum_squares", [P, TILES])
    mean_eps = kit.sb("mean_squares_eps", [P, TILES])
    half_power = kit.sb("minus_half", [P, TILES])
    rstd = kit.sb("rms_rstd", [P, TILES])
    yt = kit.sb("y_turned", [P, 2, XB, P])
    s_cum = kit.sem("cum_done")
    s_fac = kit.sem("factor_exp_done")
    s_fs = kit.sem("source_factor_done")
    s_xt = kit.sem("x_turned")
    s_xtok = kit.sem("x_tok_done")
    s_g = kit.sem("g_done")
    s_gs = kit.sem("g_saved")
    s_gm = kit.sem("g_masked_done")
    s_gd = kit.sem("g_diag_done")
    s_coef = kit.sem("coef_done")
    s_scaled = kit.sem("x_scaled")
    s_lvl = kit.sem("level_product_done")
    s_term = kit.sem("term_done")
    s_y = kit.sem("y_added")
    s_gate = kit.sem("y_gated")
    s_sq = kit.sem("squares_done")
    s_rms = kit.sem("rms_step")
    s_yn = kit.sem("y_normed")
    s_yt = kit.sem("y_turned_done")
    s_yts = kit.sem("y_turned_saved")
    s_out = kit.sem("out_projected")
    s_res = kit.sem("residual_added")

    products = []
    for i in range(TILES):
        products += [(i, k) for k in range(LEVELS)]
        if i % 2:
            products.append((i, LEVELS))
    first = {}
    last = {}
    for n, (i, k) in enumerate(products):
        first.setdefault(i, n)
        last[i] = n
    adds = [n + 2 + i for n, (i, k) in enumerate(products)]
    starts = [first[i] + i for i in range(TILES)]

    def scaled_before(i):
        return 2 * i + (i + 1) // 2

    def bank_of(n):
        return bank[n % 4]

    with nc.Block() as block:
        @block.tensor
        def _(pe):
            pe.wait_ge(s_ssd_consts, 48)
            for m in range(2 * SIDES):
                if m >= 4:
                    pe.wait_ge(s_fac, m - 3)
                pe.matmul(bank[m % 4][:], cum_masks[:, m, :], d_a[:].rearrange("p t h -> p (t h)"),
                          start=True, stop=True).then_inc(s_cum, 1)
            pe.wait_ge(s_fac, 2 * SIDES)

            def turn(i):
                if i >= 1:
                    pe.wait_ge(s_xtok, i)
                for j in range(XB):
                    m = pe.transpose(bank[4][:, P * j:P * j + P], xbc[:, j, P * i:P * i + P], ident)
                m.then_inc(s_xt, 1)
                if i >= 1:
                    pe.wait_ge(s_gs, i)
                n = SEQ if i % 2 == 0 else P
                pe.matmul(bank[5][:, 0:n], xbc[:, XB, P * i:P * i + P], xbc[:, XB + 1, P * i:P * i + n],
                          start=True, stop=True).then_inc(s_g, 1)

            turn(0)
            for n, (i, k) in enumerate(products):
                if n == first[i] and i + 1 < TILES:
                    turn(i + 1)
                if n >= 4:
                    pe.wait_ge(s_term, n - 3)
                if k < LEVELS:
                    if k == 0:
                        pe.wait_ge(s_gm, i + 1)
                        pe.wait_ge(s_scaled, scaled_before(i) + 1)
                    if k == 4:
                        pe.wait_ge(s_scaled, scaled_before(i) + 2)
                    weights, moving = g_masked[:, i % 2, k, :], scaled[:, i % 2, k, :]
                else:
                    pe.wait_ge(s_scaled, scaled_before(i))
                    weights, moving = g_all[:, 0, P:SEQ], scaled[:, 0, LEVELS, :]
                pe.matmul(bank_of(n)[:], weights, moving, start=True, stop=True).then_inc(s_lvl, 1)

        @block.scalar
        def _(act):
            for m in range(2 * SIDES):
                side, k = m // SIDES, m % SIDES
                act.wait_ge(s_cum, m + 1)
                dst = (fs, fl)[side]
                act.activation(dst[:, k, :, :].rearrange("p t h -> p (t h)"), bank[m % 4][:],
                               ACT.Exp).then_inc(s_fac, 1)
            for i in range(TILES):
                act.wait_ge(s_xt, i + 1)
                if i >= 2:
                    act.wait_ge(s_scaled, scaled_before(i - 1))
                    act.wait_ge(s_y, starts[i - 2] + 1)
                act.activation(x_tok[:, i % 2, :], bank[4][:], ACT.Copy).then_inc(s_xtok, 1)
                n = SEQ if i % 2 == 0 else P
                act.wait_ge(s_g, i + 1)
                if i >= 2:
                    act.wait_ge(s_gm, i - 1)
                    act.wait_ge(s_gd, i - 1)
                    act.wait_ge(s_lvl, last[i - 1 if i % 2 == 0 else i - 2] + 1)
                act.activation(g_all[:, i % 2, 0:n], bank[5][:, 0:n], ACT.Copy).then_inc(s_gs, 1)
            for i in range(TILES):
                act.wait_ge(s_gate, i + 1)
                if i >= 2:
                    act.wait_ge(s_sq, i - 1)
                act.activation(square[:, i % 2, :], y[:, i, :], ACT.Square,
                               accum_out=mean_sq[:, i:i + 1]).then_inc(s_sq, 1)
            act.wait_ge(s_rms, 3)
            for i in range(TILES):
                act.activation(y[:, i, :], y[:, i, :], ACT.Copy, scale=rstd[:, i:i + 1]).then_inc(s_yn, 1)

        @block.vector
        def _(dve):
            dtf = dt[:].rearrange("p t h -> p (t h)")
            for k in range(SIDES):
                dve.wait_ge(s_fac, k + 1)
                f = fs[:, k, :, :].rearrange("p t h -> p (t h)")
                dve.tensor_tensor(f, f, dtf, ALU.mult).then_inc(s_fs, 1)
            dve.wait_ge(s_fs, SIDES)

            def scale(i):
                dve.wait_ge(s_xtok, i + 1)
                if i >= 2:
                    dve.wait_ge(s_lvl, last[i - 1 if i % 2 == 0 else i - 2] + 1)
                src = x_tok[:, i % 2, :].rearrange("p (h e) -> p h e", e=HEAD_DIM)
                for lo, hi in ((0, 4), (4, LEVELS)):
                    dve.tensor_tensor(scaled[:, i % 2, lo:hi, :].rearrange("p k (h e) -> p k h e", e=HEAD_DIM),
                                      bc(src, 1, hi - lo), bc(fs[:, lo:hi, i, :], 3, HEAD_DIM),
                                      ALU.mult).then_inc(s_scaled, 1)
                if i % 2 == 0:
                    dve.tensor_tensor(scaled[:, 0, LEVELS, :].rearrange("p (h e) -> p h e", e=HEAD_DIM),
                                      src, bc(fs[:, LEVELS, i, :], 2, HEAD_DIM), ALU.mult).then_inc(s_scaled, 1)

            def diag(i):
                dve.wait_ge(s_gs, i + 1)
                if i >= 2:
                    dve.wait_ge(s_gd, i - 1)
                dve.tensor_tensor_reduce(junk[:, i % 2, :], g_all[:, i % 2, 0:P], ident, 1.0, 0.0, ALU.mult,
                                         ALU.add, g_diag[:, i:i + 1]).then_inc(s_gd, 1)
                dve.wait_ge(s_gd, i + 1)
                if i >= 2:
                    dve.wait_ge(s_y, starts[i - 2] + 1)
                dve.scalar_tensor_tensor(coef[:, i % 2, :], dt[:, i, :], g_diag[:, i:i + 1], d_skip[:], ALU.mult,
                                         ALU.add).then_inc(s_coef, 1)

            scale(0)
            diag(0)
            for n, (i, k) in enumerate(products):
                if n == first[i] and i + 1 < TILES and i % 2 == 0:
                    scale(i + 1)
                    diag(i + 1)
                dve.wait_ge(s_lvl, n + 1)
                if n >= 4:
                    dve.wait_ge(s_y, adds[n - 4])
                dve.tensor_tensor(terms[:, n % 4, :].rearrange("p (h e) -> p h e", e=HEAD_DIM),
                                  bank_of(n)[:].rearrange("p (h e) -> p h e", e=HEAD_DIM),
                                  bc(fl[:, k, i, :], 2, HEAD_DIM), ALU.mult).then_inc(s_term, 1)
                if n == last[i] and i + 1 < TILES and i % 2 == 1:
                    scale(i + 1)
                    diag(i + 1)

        @block.gpsimd
        def _(pool):
            pool.memset(half_power[:], -0.5).then_inc(s_rms, 1)

            def mask(i):
                pool.wait_ge(s_gs, i + 1)
                if i >= 2:
                    pool.wait_ge(s_lvl, last[i - 2] + 1)
                pool.tensor_tensor(g_masked[:, i % 2, :, :], pair_masks[:], bc(g_all[:, i % 2, 0:P], 1, LEVELS),
                                   ALU.mult).then_inc(s_gm, 1)

            pool.wait_ge(s_ssd_consts, 48)
            mask(0)
            for n, (i, k) in enumerate(products):
                if n == first[i]:
                    if i + 1 < TILES:
                        mask(i + 1)
                    pool.wait_ge(s_coef, i + 1)
                    pool.tensor_tensor(y[:, i, :].rearrange("p (h e) -> p h e", e=HEAD_DIM),
                                       x_tok[:, i % 2, :].rearrange("p (h e) -> p h e", e=HEAD_DIM),
                                       bc(coef[:, i % 2, :], 2, HEAD_DIM), ALU.mult).then_inc(s_y, 1)
                pool.wait_ge(s_term, n + 1)
                pool.wait_ge(s_y, adds[n] - 1)
                pool.tensor_tensor(y[:, i, :], y[:, i, :], terms[:, n % 4, :], ALU.add).then_inc(s_y, 1)
                if n == last[i]:
                    pool.wait_ge(s_y, adds[n])
                    pool.tensor_tensor(y[:, i, :], y[:, i, :], zs[:, i, :], ALU.mult).then_inc(s_gate, 1)
            pool.wait_ge(s_sq, TILES)
            pool.tensor_scalar(mean_eps[:], mean_sq[:], 1.0 / HID, EPS, ALU.mult, ALU.add).then_inc(s_rms, 1)
            pool.wait_ge(s_rms, 2)
            pool.tensor_tensor(rstd[:], mean_eps[:], half_power[:], ALU.pow).then_inc(s_rms, 1)

    with nc.Block() as block:
        def project(pe, i):
            pe.wait_ge(s_yts, i + 1)
            if i >= 2:
                pe.wait_ge(s_res, i - 1)
            for j in range(XB):
                m = pe.matmul(bank[2 + i % 2][:, 0:DIM], yt[:, i % 2, j, :], w_out[:, j, :], start=(j == 0),
                              stop=(j == XB - 1))
            m.then_inc(s_out, 1)

        @block.tensor
        def _(pe):
            for i in range(TILES):
                pe.wait_ge(s_yn, i + 1)
                if i >= 2:
                    pe.wait_ge(s_yts, i - 1)
                for j in range(XB):
                    m = pe.transpose(bank[i % 2][:, P * j:P * j + P], y[:, i, P * j:P * j + P], ident)
                m.then_inc(s_yt, 1)
                if i >= 1:
                    project(pe, i - 1)
            project(pe, TILES - 1)

        @block.vector
        def _(dve):
            def residual(i):
                dve.wait_ge(s_out, i + 1)
                dve.tensor_tensor(x[:, i, :], bank[2 + i % 2][:, 0:DIM], x[:, i, :], ALU.add).then_inc(s_res, 1)

            for i in range(TILES):
                dve.wait_ge(s_yt, i + 1)
                if i >= 2:
                    dve.wait_ge(s_out, i - 1)
                dve.tensor_tensor(yt[:, i % 2, :, :], bank[i % 2][:].rearrange("p (j t) -> p j t", t=P),
                                  bc(norm_w[:], 2, P), ALU.mult).then_inc(s_yts, 1)
                if i >= 1:
                    residual(i - 1)
            residual(TILES - 1)
            dve.wait_ge(s_res, TILES)


L0_FEATURES, L0_EXPERTS, L0_TOP = 176, 8, 2
L0_BLOCKS, L0_SCORED = 14, 11
L1_FEATURES, L1_EXPERTS, L1_TOP = 256, 16, 4
L1_BLOCKS = L1_EXPERTS * L1_FEATURES // P
ALPHA, LIMIT = 1.702, 7.0


def moe(nc, G, layer):
    clamped = layer == 1
    name = f"moe{layer}"
    E, TOP = (L1_EXPERTS, L1_TOP) if clamped else (L0_EXPERTS, L0_TOP)
    BLOCKS = L1_BLOCKS if clamped else L0_BLOCKS
    FEATURES = L1_FEATURES if clamped else L0_FEATURES
    x, bank, ident = G["x"], G["bank"], G["ident"]
    w_gu_dram, w_d_dram = G[name + "_gate_up"], G[name + "_down"]
    score_dram = nc.dram_tensor(name + "_scores_dram", (E, TOKENS), F32, kind="Internal").ap()
    with ExitStack() as stack:
        kit = Kit(nc, stack, [])
        xt_hi = kit.sb(name + "_xt_hi", [P, KT, TOKENS], F16)
        xt_lo = kit.sb(name + "_xt_lo", [P, KT, TOKENS], F16)
        raw_gu = kit.sb(name + "_raw_gate_up", [P, 2, 512])
        raw_d = kit.sb(name + "_raw_down", [P, 2, DIM])
        gu_hi = kit.sb(name + "_gate_up_hi", [P, 2, 2, KT, P], F16)
        gu_lo = kit.sb(name + "_gate_up_lo", [P, 2, 2, KT, P], F16)
        d_hi = kit.sb(name + "_down_hi", [P, 2, DIM], F16)
        d_lo = kit.sb(name + "_down_lo", [P, 2, DIM], F16)
        scores = kit.sb(name + "_scores_spread", [P, BLOCKS if not clamped else E, TOKENS])
        r_raw = kit.sb(name + "_router", [P, KT, E])
        r_hi = kit.sb(name + "_router_hi", [P, KT, E], F16)
        r_lo = kit.sb(name + "_router_lo", [P, KT, E], F16)
        lower = kit.sb(name + "_lower_expert", [P, E, E])
        logits = kit.sb(name + "_logits", [P, TILES, E])
        peak = kit.sb(name + "_peak", [P, TILES])
        weight = kit.sb(name + "_weight", [P, TILES, E])
        beats = kit.sb(name + "_beats", [P, TILES, E, E])
        ties = kit.sb(name + "_ties", [P, TILES, E, E])
        rank = kit.sb(name + "_rank", [P, TILES, E])
        total = kit.sb(name + "_total", [P, TILES])
        score_t = kit.sb(name + "_scores_turned", [E, TOKENS])
        gate = kit.sb(name + "_gate", [P, 2, HALF])
        sig = kit.sb(name + "_sigmoid", [P, 2, HALF])
        up = kit.sb(name + "_up", [P, 2, HALF])
        glu = kit.sb(name + "_glu", [P, 2, HALF])
        act_out = kit.sb(name + "_activated", [P, 2, HALF])
        hid = kit.sb(name + "_hidden", [P, 2, HALF])
        h_hi = kit.sb(name + "_hidden_hi", [P, 2, HALF], F16)
        h_lo = kit.sb(name + "_hidden_lo", [P, 2, HALF], F16)
        out_t = kit.sb(name + "_out_turned", [P, 2, TOKENS])
        if clamped:
            r_bias = kit.sb(name + "_router_bias", [P, E])
            biases = kit.sb(name + "_biases", [P, 2, BLOCKS])
            down_bias = kit.sb(name + "_down_bias", [E, DIM])
        ln = LayerNorm(nc, kit, name + "_ln", x, bank, ident)
        s_small = kit.sem(name + "_small_loaded")
        s_raw_gu = [kit.sem(name + f"_raw_gate_up{p}_loaded") for p in range(2)]
        s_raw_d = [kit.sem(name + f"_raw_down{p}_loaded") for p in range(2)]
        s_gu_hi = kit.sem(name + "_gate_up_hi_done")
        s_gu_lo = kit.sem(name + "_gate_up_lo_done")
        s_d_hi = kit.sem(name + "_down_hi_done")
        s_d_lo = kit.sem(name + "_down_lo_done")
        s_r_hi = kit.sem(name + "_router_hi_done")
        s_r_lo = kit.sem(name + "_router_lo_done")
        s_logits = kit.sem(name + "_logits_done")
        s_route = kit.sem(name + "_routing_step")
        s_exp = kit.sem(name + "_routing_exp_done")
        s_routed = kit.sem(name + "_routed")
        s_score_t = kit.sem(name + "_scores_turned_done")
        s_score_s = kit.sem(name + "_scores_saved")
        s_score_w = kit.sem(name + "_scores_written")
        s_score_r = kit.sem(name + "_scores_spread_done")
        s_ones = kit.sem(name + "_ones_done")
        s_gu_mm = kit.sem(name + "_gate_up_product_done")
        s_gate = kit.sem(name + "_gate_done")
        s_read = kit.sem(name + "_gate_up_read")
        s_sig = kit.sem(name + "_sigmoid_done")
        s_glu = kit.sem(name + "_glu_done")
        s_acted = kit.sem(name + "_activated_done")
        s_turns = kit.sem(name + "_score_turn")
        s_hid = kit.sem(name + "_hidden_done")
        s_h_hi = kit.sem(name + "_hidden_hi_done")
        s_h_lo = kit.sem(name + "_hidden_lo_done")
        s_down = kit.sem(name + "_down_product_done")
        s_out_s = kit.sem(name + "_out_saved")
        s_out_t = kit.sem(name + "_out_turned_done")
        s_res = kit.sem(name + "_residual_added")
        SMALL = 5 if clamped else 2
        pieces = []
        if clamped:
            pieces = [(e, 0, P, e) for e in range(E)]
        else:
            for b in range(L0_SCORED):
                a = 0
                while a < P:
                    e = (P * b + a) // FEATURES
                    end = min(P, (e + 1) * FEATURES - P * b)
                    pieces.append((b, a, end, e))
                    a = end

        def block_stages(eng, stage):
            stage(0, 0, True, False)
            stage(1, 1, True, False)
            with eng.Fori(1, BLOCKS // 2 - 1, 1) as i:
                stage(2 * i, 0, False, False)
                stage(2 * i + 1, 1, False, False)
            stage(BLOCKS - 2, 0, False, False)
            stage(BLOCKS - 1, 1, False, True)

        with nc.Block() as block:
            @block.sync
            def _(sp):
                sp.dma_start(r_raw[:], G[name + "_router"].rearrange("(k p) e -> p k e", p=P)).then_inc(s_small, 16)
                sp.dma_start(lower[:], G[name + "_lower_expert"].partition_broadcast(P)).then_inc(s_small, 16)
                if clamped:
                    sp.dma_start(r_bias[:], G["moe1_router_bias"].partition_broadcast(P)).then_inc(s_small, 16)
                    sp.dma_start(biases[:], G["moe1_biases"]).then_inc(s_small, 16)
                    sp.dma_start(down_bias[:], G["moe1_down_bias"]).then_inc(s_small, 16)

                def stage(b, par, first, last):
                    if not first:
                        sp.wait_ge(s_gu_lo, b - 1)
                    sp.dma_start(raw_gu[:, par, :], w_gu_dram[bass.ds(b * P, P), :]).then_inc(s_raw_gu[par], 16)
                    if not first:
                        sp.wait_ge(s_d_lo, b - 1)
                    sp.dma_start(raw_d[:, par, :], w_d_dram[bass.ds(b * P, P), :]).then_inc(s_raw_d[par], 16)
                block_stages(sp, stage)

            @block.gpsimd
            def _(pool):
                ln.pool(pool)
                if not clamped:
                    pool.memset(scores[:, L0_SCORED:BLOCKS, :], 1.0).then_inc(s_ones, 1)
                pool.wait_ge(s_score_s, HALVES)
                pool.dma_start(score_dram, score_t[:]).then_inc(s_score_w, 16)
                pool.wait_ge(s_score_w, 16)
                for b, a, end, e in pieces:
                    pool.dma_start(scores[a:end, b, :], score_dram[e:e + 1, :].partition_broadcast(end - a)
                                   ).then_inc(s_score_r, 16)
                if not clamped:
                    pool.wait_ge(s_ones, 1)
                pool.wait_ge(s_score_r, 16 * len(pieces))

                def stage(b, par, first, last):
                    for h in range(HALVES):
                        u = 2 * b + h
                        later = not (first and par == 0)
                        pool.wait_ge(s_acted, u + 1)
                        if later:
                            pool.wait_ge(s_h_lo, u - 1)
                        row = scores[:, bass.ds(b, 1), HALF * h:HALF * h + HALF].squeeze(1)
                        pool.tensor_tensor(hid[:, h, :], act_out[:, h, :], row, ALU.mult).then_inc(s_hid, 1)

                if clamped:
                    def pair(i):
                        for par in range(2):
                            for h in range(HALVES):
                                u = 4 * i + 2 * par + h
                                later = not (isinstance(i, int) and i == 0 and par == 0)
                                pool.wait_ge(s_sig, u + 1)
                                if later:
                                    pool.wait_ge(s_acted, u - 1)
                                pool.tensor_tensor(glu[:, h, :], gate[:, h, :], sig[:, h, :],
                                                   ALU.mult).then_inc(s_glu, 1)
                                pool.wait_ge(s_acted, u + 1)
                                if later:
                                    pool.wait_ge(s_h_lo, u - 1)
                                pool.sem_inc(s_turns, 1)
                                row = scores[:, bass.ds(i, 1), HALF * h:HALF * h + HALF].squeeze(1)
                                pool.tensor_tensor(hid[:, h, :], act_out[:, h, :], row, ALU.mult).then_inc(s_hid, 1)
                    pair(0)
                    with pool.Fori(1, E, 1) as i:
                        pair(i)
                else:
                    block_stages(pool, stage)

            @block.scalar
            def _(act):
                act.wait_ge(s_small, 16 * SMALL)
                act.activation(r_hi[:], r_raw[:], ACT.Copy).then_inc(s_r_hi, 1)
                act.wait_ge(s_raw_gu[0], 16)
                act.activation(gu_hi[:, 0].rearrange("p g k f -> p (g k f)"), raw_gu[:, 0, :],
                               ACT.Copy).then_inc(s_gu_hi, 1)
                ln.scalar_hi(act, xt_hi)
                act.wait_ge(s_route, 2)
                act.activation(weight[:], weight[:], ACT.Exp).then_inc(s_exp, 1)
                for h in range(HALVES):
                    act.wait_ge(s_score_t, h + 1)
                    act.activation(score_t[:, HALF * h:HALF * h + HALF], bank[4 + h][0:E, :],
                                   ACT.Copy).then_inc(s_score_s, 1)

                def hidden_hi(u, h, later):
                    act.wait_ge(s_hid, u + 1)
                    if later:
                        act.wait_ge(s_down, u - 1)
                    act.activation(h_hi[:, h, :], hid[:, h, :], ACT.Copy).then_inc(s_h_hi, 1)

                def stage(b, par, first, last):
                    for h in range(HALVES):
                        u = 2 * b + h
                        if not (first and par == 0 and h == 0):
                            hidden_hi(u - 1, 1 - h, not (first and (par == 0 or h == 0)))
                        if clamped:
                            act.wait_ge(s_gate, u + 1)
                            if not (first and par == 0):
                                act.wait_ge(s_glu, u - 1)
                            act.activation(sig[:, h, :], gate[:, h, :], ACT.Sigmoid, scale=ALPHA).then_inc(s_sig, 1)
                        else:
                            act.wait_ge(s_gu_mm, u + 1)
                            if not (first and par == 0):
                                act.wait_ge(s_acted, u - 1)
                            act.activation(gate[:, h, :], bank[2 * h][:], ACT.Silu).then_inc(s_gate, 1)
                        if h == 0 and not last:
                            act.wait_ge(s_raw_gu[1 - par], raw_loaded(b + 1, 1 - par))
                            act.wait_ge(s_gu_mm, 2 * b if not (first and par == 0) else 1)
                            act.activation(gu_hi[:, 1 - par].rearrange("p g k f -> p (g k f)"), raw_gu[:, 1 - par, :],
                                           ACT.Copy).then_inc(s_gu_hi, 1)
                        if h == 1:
                            act.wait_ge(s_raw_d[par], raw_loaded(b, par))
                            if not first:
                                act.wait_ge(s_down, 2 * b - 2)
                            act.activation(d_hi[:, par, :], raw_d[:, par, :], ACT.Copy).then_inc(s_d_hi, 1)

                def raw_loaded(b, par):
                    return 8 * (b - par) + 16

                block_stages(act, stage)
                hidden_hi(2 * BLOCKS - 1, 1, True)
                act.wait_ge(s_down, 2 * BLOCKS)
                for o in range(2):
                    act.activation(out_t[:, o, 0:HALF], bank[4 + 2 * o][:], ACT.Copy).then_inc(s_out_s, 1)

            @block.vector
            def _(dve):
                ln.vector_stats(dve)
                dve.wait_ge(s_r_hi, 1)
                dve.tensor_tensor(r_lo[:], r_raw[:], r_hi[:], ALU.subtract).then_inc(s_r_lo, 1)
                if clamped:
                    dve.tensor_scalar(biases[:, 1, :], biases[:, 1, :], 1.0, None, ALU.add).then_inc(s_r_lo, 1)
                ln.vector_normalize(dve)
                ln.vector_lo(dve, xt_hi, xt_lo)
                dve.wait_ge(s_gu_hi, 1)
                dve.tensor_tensor(gu_lo[:, 0].rearrange("p g k f -> p (g k f)"), raw_gu[:, 0, :],
                                  gu_hi[:, 0].rearrange("p g k f -> p (g k f)"), ALU.subtract).then_inc(s_gu_lo, 1)
                n = 0

                def step(ins):
                    nonlocal n
                    n += 1
                    ins.then_inc(s_route, 1)
                    dve.wait_ge(s_route, n)

                dve.wait_ge(s_logits, 1)
                lg = bank[4][:, 0:TILES * E].rearrange("p (t e) -> p t e", e=E)
                if clamped:
                    dve.tensor_tensor(logits[:], lg, bc(r_bias[:], 1, TILES), ALU.add).then_inc(s_routed, 1)
                else:
                    dve.tensor_copy(logits[:], lg).then_inc(s_routed, 1)
                dve.wait_ge(s_routed, 1)
                step(dve.tensor_reduce(peak[:], logits[:], AX.X, ALU.max))
                step(dve.tensor_tensor(weight[:], logits[:], bc(peak[:], 2, E), ALU.subtract))
                dve.wait_ge(s_exp, 1)
                ranked = logits
                if not clamped:
                    step(dve.tensor_reduce(total[:], weight[:], AX.X, ALU.add))
                    step(dve.reciprocal(total[:], total[:]))
                    step(dve.tensor_tensor(weight[:], weight[:], bc(total[:], 2, E), ALU.mult))
                    ranked = weight
                mine, other = bc(ranked[:], 3, E), bc(ranked[:], 2, E)
                step(dve.tensor_tensor(beats[:], other, mine, ALU.is_gt))
                step(dve.tensor_tensor(ties[:], other, mine, ALU.is_equal))
                step(dve.tensor_tensor(ties[:], ties[:], bc(lower[:], 1, TILES), ALU.mult))
                step(dve.tensor_tensor(beats[:], beats[:], ties[:], ALU.add))
                step(dve.tensor_reduce(rank[:], beats[:], AX.X, ALU.add))
                step(dve.scalar_tensor_tensor(weight[:], rank[:], float(TOP), weight[:], ALU.is_lt, ALU.mult))
                step(dve.tensor_reduce(total[:], weight[:], AX.X, ALU.add))
                if not clamped:
                    step(dve.tensor_scalar(total[:], total[:], 1e-20, None, ALU.add))
                step(dve.reciprocal(total[:], total[:]))
                dve.tensor_tensor(weight[:], weight[:], bc(total[:], 2, E), ALU.mult).then_inc(s_routed, 1)

                def hidden_lo(u, h, later):
                    dve.wait_ge(s_h_hi, u + 1)
                    dve.tensor_tensor(h_lo[:, h, :], hid[:, h, :], h_hi[:, h, :], ALU.subtract).then_inc(s_h_lo, 1)

                def stage(b, par, first, last):
                    for h in range(HALVES):
                        u = 2 * b + h
                        later = not (first and par == 0)
                        if clamped:
                            dve.wait_ge(s_gu_mm, u + 1)
                            if later:
                                dve.wait_ge(s_glu, u - 1)
                            dve.tensor_scalar(gate[:, h, :], bank[2 * h][:], bias_of(0, b), LIMIT, ALU.add,
                                              ALU.min).then_inc(s_gate, 1)
                            if later:
                                dve.wait_ge(s_acted, u - 1)
                            dve.tensor_scalar(up[:, h, :], bank[2 * h + 1][:], bias_of(1, b), LIMIT + 1.0, ALU.add,
                                              ALU.min).then_inc(s_read, 1)
                        if not (first and par == 0 and h == 0):
                            hidden_lo(u - 1, 1 - h, not (first and (par == 0 or h == 0)))
                        if h == 0 and not last:
                            dve.wait_ge(s_gu_hi, b + 2)
                            dve.tensor_tensor(gu_lo[:, 1 - par].rearrange("p g k f -> p (g k f)"), raw_gu[:, 1 - par, :],
                                              gu_hi[:, 1 - par].rearrange("p g k f -> p (g k f)"),
                                              ALU.subtract).then_inc(s_gu_lo, 1)
                        if clamped:
                            dve.wait_ge(s_glu, u + 1)
                            dve.wait_ge(s_read, u + 1)
                            if later:
                                dve.wait_ge(s_hid, u - 1)
                            dve.scalar_tensor_tensor(act_out[:, h, :], up[:, h, :], 1.0 - LIMIT, glu[:, h, :],
                                                     ALU.max, ALU.mult).then_inc(s_acted, 1)
                        else:
                            dve.wait_ge(s_gate, u + 1)
                            if later:
                                dve.wait_ge(s_hid, u - 1)
                            dve.tensor_tensor(act_out[:, h, :], gate[:, h, :], bank[2 * h + 1][:],
                                              ALU.mult).then_inc(s_acted, 1)
                        if h == 1:
                            dve.wait_ge(s_d_hi, b + 1)
                            dve.tensor_tensor(d_lo[:, par, :], raw_d[:, par, :], d_hi[:, par, :],
                                              ALU.subtract).then_inc(s_d_lo, 1)

                def bias_of(which, b):
                    return biases[:, which, bass.ds(b, 1)]

                block_stages(dve, stage)
                hidden_lo(2 * BLOCKS - 1, 1, True)
                dve.wait_ge(s_down, 2 * BLOCKS)
                for o in range(2):
                    dve.tensor_copy(out_t[:, o, HALF:TOKENS], bank[5 + 2 * o][:]).then_inc(s_out_s, 1)
                for j in range(TILES // 2):
                    dve.wait_ge(s_out_t, j + 1)
                    dve.tensor_tensor(x[:, 2 * j:2 * j + 2, :], x[:, 2 * j:2 * j + 2, :],
                                      bank[j][:].rearrange("p (t d) -> p t d", d=DIM), ALU.add).then_inc(s_res, 1)
                dve.wait_ge(s_res, TILES // 2)

            @block.tensor
            def _(pe):
                ln.tensor(pe)
                pe.wait_ge(s_r_lo, 2 if clamped else 1)
                for i in range(TILES):
                    pe.wait_ge(ln.s_lo, 2 * (i // 4 + 1))
                    t = slice(P * i, P * i + P)
                    for k in range(KT):
                        m = three_products(pe, bank[4][:, E * i:E * i + E], xt_hi[:, k, t], xt_lo[:, k, t],
                                           r_hi[:, k, :], r_lo[:, k, :], k == 0, k == KT - 1)
                m.then_inc(s_logits, 1)

                def gate_up(b, par, h, later):
                    u = 2 * b + h
                    pe.wait_ge(s_gu_lo, b + 1)
                    if later:
                        pe.wait_ge(s_read if clamped else s_acted, u - 1)
                    for g in range(2):
                        for k in range(KT):
                            t = slice(HALF * h, HALF * h + HALF)
                            m = three_products(pe, bank[2 * h + g][:], gu_hi[:, par, g, k, :], gu_lo[:, par, g, k, :],
                                               xt_hi[:, k, t], xt_lo[:, k, t], k == 0, k == KT - 1)
                    m.then_inc(s_gu_mm, 1)

                def down(b, par, h, first, last):
                    pe.wait_ge(s_h_lo, 2 * b + h + 1)
                    pe.wait_ge(s_d_lo, b + 1)
                    for o in range(2):
                        m = three_products(pe, bank[4 + 2 * o + h][:], d_hi[:, par, P * o:P * o + P],
                                           d_lo[:, par, P * o:P * o + P], h_hi[:, h, :], h_lo[:, h, :],
                                           first and not clamped, last, skip_group_check=True)
                    m.then_inc(s_down, 1)

                gate_up(0, 0, 0, False)
                gate_up(0, 0, 1, False)
                pe.wait_ge(s_routed, 2)
                for h in range(HALVES):
                    for i in range(4 * h, 4 * h + 4):
                        m = pe.transpose(bank[4 + h][0:E, P * (i % 4):P * (i % 4) + P], weight[:, i, :], ident)
                    m.then_inc(s_score_t, 1)
                pe.wait_ge(s_score_s, HALVES)
                if clamped:
                    for o in range(2):
                        for h in range(HALVES):
                            pe.matmul(bank[4 + 2 * o + h][:], down_bias[:, P * o:P * o + P],
                                      score_t[:, HALF * h:HALF * h + HALF], start=True, stop=False,
                                      skip_group_check=True)

                def turn(b, par, first):
                    for h in range(HALVES):
                        gate_up(b + 1, 1 - par, h, True)
                        down(b, par, h, first, False)

                turn(0, 0, True)
                with pe.Fori(1, BLOCKS // 2, 1) as i:
                    turn(2 * i - 1, 1, False)
                    turn(2 * i, 0, False)
                for h in range(HALVES):
                    down(BLOCKS - 1, 1, h, False, True)
                pe.wait_ge(s_out_s, 4)
                for i in range(TILES):
                    for o in range(2):
                        c = DIM * (i % 2) + P * o
                        m = pe.transpose(bank[i // 2][:, c:c + P], out_t[:, o, P * i:P * i + P], ident)
                    if i % 2:
                        m.then_inc(s_out_t, 1)
        kit.retire_semaphores()


BF16 = mybir.dt.bfloat16
ATT_HEADS, ATT_DIM, PAD = 16, 16, 32
GROUPS = ATT_HEADS * PAD // P
SCALE_ROOT = ATT_DIM ** -0.25
SPAN = 3 * P
BATCHES = TOKENS // SEQ


def attention(nc, G):
    x, bank, banks, ident = G["x"], G["bank"], G["banks"], G["ident"]
    with ExitStack() as stack:
        kit = Kit(nc, stack, [])
        q_t = kit.sb("q_turned", [P, GROUPS, TOKENS])
        k_t = kit.sb("k_turned", [P, GROUPS, TOKENS])
        v = kit.sb("v_and_ones", [P, TILES, ATT_HEADS, PAD])
        w_o = kit.sb("w_o", [P, GROUPS, DIM])
        o_raw = kit.sb("attended", [P, GROUPS, TOKENS])
        bo = kit.sb("bo_rows", [P, DIM])
        consts = kit.sb("attention_consts", [P, 4, P])
        consts16 = kit.sb("attention_consts16", [P, 3, P], BF16)
        s_const16 = kit.sem("attention_consts16_done")
        s_late = kit.sem("attention_late_loaded")
        with ExitStack() as inner:
            attention_projections(nc, G, kit.part(inner), q_t, k_t, v, w_o, bo, consts, consts16, s_const16, s_late)
        with ExitStack() as inner:
            attention_heads(nc, G, kit.part(inner), q_t, k_t, v, w_o, o_raw, consts, consts16)
        kit.retire_semaphores()


def attention_projections(nc, G, kit, q_t, k_t, v, w_o, bo, consts, consts16, s_const16, s_late):
    x, bank, ident = G["x"], G["bank"], G["ident"]
    WIDTH = 2 * GROUPS * P + DIM
    raw = kit.sb("w_qkv_raw", [P, KT, WIDTH])
    w_hi = kit.sb("w_qkv_hi", [P, KT, WIDTH], F16)
    w_lo = kit.sb("w_qkv_lo", [P, KT, WIDTH], F16)
    xt_hi = kit.sb("attention_xt_hi", [P, KT, TOKENS], F16)
    xt_lo = kit.sb("attention_xt_lo", [P, KT, TOKENS], F16)
    biases = kit.sb("qk_biases", [P, 2, GROUPS])
    half_biases = kit.sb("qk_biases_scaled", [P, 2, GROUPS])
    bv = kit.sb("bv_rows", [P, DIM])
    ln = LayerNorm(nc, kit, "attention_ln", x, bank, ident)
    s_w = kit.sem("w_qkv_loaded")
    s_small = kit.sem("attention_small_loaded")
    s_w_hi = kit.sem("w_qkv_hi_done")
    s_w_lo = kit.sem("w_qkv_lo_done")
    s_bias = kit.sem("qk_biases_done")
    s_mm = kit.sem("qkv_projected")
    s_q = kit.sem("q_done")
    s_k = kit.sem("k_done")
    s_v = kit.sem("v_done")
    s_pad = kit.sem("v_pad_done")
    s_bo = kit.sem("bo_added")
    QK = 2 * GROUPS * HALVES

    def unit(u):
        return u % 2, (u // 2) % GROUPS, u // (2 * GROUPS)

    with nc.Block() as block:
        @block.sync
        def _(sp):
            sp.dma_start(raw[:], G["w_qkv"].rearrange("(k p) n -> p k n", p=P)).then_inc(s_w, 16)
            sp.dma_start(biases[:], G["qk_bias"]).then_inc(s_small, 16)
            sp.dma_start(bv[:], G["bv"].partition_broadcast(P)).then_inc(s_small, 16)
            sp.dma_start(bo[:], G["bo"].partition_broadcast(P)).then_inc(s_small, 16)
            sp.dma_start(consts[:], G["attention_consts"]).then_inc(s_small, 16)
            sp.dma_start(w_o[:], G["w_o"].rearrange("(g p) n -> p g n", p=P)).then_inc(s_small, 16)

        @block.gpsimd
        def _(pool):
            pool.memset(v[:], 0.0).then_inc(s_pad, 1)
            pool.wait_ge(s_pad, 1)
            pool.memset(v[:, :, :, ATT_DIM:ATT_DIM + 1], 1.0).then_inc(s_pad, 1)
            ln.pool(pool)
            pool.wait_ge(s_small, 80)
            pool.tensor_copy(consts16[:], consts[:, 0:3, :]).then_inc(s_const16, 1)
            pool.wait_ge(ln.s_xn, TILES)
            pool.tensor_tensor(x[:], x[:], bc(bo[:], 1, TILES), ALU.add).then_inc(s_bo, 1)
            pool.wait_ge(s_bo, 1)
            pool.wait_ge(s_const16, 1)

        @block.scalar
        def _(act):
            act.wait_ge(s_w, 16)
            for k in range(KT):
                act.activation(w_hi[:, k, :], raw[:, k, :], ACT.Copy).then_inc(s_w_hi, 1)
            act.wait_ge(s_small, 80)
            act.activation(half_biases[:], biases[:], ACT.Copy, scale=SCALE_ROOT).then_inc(s_bias, 1)
            ln.scalar_hi(act, xt_hi)
            act.wait_ge(s_bias, 1)
            for u in range(1, QK, 2):
                _, g, h = unit(u)
                act.wait_ge(s_mm, u + 1)
                act.activation(k_t[:, g, HALF * h:HALF * h + HALF], bank[4 + u % 4][:], ACT.Identity,
                               bias=half_biases[:, 1, g:g + 1], scale=SCALE_ROOT).then_inc(s_k, 1)

        @block.vector
        def _(dve):
            ln.vector_stats(dve)
            ln.vector_normalize(dve)
            for k in range(KT):
                dve.wait_ge(s_w_hi, k + 1)
                dve.tensor_tensor(w_lo[:, k, :], raw[:, k, :], w_hi[:, k, :], ALU.subtract).then_inc(s_w_lo, 1)
            ln.vector_lo(dve, xt_hi, xt_lo)
            dve.wait_ge(s_bias, 1)
            for u in range(0, QK, 2):
                _, g, h = unit(u)
                dve.wait_ge(s_mm, u + 1)
                dve.tensor_scalar(q_t[:, g, HALF * h:HALF * h + HALF], bank[4 + u % 4][:], SCALE_ROOT,
                                  half_biases[:, 0, g:g + 1], ALU.mult, ALU.add).then_inc(s_q, 1)
            dve.wait_ge(s_pad, 2)
            for i in range(TILES):
                dve.wait_ge(s_mm, QK + i + 1)
                dve.tensor_tensor(v[:, i, :, 0:ATT_DIM],
                                  bank[4 + i % 4][:, 0:DIM].rearrange("p (h d) -> p h d", d=ATT_DIM),
                                  bv[:].rearrange("p (h d) -> p h d", d=ATT_DIM), ALU.add).then_inc(s_v, 1)
            dve.wait_ge(s_v, TILES)

        @block.tensor
        def _(pe):
            ln.tensor(pe)
            pe.wait_ge(s_w_lo, KT)
            for u in range(QK):
                which, g, h = unit(u)
                pe.wait_ge(ln.s_lo, 2 * (h + 1))
                if u >= 4:
                    pe.wait_ge((s_q, s_k)[which], u // 2 - 1)
                c = P * (GROUPS * which + g)
                t = slice(HALF * h, HALF * h + HALF)
                for k in range(KT):
                    m = three_products(pe, bank[4 + u % 4][:], w_hi[:, k, c:c + P], w_lo[:, k, c:c + P],
                                       xt_hi[:, k, t], xt_lo[:, k, t], k == 0, k == KT - 1)
                m.then_inc(s_mm, 1)
            for i in range(TILES):
                if i < 4:
                    pe.wait_ge((s_q, s_k)[i % 2], QK // 2 - 1 + i // 2)
                else:
                    pe.wait_ge(s_v, i - 3)
                t = slice(P * i, P * i + P)
                c = slice(2 * GROUPS * P, WIDTH)
                for k in range(KT):
                    m = three_products(pe, bank[4 + i % 4][:, 0:DIM], xt_hi[:, k, t], xt_lo[:, k, t], w_hi[:, k, c],
                                       w_lo[:, k, c], k == 0, k == KT - 1)
                m.then_inc(s_mm, 1)


def attention_heads(nc, G, kit, q_t, k_t, v, w_o, o_raw, consts, consts16):
    x, bank, banks, ident = G["x"], G["bank"], G["banks"], G["ident"]
    UNITS = BATCHES * GROUPS * 2
    peaks = kit.sb("minus_peaks", [P, 2, 2, 4, PAD])
    probs = kit.sb("probs", [P, 2, 2, SPAN])
    inverse = kit.sb("inverse_sums", [P, 2, SEQ])
    s_zero = kit.sem("peaks_cleared")
    s_s = kit.sem("scores_done")
    s_peak = kit.sem("peak_done")
    s_turn = kit.sem("peaks_turned")
    s_aug = kit.sem("q_augmented")
    s_st = kit.sem("turned_scores_done")
    s_exp = kit.sem("probs_done")
    s_pv = kit.sem("attended_done")
    s_raw = kit.sem("attended_saved")
    s_sum = kit.sem("sums_spread")
    s_inv = kit.sem("inverse_done")
    s_norm = kit.sem("attended_normed")
    s_out = kit.sem("attention_projected")
    s_res = kit.sem("attention_residual_added")
    ident16, mask, mask_t = consts16[:, 0, :], consts16[:, 1, :], consts16[:, 2, :]
    spread = consts[:, 3, :]

    def unit(n):
        return n // (2 * GROUPS), (n // 2) % GROUPS, n % 2

    def add_mask(pe, out_bank, m):
        out = banks[:, out_bank, 0:SPAN + P].rearrange("p (c n) -> p c n", n=P)[:, 0:3:2, :]
        return pe.matmul(out, ident16, bc(m, 1, 2), start=False, stop=True, skip_group_check=True)

    with nc.Block() as block:
        @block.tensor
        def _(pe):
            def scores(n):
                b, g, pair = unit(n)
                if n >= 2:
                    pe.wait_ge(s_aug, n - 1)
                for jj in range(2):
                    r = slice(PAD * (2 * pair + jj), PAD * (2 * pair + jj) + PAD)
                    bk = 2 * (n % 2) + jj
                    for qt in range(2):
                        q = q_t[r, g, SEQ * b + P * qt:SEQ * b + P * qt + P]
                        keys = k_t[r, g, SEQ * b:SEQ * b + P * (qt + 1)]
                        pe.matmul(banks[:, bk, P * qt:P * qt + P * (qt + 1)], q, keys, start=(qt == 0), stop=False,
                                  skip_group_check=True)
                    m = add_mask(pe, bk, mask)
                m.then_inc(s_s, 1)

            def turn_peaks(n):
                pe.wait_ge(s_peak, n + 1)
                for qt in range(2):
                    m = pe.transpose(banks[:, 2 * (n % 2) + qt, SPAN:SPAN + P],
                                     peaks[:, n % 2, qt].rearrange("p j e -> p (j e)"), ident)
                m.then_inc(s_turn, 1)

            def turned_scores(n):
                b, g, pair = unit(n)
                pe.wait_ge(s_aug, n + 1)
                if n >= 1:
                    pe.wait_ge(s_exp, n)
                for jj in range(2):
                    r = slice(PAD * (2 * pair + jj), PAD * (2 * pair + jj) + PAD)
                    for kb in range(2):
                        keys = k_t[r, g, SEQ * b + P * kb:SEQ * b + P * kb + P]
                        q = q_t[r, g, SEQ * b + P * kb:SEQ * b + SEQ]
                        pe.matmul(banks[:, 4 + jj, SEQ * kb:SEQ + P * kb], keys, q, start=(kb == 0), stop=False,
                                  skip_group_check=True)
                    m = add_mask(pe, 4 + jj, mask_t)
                m.then_inc(s_st, 1)

            def attend(n):
                b, g, pair = unit(n)
                bg = n // 2
                pe.wait_ge(s_exp, n + 1)
                if pair == 0 and bg >= 2:
                    pe.wait_ge(s_inv, bg - 1)
                for jj in range(2):
                    j = 2 * pair + jj
                    out = bank[6 + bg % 2][PAD * j:PAD * j + PAD]
                    pe.matmul(out[:, 0:SEQ], v[:, 2 * b, 4 * g + j, :], probs[:, n % 2, jj, 0:SEQ], start=True,
                              stop=False)
                    m = pe.matmul(out[:, P:SEQ], v[:, 2 * b + 1, 4 * g + j, :], probs[:, n % 2, jj, SEQ:SPAN],
                                  start=False, stop=True)
                m.then_inc(s_pv, 1)

            def spread_sums(bg):
                b, g = bg // GROUPS, bg % GROUPS
                pe.wait_ge(s_raw, bg + 1)
                pe.matmul(bank[6 + bg % 2][:, SEQ:2 * SEQ], spread, o_raw[:, g, SEQ * b:SEQ * b + SEQ], start=True,
                          stop=True).then_inc(s_sum, 1)

            scores(0)
            for n in range(UNITS + 3):
                if n + 1 < UNITS:
                    scores(n + 1)
                if n < UNITS:
                    turn_peaks(n)
                if 1 <= n <= UNITS:
                    turned_scores(n - 1)
                if 2 <= n <= UNITS + 1:
                    attend(n - 2)
                if n >= 4 and n % 2 == 0:
                    spread_sums(n // 2 - 2)

        @block.gpsimd
        def _(pool):
            pool.memset(peaks[:], 0.0).then_inc(s_zero, 1)
            for bg in range(UNITS // 2):
                b, g = bg // GROUPS, bg % GROUPS
                pool.wait_ge(s_inv, bg + 1)
                o = o_raw[:, g, SEQ * b:SEQ * b + SEQ]
                pool.tensor_tensor(o, o, inverse[:, bg % 2, :], ALU.mult).then_inc(s_norm, 1)
            pool.wait_ge(s_norm, UNITS // 2)

        @block.scalar
        def _(act):
            for n in range(UNITS + 1):
                if n < UNITS:
                    act.wait_ge(s_st, n + 1)
                    if n >= 2:
                        act.wait_ge(s_pv, n - 1)
                    act.activation(probs[:, n % 2], banks[:, 4:6, 0:SPAN], ACT.Exp).then_inc(s_exp, 1)
                if n >= 1 and n % 2 == 0:
                    bg = n // 2 - 1
                    b, g = bg // GROUPS, bg % GROUPS
                    act.wait_ge(s_pv, n)
                    act.activation(o_raw[:, g, SEQ * b:SEQ * b + SEQ], bank[6 + bg % 2][:, 0:SEQ],
                                   ACT.Copy).then_inc(s_raw, 1)

        @block.vector
        def _(dve):
            dve.wait_ge(s_zero, 1)

            def peak(n):
                pair = n % 2
                dve.wait_ge(s_s, n + 1)
                if n >= 2:
                    dve.wait_ge(s_turn, n - 1)
                for qt in range(2):
                    dst = peaks[:, n % 2, qt, 2 * pair:2 * pair + 2, ATT_DIM:ATT_DIM + 1]
                    m = dve.tensor_reduce(dst.squeeze(2), banks[:, 2 * (n % 2):2 * (n % 2) + 2, P * qt:P * (2 * qt + 1)],
                                          AX.X, ALU.max, negate=True)
                m.then_inc(s_peak, 1)

            def augment(n):
                b, g, pair = unit(n)
                r = slice(2 * PAD * pair, 2 * PAD * pair + 2 * PAD)
                dve.wait_ge(s_turn, n + 1)
                q = q_t[r, g, SEQ * b:SEQ * b + SEQ].rearrange("p (t n) -> p t n", n=P)
                dve.tensor_tensor(q, q, banks[r, 2 * (n % 2):2 * (n % 2) + 2, SPAN:SPAN + P],
                                  ALU.add).then_inc(s_aug, 1)

            def invert(bg):
                dve.wait_ge(s_sum, bg + 1)
                if bg >= 2:
                    dve.wait_ge(s_norm, bg - 1)
                dve.reciprocal(inverse[:, bg % 2, :], bank[6 + bg % 2][:, SEQ:2 * SEQ]).then_inc(s_inv, 1)

            for n in range(UNITS):
                peak(n)
                augment(n)
                if n >= 5 and n % 2 == 1:
                    invert((n - 5) // 2)
            invert(UNITS // 2 - 2)
            invert(UNITS // 2 - 1)

    with nc.Block() as block:
        @block.tensor
        def _(pe):
            for i in range(TILES):
                if i >= 4:
                    pe.wait_ge(s_res, i - 3)
                for g in range(GROUPS):
                    m = pe.matmul(bank[i % 4][:, 0:DIM], o_raw[:, g, P * i:P * i + P], w_o[:, g, :], start=(g == 0),
                                  stop=(g == GROUPS - 1))
                m.then_inc(s_out, 1)

        @block.vector
        def _(dve):
            for i in range(TILES):
                dve.wait_ge(s_out, i + 1)
                dve.tensor_tensor(x[:, i, :], x[:, i, :], bank[i % 4][:, 0:DIM], ALU.add).then_inc(s_res, 1)
            dve.wait_ge(s_res, TILES)


def run_stages(nc, G):
    mamba(nc, G)
    moe(nc, G, 0)
    attention(nc, G)
    moe(nc, G, 1)


def more_layout(i, a):
    moe_layout(i, a)
    attention_layout(i, a)


def store(nc, G):
    with ExitStack() as stack:
        s_stored = Kit(nc, stack, []).sem("output_stored")
        with nc.Block() as block:
            @block.sync
            def _(sp):
                sp.dma_start(G["out"].rearrange("(t p) d -> p t d", p=P), G["x"][:]).then_inc(s_stored, 16)
                sp.wait_ge(s_stored, 16)


def build(nc, inputs, out):
    with ExitStack() as stack:
        kit = Kit(nc, stack, [])
        G = dict(inputs)
        G["x_in"] = inputs["x"]
        G["ident_in"] = inputs["ident"]
        G["out"] = out
        G["x"] = kit.sb("residual", [P, TILES, DIM])
        G["ident"] = kit.sb("identity", [P, P])[:]
        G["banks"] = stack.enter_context(nc.psum_tensor("banks", [P, 8, 512], F32))
        G["bank"] = [G["banks"][:, b, :] for b in range(8)]
        G["s_ident"] = kit.sem("identity_loaded")
        run_stages(nc, G)
        store(nc, G)


def level_masks():
    import numpy as np
    t = np.arange(P)
    cum = np.zeros((2, LEVELS + 1, P, P), np.float32)
    pair = np.zeros((LEVELS, P, P), np.float32)
    for k in range(LEVELS):
        half = 1 << k
        second = (t // half) % 2 == 1
        block = t // (2 * half)
        ref = block * 2 * half + half - 1
        r = t[:, None]
        cum[0, k] = (~second)[None] & (r > t[None]) & (r <= ref[None])
        cum[1, k] = second[None] & (r > ref[None]) & (r <= t[None])
        pair[k] = (~second)[:, None] & second[None] & (block[:, None] == block[None])
    cum[0, LEVELS] = t[:, None] > t[None]
    cum[1, LEVELS] = t[:, None] <= t[None]
    return cum.reshape(-1, P, P).transpose(1, 0, 2), pair.transpose(1, 0, 2)


def layout(i):
    import numpy as np
    cum, pair = level_masks()
    a = {
        "x": i["L0_attn_x"].reshape(TOKENS, DIM),
        "ident": np.eye(P, dtype=np.float32),
        "w_in": i["L0_attn_in_proj_w"].T,
        "conv_w": i["L0_attn_conv_w"],
        "dt_bias": i["L0_attn_dt_bias"],
        "A_log": i["L0_attn_A_log"],
        "D": i["L0_attn_D"],
        "norm_w": i["L0_attn_norm_w"].reshape(-1, P).T,
        "w_out": i["L0_attn_out_proj_w"].T,
        "cum_masks": cum,
        "pair_masks": pair,
    }
    more_layout(i, a)
    return a


def kernel(**inputs):
    import numpy as np
    import concourse.bacc as bacc
    from concourse.bass_utils import run_bass_kernel_spmd

    nc = bacc.Bacc("TRN2", target_bir_lowering=False, num_devices=1)
    arrays = {k + "_dram": np.ascontiguousarray(v) for k, v in layout({k: np.asarray(v) for k, v in inputs.items()}).items()}
    aps = {k[:-5]: nc.dram_tensor(k, v.shape, mybir.dt.from_np(v.dtype), kind="ExternalInput").ap()
           for k, v in arrays.items()}
    out = nc.dram_tensor("out_dram", (TOKENS, DIM), F32, kind="ExternalOutput").ap()
    build(nc, aps, out)
    result = run_bass_kernel_spmd(nc, [arrays], core_ids=[0])
    return result.results[0]["out_dram"].reshape(4, SEQ, DIM)


def moe_blocks(gate, up, down):
    import numpy as np
    n = -(-gate.shape[0] // (2 * P)) * 2 * P
    pad = lambda w: np.concatenate([w, np.zeros((n - w.shape[0], DIM), w.dtype)])
    gu = np.stack([pad(gate), pad(up)]).reshape(2, n // P, P, KT, P)
    return gu.transpose(1, 4, 0, 3, 2).reshape(n, 2 * KT * P), pad(down)


def moe_layout(i, a):
    import numpy as np
    cat = np.concatenate
    a["moe0_gate_up"], a["moe0_down"] = moe_blocks(
        cat([i["L0_ffn_expert_gate"].reshape(-1, DIM), i["L0_ffn_shared_gate"]]),
        cat([i["L0_ffn_expert_up"].reshape(-1, DIM), i["L0_ffn_shared_up"]]),
        cat([i["L0_ffn_expert_down"].transpose(0, 2, 1).reshape(-1, DIM), i["L0_ffn_shared_down"].T]))
    a["moe0_router"] = i["L0_ffn_gate_w"].T
    a["moe0_lower_expert"] = np.tril(np.ones((L0_EXPERTS, L0_EXPERTS), np.float32), -1)
    w = i["L1_ffn_gate_up_proj"]
    a["moe1_gate_up"], a["moe1_down"] = moe_blocks(
        w[:, :, 0::2].transpose(0, 2, 1).reshape(-1, DIM), w[:, :, 1::2].transpose(0, 2, 1).reshape(-1, DIM),
        i["L1_ffn_down_proj"].reshape(-1, DIM))
    a["moe1_router"] = i["L1_ffn_router_weight"].T
    a["moe1_lower_expert"] = np.tril(np.ones((L1_EXPERTS, L1_EXPERTS), np.float32), -1)
    a["moe1_router_bias"] = i["L1_ffn_router_bias"]
    a["moe1_biases"] = i["L1_ffn_gate_up_proj_bias"].reshape(-1, P, 2).transpose(1, 2, 0)
    a["moe1_down_bias"] = i["L1_ffn_down_proj_bias"]


def attention_layout(i, a):
    import numpy as np

    def padded(w):
        w = w.reshape(ATT_HEADS, ATT_DIM, -1)
        return np.concatenate([w, np.zeros_like(w)], axis=1).reshape(ATT_HEADS * PAD, -1)

    k_bias = padded(i["L1_attn_bk"]).reshape(ATT_HEADS, PAD).copy()
    k_bias[:, ATT_DIM] = 1.0 / SCALE_ROOT
    a["w_qkv"] = np.concatenate([padded(i["L1_attn_Wq"]), padded(i["L1_attn_Wk"]), i["L1_attn_Wv"]]).T
    a["qk_bias"] = np.stack([padded(i["L1_attn_bq"]).reshape(GROUPS, P), k_bias.reshape(GROUPS, P)]).transpose(2, 0, 1)
    a["bv"] = i["L1_attn_bv"]
    a["bo"] = i["L1_attn_bo"]
    a["w_o"] = padded(i["L1_attn_Wo"].T)
    t = np.arange(P)
    above = np.where(t[None] > t[:, None], -1e30, 0.0)
    spread = (t[:, None] % PAD == ATT_DIM) & (t[:, None] // PAD == t[None] // PAD)
    a["attention_consts"] = np.stack([np.eye(P), above, above.T, spread]).transpose(1, 0, 2).astype(np.float32)
```

```python
from contextlib import ExitStack

import concourse.bass as bass
from concourse import mybir

F32 = mybir.dt.float32
F16 = mybir.dt.float16
ALU = mybir.AluOpType
ACT = mybir.ActivationFunctionType
AX = mybir.AxisListType

P = 128
TOKENS = 1024
DIM = 256
TILES = TOKENS // P
KT = DIM // P
HALF = 512
HALVES = TOKENS // HALF
EPS = 1e-5

HID = 512
HEADS = 64
HEAD_DIM = HID // HEADS
CONV_BLOCKS = 6
XB = HID // P
TAPS = 4
SEQ = 256
LEVELS = 7
Z0, X0, DT0 = 0, HID, HID + 768


class Kit:

    def __init__(self, nc, stack, taken):
        self.nc, self.stack, self.taken = nc, stack, taken

    def part(self, stack):
        return Kit(self.nc, stack, self.taken)

    def sb(self, name, shape, dtype=F32):
        return self.stack.enter_context(self.nc.sbuf_tensor(name, shape, dtype))

    def sem(self, name):
        self.taken.append(self.nc.alloc_semaphore(name))
        return self.taken[-1]

    def retire_semaphores(self):
        with self.nc.Block() as block:
            @block.sync
            def _(sp):
                for sem in self.taken:
                    sp.sem_clear(sem)
        for sem in self.taken:
            self.nc.release_semaphore(sem)
        self.taken.clear()


def bc(ap, axis, n):
    ap = ap.unsqueeze(axis)
    shape = list(ap.shape)
    shape[axis] = n
    return ap.broadcast_to(shape)


class LayerNorm:

    def __init__(self, nc, kit, name, x, bank, ident):
        self.nc, self.x, self.bank, self.ident = nc, x, bank, ident
        self.stats = kit.sb(name + "_stats", [P, TILES, 6])
        self.mv = kit.sb(name + "_mean_var", [P, TILES, 2])
        self.var = kit.sb(name + "_var", [P, TILES])
        self.half_power = kit.sb(name + "_minus_half", [P, TILES])
        self.rstd = kit.sb(name + "_rstd", [P, TILES])
        self.xn = kit.sb(name + "_xn", [P, TILES, DIM])
        self.s_stats = kit.sem(name + "_stats_done")
        self.s_mv = kit.sem(name + "_mean_var_done")
        self.s_rstd = kit.sem(name + "_rstd_done")
        self.s_pool = kit.sem(name + "_pool_step")
        self.s_xn = kit.sem(name + "_xn_done")
        self.s_turned = kit.sem(name + "_turned")
        self.s_hi = kit.sem(name + "_hi_done")
        self.s_lo = kit.sem(name + "_lo_done")

    def vector_stats(self, dve, arrived=None):
        for i in range(TILES):
            if arrived is not None:
                arrived(i)
            dve.bn_stats(self.stats[:, i, :], self.x[:, i, :]).then_inc(self.s_stats, 1)
        for i in range(TILES):
            dve.wait_ge(self.s_stats, i + 1)
            dve.bn_aggr(self.mv[:, i, :], self.stats[:, i, :]).then_inc(self.s_mv, 1)

    def pool(self, pool):
        pool.memset(self.half_power[:], -0.5).then_inc(self.s_pool, 1)
        pool.wait_ge(self.s_mv, TILES)
        pool.tensor_scalar(self.var[:], self.mv[:, :, 1], EPS, 1.0, ALU.add, ALU.mult).then_inc(self.s_pool, 1)
        pool.wait_ge(self.s_pool, 2)
        pool.tensor_tensor(self.rstd[:], self.var[:], self.half_power[:], ALU.pow).then_inc(self.s_rstd, 1)

    def vector_normalize(self, dve):
        dve.wait_ge(self.s_rstd, 1)
        for i in range(TILES):
            dve.tensor_scalar(self.xn[:, i, :], self.x[:, i, :], self.mv[:, i, 0:1], self.rstd[:, i:i + 1],
                              ALU.subtract, ALU.mult).then_inc(self.s_xn, 1)

    def tensor(self, pe):
        for h in range(HALVES):
            for i in range(4 * h, 4 * h + 4):
                pe.wait_ge(self.s_xn, i + 1)
                for k in range(KT):
                    m = pe.transpose(self.bank[2 * h + k][:, P * (i % 4):P * (i % 4) + P],
                                     self.xn[:, i, P * k:P * k + P], self.ident)
            m.then_inc(self.s_turned, 1)

    def scalar_hi(self, act, hi, banks=range(4)):
        for b in banks:
            act.wait_ge(self.s_turned, b // 2 + 1)
            act.activation(hi[:, b % 2, HALF * (b // 2):HALF * (b // 2) + HALF], self.bank[b][:],
                           ACT.Copy).then_inc(self.s_hi, 1)

    def vector_lo(self, dve, hi, lo, banks=range(4)):
        for b in banks:
            dve.wait_ge(self.s_hi, b + 1)
            sl = slice(HALF * (b // 2), HALF * (b // 2) + HALF)
            dve.tensor_tensor(lo[:, b % 2, sl], self.bank[b][:], hi[:, b % 2, sl],
                              ALU.subtract).then_inc(self.s_lo, 1)


def three_products(pe, out, w_hi, w_lo, x_hi, x_lo, start, stop, **kw):
    pe.matmul(out, w_hi, x_hi, start=start, stop=False, **kw)
    pe.matmul(out, w_hi, x_lo, start=False, stop=False, **kw)
    return pe.matmul(out, w_lo, x_hi, start=False, stop=stop, **kw)


def mamba(nc, G):
    x, bank, ident = G["x"], G["bank"], G["ident"]
    with ExitStack() as stack:
        kit = Kit(nc, stack, [])
        xbc = kit.sb("xbc", [P, CONV_BLOCKS, TOKENS])
        zs = kit.sb("silu_z", [P, TILES, HID])
        dt = kit.sb("dt", [P, TILES, HEADS])
        d_a = kit.sb("dt_times_A", [P, TILES, HEADS])
        d_skip = kit.sb("D_rows", [P, HEADS])
        norm_w = kit.sb("norm_w", [P, XB])
        w_out = kit.sb("w_out", [P, XB, DIM])
        cum_masks = kit.sb("cum_masks", [P, 2 * (LEVELS + 1), P])
        pair_masks = kit.sb("pair_masks", [P, LEVELS, P])
        s_ssd_consts = kit.sem("ssd_consts_loaded")
        with ExitStack() as inner:
            mamba_projections(nc, G, kit.part(inner), x, bank, ident, xbc, zs, dt, d_a, d_skip, norm_w, w_out,
                              cum_masks, pair_masks, s_ssd_consts)
        with ExitStack() as inner:
            mamba_scan(nc, G, kit.part(inner), x, bank, ident, xbc, zs, dt, d_a, d_skip, norm_w, w_out,
                       cum_masks, pair_masks, s_ssd_consts)
        kit.retire_semaphores()


def mamba_projections(nc, G, kit, x, bank, ident, xbc, zs, dt, d_a, d_skip, norm_w, w_out, cum_masks,
                      pair_masks, s_ssd_consts):
    D_IN = 2 * HID + 256 + HEADS
    w_raw = kit.sb("w_in_raw", [P, KT, D_IN])
    w_hi = kit.sb("w_in_hi", [P, KT, D_IN], F16)
    w_lo = kit.sb("w_in_lo", [P, KT, D_IN], F16)
    xt_hi = kit.sb("xt_hi", [P, KT, TOKENS], F16)
    xt_lo = kit.sb("xt_lo", [P, KT, TOKENS], F16)
    conv_w = kit.sb("conv_w", [P, CONV_BLOCKS, TAPS])
    dt_bias = kit.sb("dt_bias_rows", [P, HEADS])
    a_log = kit.sb("A_log_rows", [P, HEADS])
    a_exp = kit.sb("A_exp_rows", [P, HEADS])
    dt_v = kit.sb("dt_shifted", [P, TILES, HEADS])
    dt_e = kit.sb("dt_exp", [P, TILES, HEADS])
    dt_l = kit.sb("dt_log", [P, TILES, HEADS])
    ln = LayerNorm(nc, kit, "ln0", x, bank, ident)
    s_x = [kit.sem(f"x_tile{i}_loaded") for i in range(TILES)]
    s_w = kit.sem("w_in_loaded")
    s_small = kit.sem("small_loaded")
    s_w_hi = kit.sem("w_in_hi_done")
    s_w_lo = kit.sem("w_in_lo_done")
    s_mm = kit.sem("projected")
    s_dt_mm = kit.sem("dt_projected")
    s_tap0 = kit.sem("first_tap_done")
    s_taps = kit.sem("tap_done")
    s_silu = kit.sem("silu_x_done")
    s_z = kit.sem("silu_z_done")
    s_dt = kit.sem("dt_step")
    UNITS = CONV_BLOCKS * HALVES
    SMALL = 5

    def mm_bank(u):
        return bank[4 + u % 3]

    with nc.Block() as block:
        @block.sync
        def _(sp):
            for i in range(TILES):
                sp.dma_start(x[:, i, :], G["x_in"][P * i:P * i + P, :]).then_inc(s_x[i], 16)
            sp.dma_start(conv_w[:], G["conv_w"].rearrange("(j p) t -> p j t", p=P)).then_inc(s_small, 16)
            sp.dma_start(dt_bias[:], G["dt_bias"].partition_broadcast(P)).then_inc(s_small, 16)
            sp.dma_start(a_log[:], G["A_log"].partition_broadcast(P)).then_inc(s_small, 16)
            sp.dma_start(d_skip[:], G["D"].partition_broadcast(P)).then_inc(s_small, 16)
            sp.dma_start(norm_w[:], G["norm_w"]).then_inc(s_small, 16)
            sp.dma_start(cum_masks[:], G["cum_masks"]).then_inc(s_ssd_consts, 16)
            sp.dma_start(pair_masks[:], G["pair_masks"]).then_inc(s_ssd_consts, 16)
            sp.dma_start(w_out[:], G["w_out"].rearrange("(j p) n -> p j n", p=P)).then_inc(s_ssd_consts, 16)

        @block.gpsimd
        def _(pool):
            ln.pool(pool)

        @block.scalar
        def _(act):
            act.dma_start(ident, G["ident_in"]).then_inc(G["s_ident"], 16)
            act.dma_start(w_raw[:], G["w_in"].rearrange("(k p) n -> p k n", p=P)).then_inc(s_w, 16)
            act.wait_ge(s_w, 16)
            for k in range(KT):
                act.activation(w_hi[:, k, :], w_raw[:, k, :], ACT.Copy).then_inc(s_w_hi, 1)
            ln.scalar_hi(act, xt_hi)
            act.wait_ge(s_small, 16 * SMALL)

            def first_tap(u):
                fb, h = u % CONV_BLOCKS, u // CONV_BLOCKS
                act.wait_ge(s_mm, u + 1)
                act.activation(xbc[:, fb, HALF * h:HALF * h + HALF], mm_bank(u)[:], ACT.Copy,
                               scale=conv_w[:, fb, TAPS - 1:TAPS]).then_inc(s_tap0, 1)

            def silu_x(u):
                fb, h = u % CONV_BLOCKS, u // CONV_BLOCKS
                act.wait_ge(s_taps, 3 * (u + 1))
                act.activation(xbc[:, fb, HALF * h:HALF * h + HALF], xbc[:, fb, HALF * h:HALF * h + HALF],
                               ACT.Silu).then_inc(s_silu, 1)

            for u in range(UNITS):
                first_tap(u)
                if u >= 2:
                    silu_x(u - 2)
            silu_x(UNITS - 2)
            silu_x(UNITS - 1)
            for i in range(TILES):
                act.wait_ge(s_mm, UNITS + i + 1)
                act.activation(zs[:, i, :], mm_bank(UNITS + i)[:], ACT.Silu).then_inc(s_z, 1)
            act.activation(a_exp[:], a_log[:], ACT.Exp).then_inc(s_dt, 1)
            act.wait_ge(s_dt, 2)
            act.activation(dt_e[:], dt_v[:], ACT.Abs).then_inc(s_dt, 1)
            act.wait_ge(s_dt, 3)
            act.activation(dt_e[:], dt_e[:], ACT.Exp, scale=-1.0).then_inc(s_dt, 1)
            act.wait_ge(s_dt, 4)
            act.activation(dt_l[:], dt_e[:], ACT.Ln, bias=1.0).then_inc(s_dt, 1)

        @block.tensor
        def _(pe):
            pe.wait_ge(G["s_ident"], 16)
            ln.tensor(pe)
            pe.wait_ge(s_w_lo, KT)
            for u in range(UNITS):
                fb, h = u % CONV_BLOCKS, u // CONV_BLOCKS
                pe.wait_ge(ln.s_lo, 2 * (h + 1))
                if u >= 3:
                    pe.wait_ge(s_taps, 3 * (u - 2))
                for k in range(KT):
                    c = slice(X0 + P * fb, X0 + P * fb + P)
                    t = slice(HALF * h, HALF * h + HALF)
                    m = three_products(pe, mm_bank(u)[:], w_hi[:, k, c], w_lo[:, k, c], xt_hi[:, k, t],
                                       xt_lo[:, k, t], k == 0, k == KT - 1)
                m.then_inc(s_mm, 1)
            for i in range(TILES):
                u = UNITS + i
                if i < 3:
                    pe.wait_ge(s_taps, 3 * (u - 2))
                else:
                    pe.wait_ge(s_z, i - 2)
                t = slice(P * i, P * i + P)
                for k in range(KT):
                    m = three_products(pe, mm_bank(u)[:], xt_hi[:, k, t], xt_lo[:, k, t], w_hi[:, k, Z0:Z0 + HID],
                                       w_lo[:, k, Z0:Z0 + HID], k == 0, k == KT - 1)
                m.then_inc(s_mm, 1)
                for k in range(KT):
                    m = three_products(pe, bank[7][:, HEADS * i:HEADS * i + HEADS], xt_hi[:, k, t], xt_lo[:, k, t],
                                       w_hi[:, k, DT0:D_IN], w_lo[:, k, DT0:D_IN], k == 0, k == KT - 1)
            m.then_inc(s_dt_mm, 1)

        @block.vector
        def _(dve):
            ln.vector_stats(dve, lambda i: dve.wait_ge(s_x[i], 16))
            ln.vector_normalize(dve)
            for k in range(KT):
                dve.wait_ge(s_w_hi, k + 1)
                dve.tensor_tensor(w_lo[:, k, :], w_raw[:, k, :], w_hi[:, k, :], ALU.subtract).then_inc(s_w_lo, 1)
            ln.vector_lo(dve, xt_hi, xt_lo)
            for u in range(UNITS):
                fb, h = u % CONV_BLOCKS, u // CONV_BLOCKS
                dve.wait_ge(s_tap0, u + 1)
                src = mm_bank(u)[:].rearrange("p (b s) -> p b s", s=SEQ)
                acc = xbc[:, fb, HALF * h:HALF * h + HALF].rearrange("p (b s) -> p b s", s=SEQ)
                for tap in range(1, TAPS):
                    if tap > 1:
                        dve.wait_ge(s_taps, 3 * u + tap - 1)
                    dve.scalar_tensor_tensor(acc[:, :, tap:], src[:, :, :SEQ - tap],
                                             conv_w[:, fb, TAPS - 1 - tap:TAPS - tap], acc[:, :, tap:],
                                             ALU.mult, ALU.add).then_inc(s_taps, 1)
            dve.wait_ge(s_dt_mm, 1)
            dve.wait_ge(s_dt, 1)
            dve.tensor_tensor(dt_v[:], bank[7][:].rearrange("p (t h) -> p t h", h=HEADS),
                              bc(dt_bias[:], 1, TILES), ALU.add).then_inc(s_dt, 1)
            dve.wait_ge(s_dt, 5)
            dve.scalar_tensor_tensor(dt[:], dt_v[:], 0.0, dt_l[:], ALU.max, ALU.add).then_inc(s_dt, 1)
            dve.wait_ge(s_dt, 6)
            dve.scalar_tensor_tensor(d_a[:], dt[:], -1.0, bc(a_exp[:], 1, TILES), ALU.mult,
                                     ALU.mult).then_inc(s_dt, 1)
            dve.wait_ge(s_dt, 7)


def mamba_scan(nc, G, kit, x, bank, ident, xbc, zs, dt, d_a, d_skip, norm_w, w_out, cum_masks, pair_masks,
               s_ssd_consts):
    SIDES = LEVELS + 1
    BUFS = 6
    ADD_LAG = 3
    fs = kit.sb("source_factors", [P, SIDES, TILES, HEADS])
    fl = kit.sb("target_factors", [P, SIDES, TILES, HEADS])
    x_tok = kit.sb("x_tok", [P, 2, HID])
    scaled = kit.sb("scaled_x", [P, 2, SIDES, HID])
    g_all = kit.sb("g_scores", [P, 3, SEQ])
    g_masked = kit.sb("g_masked", [P, 2, LEVELS, P])
    g_diag = kit.sb("g_diag", [P, TILES])
    junk = kit.sb("diag_products", [P, 2, P])
    coef = kit.sb("diag_coef", [P, 2, HEADS])
    terms = kit.sb("terms", [P, BUFS, HID])
    y = kit.sb("y", [P, TILES, HID])
    square = kit.sb("squares", [P, 2, HID])
    mean_sq = kit.sb("sum_squares", [P, TILES])
    mean_eps = kit.sb("mean_squares_eps", [P, TILES])
    half_power = kit.sb("minus_half", [P, TILES])
    rstd = kit.sb("rms_rstd", [P, TILES])
    yt = kit.sb("y_turned", [P, 2, XB, P])
    s_cum = kit.sem("cum_done")
    s_fac = kit.sem("factor_exp_done")
    s_fs = kit.sem("source_factor_done")
    s_xt = kit.sem("x_turned")
    s_xtok = kit.sem("x_tok_done")
    s_g = kit.sem("g_done")
    s_gs = kit.sem("g_saved")
    s_gm = kit.sem("g_masked_done")
    s_gd = kit.sem("g_diag_done")
    s_coef = kit.sem("coef_done")
    s_scaled = kit.sem("x_scaled")
    s_lvl = kit.sem("level_product_done")
    s_term = kit.sem("term_done")
    s_y = kit.sem("y_added")
    s_acc = kit.sem("term_accumulated")
    s_sum = kit.sem("y_summed")
    s_gate = kit.sem("y_gated")
    s_sq = kit.sem("squares_done")
    s_const = kit.sem("half_power_done")
    s_wout = kit.sem("w_out_scaled")
    s_mean = kit.sem("mean_squares_done")
    s_rms = kit.sem("rms_rstd_done")
    s_yt = kit.sem("y_turned_done")
    s_yts = kit.sem("y_turned_saved")
    s_out = kit.sem("out_projected")
    s_res = kit.sem("residual_added")

    products = []
    for i in range(TILES):
        levels = ([LEVELS] if i % 2 else []) + list(range(LEVELS))
        products += [(i, k, place) for place, k in enumerate(levels)]
    ON_PE = (2, 3, 4)
    last = {i: n for n, (i, k, place) in enumerate(products)}
    y_count, acc_count = {}, {}
    start_count = {}
    ys = accs = 0
    for n, (i, k, place) in enumerate(products):
        if place == 0:
            ys += 1
            start_count[i] = ys
        if place in ON_PE:
            accs += 1
        else:
            ys += 1
        y_count[n], acc_count[n] = ys, accs

    def scaled_count(i, k):
        return 8 * i - i // 2 + k + 1

    def wait_consumed(eng, n):
        if products[n][2] in ON_PE:
            eng.wait_ge(s_acc, acc_count[n])
        else:
            eng.wait_ge(s_y, y_count[n])

    def by_head(ap):
        return ap.rearrange("p (h e) -> p h e", e=HEAD_DIM)

    with nc.Block() as block:
        @block.tensor
        def _(pe):
            pe.wait_ge(s_ssd_consts, 48)
            for m in range(2 * SIDES):
                if m >= 4:
                    pe.wait_ge(s_fac, m - 3)
                pe.matmul(bank[m % 4][:], cum_masks[:, m, :], d_a[:].rearrange("p t h -> p (t h)"),
                          start=True, stop=True).then_inc(s_cum, 1)

            def turn(i):
                if i >= 1:
                    pe.wait_ge(s_xtok, i)
                for j in range(XB):
                    m = pe.transpose(bank[4][:, P * j:P * j + P], xbc[:, j, P * i:P * i + P], ident)
                m.then_inc(s_xt, 1)
                if i >= 1:
                    pe.wait_ge(s_gs, i)
                n = SEQ if i % 2 == 0 else P
                pe.matmul(bank[5][:, 0:n], xbc[:, XB, P * i:P * i + P], xbc[:, XB + 1, P * i:P * i + n],
                          start=True, stop=True).then_inc(s_g, 1)

            def accumulate(n):
                i, k, place = products[n]
                if place == ON_PE[0] and i >= 1:
                    pe.wait_ge(s_sum, i)
                pe.wait_ge(s_term, n + 1)
                pe.matmul(bank[6][:], ident, terms[:, n % BUFS, :], start=(place == ON_PE[0]),
                          stop=(place == ON_PE[-1])).then_inc(s_acc, 1)

            def turn_y(i):
                pe.wait_ge(s_gate, i + 1)
                if i >= 1:
                    pe.wait_ge(s_yts, i)
                for j in range(XB):
                    m = pe.transpose(bank[3][:, P * j:P * j + P], y[:, i, P * j:P * j + P], ident)
                m.then_inc(s_yt, 1)

            def project(i):
                pe.wait_ge(s_yts, i + 1)
                if i == 0:
                    pe.wait_ge(s_wout, 1)
                else:
                    pe.wait_ge(s_res, i)
                for j in range(XB):
                    m = pe.matmul(bank[7][:, 0:DIM], yt[:, i % 2, j, :], w_out[:, j, :], start=(j == 0),
                                  stop=(j == XB - 1))
                m.then_inc(s_out, 1)

            turn(0)
            turn(1)
            pe.wait_ge(s_fac, 2 * SIDES)
            for n, (i, k, place) in enumerate(products):
                if n >= 3:
                    pe.wait_ge(s_term, n - 2)
                if k < LEVELS:
                    if k == 0:
                        pe.wait_ge(s_gm, 2 * i + 1)
                    if k == 4:
                        pe.wait_ge(s_gm, 2 * i + 2)
                    pe.wait_ge(s_scaled, scaled_count(i, k))
                    weights, moving = g_masked[:, i % 2, k, :], scaled[:, i % 2, k, :]
                else:
                    pe.wait_ge(s_scaled, scaled_count(i - 1, k))
                    pe.wait_ge(s_gs, i)
                    weights, moving = g_all[:, (i - 1) % 3, P:SEQ], scaled[:, 0, LEVELS, :]
                pe.matmul(bank[n % 3][:], weights, moving, start=True, stop=True).then_inc(s_lvl, 1)
                if n >= ADD_LAG and products[n - ADD_LAG][2] in ON_PE:
                    accumulate(n - ADD_LAG)
                if place == 4 and i + 2 < TILES:
                    turn(i + 2)
                if place == 6 and i >= 1:
                    turn_y(i - 1)
                if place == 2 and i >= 2:
                    project(i - 2)
            turn_y(TILES - 1)
            project(TILES - 2)
            project(TILES - 1)

        @block.scalar
        def _(act):
            for m in range(2 * SIDES):
                side, k = m // SIDES, m % SIDES
                act.wait_ge(s_cum, m + 1)
                dst = (fs, fl)[side]
                act.activation(dst[:, k, :, :].rearrange("p t h -> p (t h)"), bank[m % 4][:],
                               ACT.Exp).then_inc(s_fac, 1)

            def save_turned(i):
                act.wait_ge(s_xt, i + 1)
                if i >= 2:
                    act.wait_ge(s_scaled, scaled_count(i - 2, LEVELS - 1 if i % 2 else LEVELS))
                    act.wait_ge(s_y, start_count[i - 2])
                act.activation(x_tok[:, i % 2, :], bank[4][:], ACT.Copy).then_inc(s_xtok, 1)
                n = SEQ if i % 2 == 0 else P
                act.wait_ge(s_g, i + 1)
                if i >= 3:
                    act.wait_ge(s_gm, 2 * (i - 2))
                    act.wait_ge(s_gd, i - 2)
                    act.wait_ge(s_lvl, last[i - 3] + 2)
                act.activation(g_all[:, i % 3, 0:n], bank[5][:, 0:n], ACT.Copy).then_inc(s_gs, 1)

            def squares(i):
                act.wait_ge(s_gate, i + 1)
                if i >= 2:
                    act.wait_ge(s_sq, i - 1)
                act.activation(square[:, i % 2, :], y[:, i, :], ACT.Square,
                               accum_out=mean_sq[:, i:i + 1]).then_inc(s_sq, 1)

            def save_y(i):
                act.wait_ge(s_yt, i + 1)
                if i >= 2:
                    act.wait_ge(s_out, i - 1)
                act.activation(yt[:, i % 2].rearrange("p j t -> p (j t)"), bank[3][:], ACT.Copy).then_inc(s_yts, 1)

            save_turned(0)
            save_turned(1)
            for i in range(TILES + 1):
                if i >= 1:
                    squares(i - 1)
                if i + 2 < TILES:
                    save_turned(i + 2)
                if i >= 1:
                    save_y(i - 1)

        @block.vector
        def _(dve):
            dtf = dt[:].rearrange("p t h -> p (t h)")
            for k in range(SIDES):
                dve.wait_ge(s_fac, k + 1)
                f = fs[:, k, :, :].rearrange("p t h -> p (t h)")
                dve.tensor_tensor(f, f, dtf, ALU.mult).then_inc(s_fs, 1)
            dve.wait_ge(s_fs, SIDES)

            def scale(i, k):
                if k == 0:
                    dve.wait_ge(s_xtok, i + 1)
                dve.tensor_tensor(by_head(scaled[:, i % 2, k, :]), by_head(x_tok[:, i % 2, :]),
                                  bc(fs[:, k, i, :], 2, HEAD_DIM), ALU.mult).then_inc(s_scaled, 1)

            def diag(i):
                dve.wait_ge(s_gs, i + 1)
                if i >= 2:
                    dve.wait_ge(s_gd, i - 1)
                dve.tensor_tensor_reduce(junk[:, i % 2, :], g_all[:, i % 3, 0:P], ident, 1.0, 0.0, ALU.mult,
                                         ALU.add, g_diag[:, i:i + 1]).then_inc(s_gd, 1)
                dve.wait_ge(s_gd, i + 1)
                if i >= 2:
                    dve.wait_ge(s_y, start_count[i - 2])
                dve.scalar_tensor_tensor(coef[:, i % 2, :], dt[:, i, :], g_diag[:, i:i + 1], d_skip[:], ALU.mult,
                                         ALU.add).then_inc(s_coef, 1)

            def add_accumulated(i):
                dve.wait_ge(s_acc, acc_count[last[i]])
                dve.wait_ge(s_y, y_count[last[i]])
                dve.tensor_tensor(y[:, i, :], y[:, i, :], bank[6][:], ALU.add).then_inc(s_sum, 1)

            def residual(i):
                dve.wait_ge(s_out, i + 1)
                dve.wait_ge(s_rms, i + 1)
                dve.scalar_tensor_tensor(x[:, i, :], bank[7][:, 0:DIM], rstd[:, i:i + 1], x[:, i, :], ALU.mult,
                                         ALU.add).then_inc(s_res, 1)

            for k in range(SIDES):
                scale(0, k)
            diag(0)
            for n, (i, k, place) in enumerate(products):
                dve.wait_ge(s_lvl, n + 1)
                if n >= BUFS:
                    wait_consumed(dve, n - BUFS)
                dve.tensor_tensor(by_head(terms[:, n % BUFS, :]), by_head(bank[n % 3][:]),
                                  bc(fl[:, k, i, :], 2, HEAD_DIM), ALU.mult).then_inc(s_term, 1)
                if i + 1 < TILES:
                    scale(i + 1, place)
                    if place == 1:
                        diag(i + 1)
                if place == 3 and i >= 1:
                    add_accumulated(i - 1)
                if place == 5 and i >= 2:
                    residual(i - 2)
            add_accumulated(TILES - 1)
            residual(TILES - 2)
            residual(TILES - 1)
            dve.wait_ge(s_res, TILES)

        @block.gpsimd
        def _(pool):
            pool.memset(half_power[:], -0.5).then_inc(s_const, 1)

            def mask(i, part):
                lo, hi = ((0, 4), (4, LEVELS))[part]
                pool.wait_ge(s_gs, i + 1)
                if i >= 2:
                    pool.wait_ge(s_lvl, last[i - 2] + 1)
                pool.tensor_tensor(g_masked[:, i % 2, lo:hi, :], pair_masks[:, lo:hi, :],
                                   bc(g_all[:, i % 3, 0:P], 1, hi - lo), ALU.mult).then_inc(s_gm, 1)

            def gate(i):
                pool.wait_ge(s_sum, i + 1)
                pool.tensor_tensor(y[:, i, :], y[:, i, :], zs[:, i, :], ALU.mult).then_inc(s_gate, 1)

            def rms(i):
                pool.wait_ge(s_sq, i + 1)
                pool.tensor_scalar(mean_eps[:, i:i + 1], mean_sq[:, i:i + 1], 1.0 / HID, EPS, ALU.mult,
                                   ALU.add).then_inc(s_mean, 1)
                pool.wait_ge(s_mean, i + 1)
                if i == 0:
                    pool.wait_ge(s_const, 1)
                pool.tensor_tensor(rstd[:, i:i + 1], mean_eps[:, i:i + 1], half_power[:, i:i + 1],
                                   ALU.pow).then_inc(s_rms, 1)

            pool.wait_ge(s_ssd_consts, 48)
            pool.tensor_tensor(w_out[:], w_out[:], bc(norm_w[:], 2, DIM), ALU.mult).then_inc(s_wout, 1)
            mask(0, 0)
            mask(0, 1)
            for n, (i, k, place) in enumerate(products):
                if place == 0:
                    pool.wait_ge(s_coef, i + 1)
                    pool.tensor_tensor(by_head(y[:, i, :]), by_head(x_tok[:, i % 2, :]),
                                       bc(coef[:, i % 2, :], 2, HEAD_DIM), ALU.mult).then_inc(s_y, 1)
                if place in (2, 4) and i + 1 < TILES:
                    mask(i + 1, place // 2 - 1)
                if place not in ON_PE:
                    pool.wait_ge(s_term, n + 1)
                    pool.wait_ge(s_y, y_count[n] - 1)
                    pool.tensor_tensor(y[:, i, :], y[:, i, :], terms[:, n % BUFS, :], ALU.add).then_inc(s_y, 1)
                if place == 4 and i >= 1:
                    gate(i - 1)
                if place == 6 and i >= 1:
                    rms(i - 1)
            gate(TILES - 1)
            rms(TILES - 1)
            pool.wait_ge(s_rms, TILES)


L0_FEATURES, L0_EXPERTS, L0_TOP = 176, 8, 2
L0_BLOCKS, L0_SCORED = 14, 11
L1_FEATURES, L1_EXPERTS, L1_TOP = 256, 16, 4
L1_BLOCKS = L1_EXPERTS * L1_FEATURES // P
ALPHA, LIMIT = 1.702, 7.0


def moe(nc, G, layer):
    clamped = layer == 1
    name = f"moe{layer}"
    E, TOP = (L1_EXPERTS, L1_TOP) if clamped else (L0_EXPERTS, L0_TOP)
    BLOCKS = L1_BLOCKS if clamped else L0_BLOCKS
    FEATURES = L1_FEATURES if clamped else L0_FEATURES
    x, bank, ident = G["x"], G["bank"], G["ident"]
    w_gu_dram, w_d_dram = G[name + "_gate_up"], G[name + "_down"]
    score_dram = nc.dram_tensor(name + "_scores_dram", (E, TOKENS), F32, kind="Internal").ap()
    with ExitStack() as stack:
        kit = Kit(nc, stack, [])
        xt_hi = kit.sb(name + "_xt_hi", [P, KT, TOKENS], F16)
        xt_lo = kit.sb(name + "_xt_lo", [P, KT, TOKENS], F16)
        raw_gu = kit.sb(name + "_raw_gate_up", [P, 2, 512])
        raw_d = kit.sb(name + "_raw_down", [P, 2, DIM])
        gu_hi = kit.sb(name + "_gate_up_hi", [P, 2, 2, KT, P], F16)
        gu_lo = kit.sb(name + "_gate_up_lo", [P, 2, 2, KT, P], F16)
        d_hi = kit.sb(name + "_down_hi", [P, 2, DIM], F16)
        d_lo = kit.sb(name + "_down_lo", [P, 2, DIM], F16)
        scores = kit.sb(name + "_scores_spread", [P, BLOCKS if not clamped else E, TOKENS])
        r_raw = kit.sb(name + "_router", [P, KT, E])
        r_hi = kit.sb(name + "_router_hi", [P, KT, E], F16)
        r_lo = kit.sb(name + "_router_lo", [P, KT, E], F16)
        lower = kit.sb(name + "_lower_expert", [P, E, E])
        logits = kit.sb(name + "_logits", [P, TILES, E])
        peak = kit.sb(name + "_peak", [P, TILES])
        weight = kit.sb(name + "_weight", [P, TILES, E])
        beats = kit.sb(name + "_beats", [P, TILES, E, E])
        ties = kit.sb(name + "_ties", [P, TILES, E, E])
        rank = kit.sb(name + "_rank", [P, TILES, E])
        total = kit.sb(name + "_total", [P, TILES])
        score_t = kit.sb(name + "_scores_turned", [E, TOKENS])
        gate = kit.sb(name + "_gate", [P, 2, HALF])
        sig = kit.sb(name + "_sigmoid", [P, 2, HALF])
        act_out = kit.sb(name + "_activated", [P, 2, HALF])
        hid = kit.sb(name + "_hidden", [P, 2, HALF])
        h_hi = kit.sb(name + "_hidden_hi", [P, 2, HALF], F16)
        h_lo = kit.sb(name + "_hidden_lo", [P, 2, HALF], F16)
        out_t = kit.sb(name + "_out_turned", [P, 2, TOKENS])
        if clamped:
            up = kit.sb(name + "_up", [P, 2, HALF])
            up_clipped = kit.sb(name + "_up_clipped", [P, 2, HALF])
            up_scored = kit.sb(name + "_up_scored", [P, 2, HALF])
            glu = kit.sb(name + "_glu", [P, 2, HALF])
            r_bias = kit.sb(name + "_router_bias", [P, E])
            biases = kit.sb(name + "_biases", [P, 2, BLOCKS])
            down_bias = kit.sb(name + "_down_bias", [E, DIM])
        ln = LayerNorm(nc, kit, name + "_ln", x, bank, ident)
        s_small = kit.sem(name + "_small_loaded")
        s_raw_gu = [kit.sem(name + f"_raw_gate_up{p}_loaded") for p in range(2)]
        s_raw_d = [kit.sem(name + f"_raw_down{p}_loaded") for p in range(2)]
        s_gu_hi = kit.sem(name + "_gate_up_hi_done")
        s_gu_lo = kit.sem(name + "_gate_up_lo_done")
        s_d_hi = kit.sem(name + "_down_hi_done")
        s_d_lo = kit.sem(name + "_down_lo_done")
        s_r_hi = kit.sem(name + "_router_hi_done")
        s_r_lo = kit.sem(name + "_router_lo_done")
        s_logits = kit.sem(name + "_logits_done")
        s_route = kit.sem(name + "_routing_step")
        s_exp = kit.sem(name + "_routing_exp_done")
        s_routed = kit.sem(name + "_routed")
        s_score_t = kit.sem(name + "_scores_turned_done")
        s_score_s = kit.sem(name + "_scores_saved")
        s_score_w = kit.sem(name + "_scores_written")
        s_spread = [kit.sem(name + f"_scores_spread_part{j}_done") for j in range(3)]
        s_ones = kit.sem(name + "_ones_done")
        s_gu_mm = kit.sem(name + "_gate_up_product_done")
        s_gate = kit.sem(name + "_gate_done")
        s_up = kit.sem(name + "_up_done")
        s_clip = kit.sem(name + "_up_clipped_done")
        s_scored = kit.sem(name + "_up_scored_done")
        s_sig = kit.sem(name + "_sigmoid_done")
        s_glu = kit.sem(name + "_glu_done")
        s_acted = kit.sem(name + "_activated_done")
        s_turns = kit.sem(name + "_score_turn")
        s_act_turns = kit.sem(name + "_bias_turn")
        s_hid = kit.sem(name + "_hidden_done")
        s_h_hi = kit.sem(name + "_hidden_hi_done")
        s_h_lo = kit.sem(name + "_hidden_lo_done")
        s_down = kit.sem(name + "_down_product_done")
        s_out_s = kit.sem(name + "_out_saved")
        s_out_t = kit.sem(name + "_out_turned_done")
        s_res = kit.sem(name + "_residual_added")
        SMALL = 5 if clamped else 2
        pieces = []
        if clamped:
            pieces = [(e, 0, P, e) for e in range(E)]
        else:
            for b in range(L0_SCORED):
                a = 0
                while a < P:
                    e = (P * b + a) // FEATURES
                    end = min(P, (e + 1) * FEATURES - P * b)
                    pieces.append((b, a, end, e))
                    a = end

        part_starts = (0, 1, 3) if clamped else (0, 2, 3)

        def part_of(b):
            return sum(b >= s for s in part_starts) - 1

        part_sizes = [sum(part_of(b) == j for b, _, _, _ in pieces) for j in range(3)]

        def block_stages(eng, stage, peeled=()):
            stage(0, 0, True, False)
            stage(1, 1, True, False)
            for b, step in enumerate(peeled, 2):
                step()
                stage(b, b % 2, False, False)
            with eng.Fori(2 if peeled else 1, BLOCKS // 2 - 1, 1) as i:
                stage(2 * i, 0, False, False)
                stage(2 * i + 1, 1, False, False)
            stage(BLOCKS - 2, 0, False, False)
            stage(BLOCKS - 1, 1, False, True)

        with nc.Block() as block:
            @block.sync
            def _(sp):
                sp.dma_start(r_raw[:], G[name + "_router"].rearrange("(k p) e -> p k e", p=P)).then_inc(s_small, 16)
                sp.dma_start(lower[:], G[name + "_lower_expert"].partition_broadcast(P)).then_inc(s_small, 16)
                if clamped:
                    sp.dma_start(r_bias[:], G["moe1_router_bias"].partition_broadcast(P)).then_inc(s_small, 16)
                    sp.dma_start(biases[:], G["moe1_biases"]).then_inc(s_small, 16)
                    sp.dma_start(down_bias[:], G["moe1_down_bias"]).then_inc(s_small, 16)

                def stage(b, par, first, last):
                    if not first:
                        sp.wait_ge(s_gu_lo, b - 1)
                    sp.dma_start(raw_gu[:, par, :], w_gu_dram[bass.ds(b * P, P), :]).then_inc(s_raw_gu[par], 16)
                    if not first:
                        sp.wait_ge(s_d_lo, b - 1)
                    sp.dma_start(raw_d[:, par, :], w_d_dram[bass.ds(b * P, P), :]).then_inc(s_raw_d[par], 16)

                def spread(parts):
                    for b, a, end, e in pieces:
                        if part_of(b) in parts:
                            sp.dma_start(scores[a:end, b, :], score_dram[e:e + 1, :].partition_broadcast(end - a)
                                         ).then_inc(s_spread[part_of(b)], 16)

                def spread_first():
                    sp.wait_ge(s_score_s, HALVES)
                    sp.dma_start(score_dram, score_t[:]).then_inc(s_score_w, 16)
                    sp.wait_ge(s_score_w, 16)
                    spread((0, 1) if clamped else (0,))

                block_stages(sp, stage, (spread_first, lambda: spread((2,) if clamped else (1, 2))))

            @block.gpsimd
            def _(pool):
                ln.pool(pool)
                if not clamped:
                    pool.memset(scores[:, L0_SCORED:BLOCKS, :], 1.0).then_inc(s_ones, 1)
                if not clamped:
                    pool.wait_ge(s_ones, 1)
                pool.wait_ge(s_spread[0], 16 * part_sizes[0])


                def stage(b, par, first, last):
                    for h in range(HALVES):
                        u = 2 * b + h
                        later = not (first and par == 0)
                        pool.wait_ge(s_acted, u + 1)
                        if later:
                            pool.wait_ge(s_h_lo, u - 1)
                        row = scores[:, bass.ds(b, 1), HALF * h:HALF * h + HALF].squeeze(1)
                        pool.tensor_tensor(hid[:, h, :], act_out[:, h, :], row, ALU.mult).then_inc(s_hid, 1)

                if clamped:
                    def pair(i):
                        for par in range(2):
                            for h in range(HALVES):
                                u = 4 * i + 2 * par + h
                                later = not (isinstance(i, int) and i == 0 and par == 0)
                                pool.wait_ge(s_clip, u + 1)
                                if later:
                                    pool.wait_ge(s_hid, u - 1)
                                pool.sem_inc(s_turns, 1)
                                row = scores[:, bass.ds(i, 1), HALF * h:HALF * h + HALF].squeeze(1)
                                pool.tensor_tensor(up_scored[:, h, :], up_clipped[:, h, :], row,
                                                   ALU.mult).then_inc(s_scored, 1)
                                pool.wait_ge(s_sig, u + 1)
                                pool.tensor_tensor(glu[:, h, :], gate[:, h, :], sig[:, h, :],
                                                   ALU.mult).then_inc(s_glu, 1)
                    pair(0)
                    pool.wait_ge(s_spread[1], 16 * part_sizes[1])
                    with pool.Fori(part_starts[1], part_starts[2], 1) as i:
                        pair(i)
                    pool.wait_ge(s_spread[2], 16 * part_sizes[2])
                    with pool.Fori(part_starts[2], E, 1) as i:
                        pair(i)
                else:
                    block_stages(pool, stage, (lambda: pool.wait_ge(s_spread[1], 16 * part_sizes[1]),
                                               lambda: pool.wait_ge(s_spread[2], 16 * part_sizes[2])))

            @block.scalar
            def _(act):
                act.wait_ge(s_small, 16 * SMALL)
                act.activation(r_hi[:], r_raw[:], ACT.Copy).then_inc(s_r_hi, 1)
                act.wait_ge(s_raw_gu[0], 16)
                act.activation(gu_hi[:, 0].rearrange("p g k f -> p (g k f)"), raw_gu[:, 0, :],
                               ACT.Copy).then_inc(s_gu_hi, 1)
                ln.scalar_hi(act, xt_hi)
                act.wait_ge(s_route, 2)
                act.activation(weight[:], weight[:], ACT.Exp).then_inc(s_exp, 1)
                for h in range(HALVES):
                    act.wait_ge(s_score_t, h + 1)
                    act.activation(score_t[:, HALF * h:HALF * h + HALF], bank[4 + h][0:E, :],
                                   ACT.Copy).then_inc(s_score_s, 1)

                def hidden_hi(u, h, later):
                    act.wait_ge(s_hid, u + 1)
                    if later:
                        act.wait_ge(s_down, u - 1)
                    act.activation(h_hi[:, h, :], hid[:, h, :], ACT.Copy).then_inc(s_h_hi, 1)

                def stage(b, par, first, last):
                    for h in range(HALVES):
                        u = 2 * b + h
                        later = not (first and par == 0)
                        if clamped:
                            act.wait_ge(s_gu_mm, u + 1)
                            if later:
                                act.wait_ge(s_clip, u - 1)
                            act.sem_inc(s_act_turns, 1)
                            act.activation(up[:, h, :], bank[2 * h + 1][:], ACT.Identity,
                                           bias=biases[:, 1, bass.ds(b, 1)]).then_inc(s_up, 1)
                            act.wait_ge(s_gate, u + 1)
                            if later:
                                act.wait_ge(s_glu, u - 1)
                            act.activation(sig[:, h, :], gate[:, h, :], ACT.Sigmoid, scale=ALPHA).then_inc(s_sig, 1)
                        if not (first and par == 0 and h == 0):
                            hidden_hi(u - 1, 1 - h, not (first and (par == 0 or h == 0)))
                        if not clamped:
                            act.wait_ge(s_gu_mm, u + 1)
                            if later:
                                act.wait_ge(s_acted, u - 1)
                            act.activation(gate[:, h, :], bank[2 * h][:], ACT.Silu).then_inc(s_gate, 1)
                        if h == 0 and not last:
                            act.wait_ge(s_raw_gu[1 - par], raw_loaded(b + 1, 1 - par))
                            act.wait_ge(s_gu_mm, 2 * b if not (first and par == 0) else 1)
                            act.activation(gu_hi[:, 1 - par].rearrange("p g k f -> p (g k f)"), raw_gu[:, 1 - par, :],
                                           ACT.Copy).then_inc(s_gu_hi, 1)
                        if h == 0:
                            act.wait_ge(s_raw_d[par], raw_loaded(b, par))
                            if not first:
                                act.wait_ge(s_down, 2 * b - 2)
                            act.activation(d_hi[:, par, :], raw_d[:, par, :], ACT.Copy).then_inc(s_d_hi, 1)

                def raw_loaded(b, par):
                    return 8 * (b - par) + 16

                block_stages(act, stage)
                hidden_hi(2 * BLOCKS - 1, 1, True)
                act.wait_ge(s_down, 2 * BLOCKS)
                for o in range(2):
                    act.activation(out_t[:, o, 0:HALF], bank[4 + 2 * o][:], ACT.Copy).then_inc(s_out_s, 1)

            @block.vector
            def _(dve):
                ln.vector_stats(dve)
                dve.wait_ge(s_r_hi, 1)
                dve.tensor_tensor(r_lo[:], r_raw[:], r_hi[:], ALU.subtract).then_inc(s_r_lo, 1)
                if clamped:
                    dve.tensor_scalar(biases[:, 1, :], biases[:, 1, :], 1.0, None, ALU.add).then_inc(s_r_lo, 1)
                ln.vector_normalize(dve)
                ln.vector_lo(dve, xt_hi, xt_lo)
                dve.wait_ge(s_gu_hi, 1)
                dve.tensor_tensor(gu_lo[:, 0].rearrange("p g k f -> p (g k f)"), raw_gu[:, 0, :],
                                  gu_hi[:, 0].rearrange("p g k f -> p (g k f)"), ALU.subtract).then_inc(s_gu_lo, 1)
                n = 0

                def step(ins):
                    nonlocal n
                    n += 1
                    ins.then_inc(s_route, 1)
                    dve.wait_ge(s_route, n)

                dve.wait_ge(s_logits, 1)
                lg = bank[4][:, 0:TILES * E].rearrange("p (t e) -> p t e", e=E)
                if clamped:
                    dve.tensor_tensor(logits[:], lg, bc(r_bias[:], 1, TILES), ALU.add).then_inc(s_routed, 1)
                else:
                    dve.tensor_copy(logits[:], lg).then_inc(s_routed, 1)
                dve.wait_ge(s_routed, 1)
                step(dve.tensor_reduce(peak[:], logits[:], AX.X, ALU.max))
                step(dve.tensor_tensor(weight[:], logits[:], bc(peak[:], 2, E), ALU.subtract))
                dve.wait_ge(s_exp, 1)
                ranked = logits
                if not clamped:
                    step(dve.tensor_reduce(total[:], weight[:], AX.X, ALU.add))
                    step(dve.reciprocal(total[:], total[:]))
                    step(dve.tensor_tensor(weight[:], weight[:], bc(total[:], 2, E), ALU.mult))
                    ranked = weight
                mine, other = bc(ranked[:], 3, E), bc(ranked[:], 2, E)
                step(dve.tensor_tensor(beats[:], other, mine, ALU.is_gt))
                step(dve.tensor_tensor(ties[:], other, mine, ALU.is_equal))
                step(dve.tensor_tensor(ties[:], ties[:], bc(lower[:], 1, TILES), ALU.mult))
                step(dve.tensor_tensor(beats[:], beats[:], ties[:], ALU.add))
                step(dve.tensor_reduce(rank[:], beats[:], AX.X, ALU.add))
                step(dve.scalar_tensor_tensor(weight[:], rank[:], float(TOP), weight[:], ALU.is_lt, ALU.mult))
                step(dve.tensor_reduce(total[:], weight[:], AX.X, ALU.add))
                if not clamped:
                    step(dve.tensor_scalar(total[:], total[:], 1e-20, None, ALU.add))
                step(dve.reciprocal(total[:], total[:]))
                dve.tensor_tensor(weight[:], weight[:], bc(total[:], 2, E), ALU.mult).then_inc(s_routed, 1)

                def hidden(u, h, later):
                    dve.wait_ge(s_glu, u + 1)
                    dve.wait_ge(s_scored, u + 1)
                    if later:
                        dve.wait_ge(s_h_lo, u - 1)
                    dve.tensor_tensor(hid[:, h, :], up_scored[:, h, :], glu[:, h, :], ALU.mult).then_inc(s_hid, 1)

                def hidden_lo(u, h):
                    dve.wait_ge(s_h_hi, u + 1)
                    dve.tensor_tensor(h_lo[:, h, :], hid[:, h, :], h_hi[:, h, :], ALU.subtract).then_inc(s_h_lo, 1)

                def stage(b, par, first, last):
                    for h in range(HALVES):
                        u = 2 * b + h
                        later = not (first and par == 0)
                        if clamped:
                            dve.wait_ge(s_gu_mm, u + 1)
                            if later:
                                dve.wait_ge(s_glu, u - 1)
                            dve.tensor_scalar(gate[:, h, :], bank[2 * h][:], biases[:, 0, bass.ds(b, 1)], LIMIT, ALU.add,
                                              ALU.min).then_inc(s_gate, 1)
                            dve.wait_ge(s_up, u + 1)
                            if later:
                                dve.wait_ge(s_scored, u - 1)
                            dve.tensor_scalar(up_clipped[:, h, :], up[:, h, :], LIMIT + 1.0, 1.0 - LIMIT, ALU.min,
                                              ALU.max).then_inc(s_clip, 1)
                        some_before = not (first and par == 0 and h == 0)
                        before_is_later = not (first and (par == 0 or h == 0))
                        if clamped and some_before:
                            hidden(u - 1, 1 - h, before_is_later)
                        if some_before:
                            hidden_lo(u - 1, 1 - h)
                        if h == 0 and not last:
                            dve.wait_ge(s_gu_hi, b + 2)
                            dve.tensor_tensor(gu_lo[:, 1 - par].rearrange("p g k f -> p (g k f)"), raw_gu[:, 1 - par, :],
                                              gu_hi[:, 1 - par].rearrange("p g k f -> p (g k f)"),
                                              ALU.subtract).then_inc(s_gu_lo, 1)
                        if not clamped:
                            dve.wait_ge(s_gate, u + 1)
                            if later:
                                dve.wait_ge(s_hid, u - 1)
                            dve.tensor_tensor(act_out[:, h, :], gate[:, h, :], bank[2 * h + 1][:],
                                              ALU.mult).then_inc(s_acted, 1)
                        if h == 0:
                            dve.wait_ge(s_d_hi, b + 1)
                            dve.tensor_tensor(d_lo[:, par, :], raw_d[:, par, :], d_hi[:, par, :],
                                              ALU.subtract).then_inc(s_d_lo, 1)

                block_stages(dve, stage)
                if clamped:
                    hidden(2 * BLOCKS - 1, 1, True)
                hidden_lo(2 * BLOCKS - 1, 1)
                dve.wait_ge(s_down, 2 * BLOCKS)
                for o in range(2):
                    dve.tensor_copy(out_t[:, o, HALF:TOKENS], bank[5 + 2 * o][:]).then_inc(s_out_s, 1)
                for j in range(TILES // 2):
                    dve.wait_ge(s_out_t, j + 1)
                    dve.tensor_tensor(x[:, 2 * j:2 * j + 2, :], x[:, 2 * j:2 * j + 2, :],
                                      bank[j][:].rearrange("p (t d) -> p t d", d=DIM), ALU.add).then_inc(s_res, 1)
                dve.wait_ge(s_res, TILES // 2)

            @block.tensor
            def _(pe):
                ln.tensor(pe)
                pe.wait_ge(s_r_lo, 2 if clamped else 1)
                for i in range(TILES):
                    pe.wait_ge(ln.s_lo, 2 * (i // 4 + 1))
                    t = slice(P * i, P * i + P)
                    for k in range(KT):
                        m = three_products(pe, bank[4][:, E * i:E * i + E], xt_hi[:, k, t], xt_lo[:, k, t],
                                           r_hi[:, k, :], r_lo[:, k, :], k == 0, k == KT - 1)
                m.then_inc(s_logits, 1)

                def gate_up(b, par, h, later):
                    u = 2 * b + h
                    pe.wait_ge(s_gu_lo, b + 1)
                    if later:
                        pe.wait_ge(s_gate if clamped else s_acted, u - 1)
                        if clamped:
                            pe.wait_ge(s_up, u - 1)
                    for g in range(2):
                        for k in range(KT):
                            t = slice(HALF * h, HALF * h + HALF)
                            m = three_products(pe, bank[2 * h + g][:], gu_hi[:, par, g, k, :], gu_lo[:, par, g, k, :],
                                               xt_hi[:, k, t], xt_lo[:, k, t], k == 0, k == KT - 1)
                    m.then_inc(s_gu_mm, 1)

                def down(b, par, h, first, last):
                    pe.wait_ge(s_h_lo, 2 * b + h + 1)
                    pe.wait_ge(s_d_lo, b + 1)
                    for o in range(2):
                        m = three_products(pe, bank[4 + 2 * o + h][:], d_hi[:, par, P * o:P * o + P],
                                           d_lo[:, par, P * o:P * o + P], h_hi[:, h, :], h_lo[:, h, :],
                                           first and not clamped, last, skip_group_check=True)
                    m.then_inc(s_down, 1)

                gate_up(0, 0, 0, False)
                gate_up(0, 0, 1, False)
                pe.wait_ge(s_routed, 2)
                for h in range(HALVES):
                    for i in range(4 * h, 4 * h + 4):
                        m = pe.transpose(bank[4 + h][0:E, P * (i % 4):P * (i % 4) + P], weight[:, i, :], ident)
                    m.then_inc(s_score_t, 1)
                pe.wait_ge(s_score_s, HALVES)
                if clamped:
                    for o in range(2):
                        for h in range(HALVES):
                            pe.matmul(bank[4 + 2 * o + h][:], down_bias[:, P * o:P * o + P],
                                      score_t[:, HALF * h:HALF * h + HALF], start=True, stop=False,
                                      skip_group_check=True)

                def turn(b, par, first):
                    for h in range(HALVES):
                        gate_up(b + 1, 1 - par, h, True)
                        down(b, par, h, first, False)

                turn(0, 0, True)
                with pe.Fori(1, BLOCKS // 2, 1) as i:
                    turn(2 * i - 1, 1, False)
                    turn(2 * i, 0, False)
                for h in range(HALVES):
                    down(BLOCKS - 1, 1, h, False, True)
                pe.wait_ge(s_out_s, 4)
                for i in range(TILES):
                    for o in range(2):
                        c = DIM * (i % 2) + P * o
                        m = pe.transpose(bank[i // 2][:, c:c + P], out_t[:, o, P * i:P * i + P], ident)
                    if i % 2:
                        m.then_inc(s_out_t, 1)
        kit.retire_semaphores()


BF16 = mybir.dt.bfloat16
ATT_HEADS, ATT_DIM = 16, 16
PAIRS = ATT_HEADS // 2
ROWS = 64
PEAK_ROW = 3 * ATT_DIM
PEAK_SCALE = 64.0
V_COLS = 2 * ATT_DIM + 1
SCALE_ROOT = ATT_DIM ** -0.25
SPAN = 3 * P
BATCHES = TOKENS // SEQ
QKV = 3 * DIM


def attention(nc, G):
    with ExitStack() as stack:
        kit = Kit(nc, stack, [])
        A = {
            "q": kit.sb("q_stacks", [P, PAIRS, TOKENS], F16),
            "k": kit.sb("k_stacks", [P, PAIRS, TOKENS], F16),
            "v": kit.sb("v_parts_and_ones", [P, TILES, ATT_HEADS, V_COLS], F16),
            "w_o": kit.sb("w_o", [P, KT, DIM]),
            "w_o_hi": kit.sb("w_o_hi", [P, KT, DIM], F16),
            "w_o_lo": kit.sb("w_o_lo", [P, KT, DIM], F16),
            "bo": kit.sb("bo_rows", [P, DIM]),
            "consts": kit.sb("attention_consts", [P, 7, P]),
            "masks": kit.sb("attention_masks", [P, 3, P], BF16),
            "select": kit.sb("attention_selections", [P, 5, P], F16),
        }
        with ExitStack() as inner:
            attention_projections(nc, G, kit.part(inner), A)
        with ExitStack() as inner:
            attention_heads(nc, G, kit.part(inner), A)
        kit.retire_semaphores()


def attention_projections(nc, G, kit, A):
    x, bank, ident = G["x"], G["bank"], G["ident"]
    v, w_o, w_o_hi, w_o_lo, bo = A["v"], A["w_o"], A["w_o_hi"], A["w_o_lo"], A["bo"]
    consts, masks, select = A["consts"], A["masks"], A["select"]
    raw = kit.sb("w_qkv_raw", [P, KT, QKV])
    w_hi = kit.sb("w_qkv_hi", [P, KT, QKV], F16)
    w_lo = kit.sb("w_qkv_lo", [P, KT, QKV], F16)
    xt_hi = kit.sb("attention_xt_hi", [P, KT, TOKENS], F16)
    xt_lo = kit.sb("attention_xt_lo", [P, KT, TOKENS], F16)
    biases = kit.sb("qk_biases", [P, 2, KT])
    root_biases = kit.sb("qk_biases_scaled", [P, 2, KT])
    stack_bias = kit.sb("k_stack_bias", [P, 1])
    bv = kit.sb("bv_rows", [P, DIM])
    v_exact = kit.sb("v_float32", [P, TILES, ATT_HEADS, ATT_DIM])
    exact = kit.sb("qk_float32", [P, 2, HALF])
    qk_hi = kit.sb("qk_hi", [P, 2, KT, TOKENS], F16)
    qk_lo = kit.sb("qk_lo", [P, 2, KT, TOKENS], F16)
    ln = LayerNorm(nc, kit, "attention_ln", x, bank, ident)
    s_w = kit.sem("w_qkv_loaded")
    s_small = kit.sem("attention_small_loaded")
    s_w_hi = kit.sem("w_qkv_hi_done")
    s_w_lo = kit.sem("w_qkv_lo_done")
    s_bias = kit.sem("qk_biases_done")
    s_const = kit.sem("attention_consts16_done")
    s_wo = kit.sem("w_o_split")
    s_mm = kit.sem("qkv_projected")
    s_exact = kit.sem("qk_float32_done")
    s_hi = kit.sem("qk_hi_done")
    s_lo = kit.sem("qk_lo_done")
    s_v = kit.sem("v_done")
    s_ones = kit.sem("v_ones_done")
    s_v_hi = kit.sem("v_hi_done")
    s_v_lo = kit.sem("v_lo_done")
    s_stacked = kit.sem("stack_selected")
    s_q = kit.sem("q_stack_saved")
    s_k = kit.sem("k_stack_saved")
    s_bo = kit.sem("bo_added")
    UNITS = 2 * KT * HALVES
    STACKS = 2 * PAIRS * HALVES

    def unit(u):
        return u % 2, (u // 2) % KT, u // (2 * KT)

    def stack_unit(s):
        return s % 2, (s // 2) % PAIRS, s // (2 * PAIRS)

    def cols(h):
        return slice(HALF * h, HALF * h + HALF)

    with nc.Block() as block:
        @block.sync
        def _(sp):
            sp.dma_start(raw[:], G["w_qkv"].rearrange("(k p) n -> p k n", p=P)).then_inc(s_w, 16)
            sp.dma_start(biases[:], G["qk_bias"]).then_inc(s_small, 16)
            sp.dma_start(stack_bias[:], G["k_stack_bias"]).then_inc(s_small, 16)
            sp.dma_start(bv[:], G["bv"].partition_broadcast(P)).then_inc(s_small, 16)
            sp.dma_start(bo[:], G["bo"].partition_broadcast(P)).then_inc(s_small, 16)
            sp.dma_start(consts[:], G["attention_consts"]).then_inc(s_small, 16)
            sp.dma_start(w_o[:], G["w_o"].rearrange("(k p) n -> p k n", p=P)).then_inc(s_small, 16)

        @block.gpsimd
        def _(pool):
            pool.memset(v[:], 1.0).then_inc(s_ones, 1)
            ln.pool(pool)
            pool.wait_ge(s_small, 96)
            pool.tensor_copy(select[:, 0, :], consts[:, 0, :]).then_inc(s_const, 1)
            pool.tensor_copy(select[:, 1:5, :], consts[:, 3:7, :]).then_inc(s_const, 1)
            pool.tensor_copy(masks[:], consts[:, 0:3, :]).then_inc(s_const, 1)
            pool.tensor_copy(w_o_hi[:], w_o[:]).then_inc(s_wo, 1)
            pool.wait_ge(s_wo, 1)
            pool.tensor_tensor(w_o_lo[:], w_o[:], w_o_hi[:], ALU.subtract).then_inc(s_wo, 1)
            pool.wait_ge(ln.s_xn, TILES)
            pool.tensor_tensor(x[:], x[:], bc(bo[:], 1, TILES), ALU.add).then_inc(s_bo, 1)
            pool.wait_ge(s_ones, 1)
            for i in range(TILES):
                pool.wait_ge(s_v, i + 1)
                pool.tensor_copy(v[:, i, :, 0:ATT_DIM], v_exact[:, i]).then_inc(s_v_hi, 1)
                pool.wait_ge(s_v_hi, i + 1)
                pool.tensor_tensor(v[:, i, :, ATT_DIM:2 * ATT_DIM], v_exact[:, i], v[:, i, :, 0:ATT_DIM],
                                   ALU.subtract).then_inc(s_v_lo, 1)
            pool.wait_ge(s_v_lo, TILES)
            pool.wait_ge(s_bo, 1)
            pool.wait_ge(s_wo, 2)
            pool.wait_ge(s_const, 3)

        @block.scalar
        def _(act):
            act.wait_ge(s_w, 16)
            for k in range(KT):
                act.activation(w_hi[:, k, :], raw[:, k, :], ACT.Copy).then_inc(s_w_hi, 1)
            act.wait_ge(s_small, 96)
            act.activation(root_biases[:], biases[:], ACT.Copy, scale=SCALE_ROOT).then_inc(s_bias, 1)
            ln.scalar_hi(act, xt_hi)
            act.wait_ge(s_bias, 1)
            for u in range(UNITS):
                which, g, h = unit(u)
                act.wait_ge(s_mm, u + 1)
                if u >= 2:
                    act.wait_ge(s_lo, u - 1)
                bias = root_biases[:, which, g:g + 1]
                act.activation(exact[:, u % 2, :], bank[4 + u % 4][:], ACT.Identity, bias=bias,
                               scale=SCALE_ROOT).then_inc(s_exact, 1)
                act.activation(qk_hi[:, which, g, cols(h)], bank[4 + u % 4][:], ACT.Identity, bias=bias,
                               scale=SCALE_ROOT).then_inc(s_hi, 1)
            for s in range(0, STACKS, 2):
                _, pair, h = stack_unit(s)
                act.wait_ge(s_stacked, s + 1)
                act.activation(A["q"][:, pair, cols(h)], bank[4 + s % 4][:], ACT.Copy).then_inc(s_q, 1)

        @block.vector
        def _(dve):
            ln.vector_stats(dve)
            ln.vector_normalize(dve)
            for k in range(KT):
                dve.wait_ge(s_w_hi, k + 1)
                dve.tensor_tensor(w_lo[:, k, :], raw[:, k, :], w_hi[:, k, :], ALU.subtract).then_inc(s_w_lo, 1)
            ln.vector_lo(dve, xt_hi, xt_lo)
            for u in range(UNITS):
                which, g, h = unit(u)
                dve.wait_ge(s_exact, u + 1)
                dve.wait_ge(s_hi, u + 1)
                dve.tensor_tensor(qk_lo[:, which, g, cols(h)], exact[:, u % 2, :], qk_hi[:, which, g, cols(h)],
                                  ALU.subtract).then_inc(s_lo, 1)
            dve.wait_ge(s_small, 96)
            for i in range(TILES):
                dve.wait_ge(s_mm, UNITS + i + 1)
                dve.tensor_tensor(v_exact[:, i],
                                  bank[4 + i % 4][:, 0:DIM].rearrange("p (h d) -> p h d", d=ATT_DIM),
                                  bv[:].rearrange("p (h d) -> p h d", d=ATT_DIM), ALU.add).then_inc(s_v, 1)
            for s in range(1, STACKS, 2):
                _, pair, h = stack_unit(s)
                dve.wait_ge(s_stacked, s + 1)
                dve.tensor_scalar(A["k"][:, pair, cols(h)], bank[4 + s % 4][:], stack_bias[:], 1.0, ALU.add,
                                  ALU.mult).then_inc(s_k, 1)

        @block.tensor
        def _(pe):
            ln.tensor(pe)
            pe.wait_ge(s_w_lo, KT)
            for u in range(UNITS):
                which, g, h = unit(u)
                pe.wait_ge(ln.s_lo, 2 * (h + 1))
                if u >= 4:
                    pe.wait_ge(s_hi, u - 3)
                c = slice(DIM * which + P * g, DIM * which + P * g + P)
                for k in range(KT):
                    m = three_products(pe, bank[4 + u % 4][:], w_hi[:, k, c], w_lo[:, k, c],
                                       xt_hi[:, k, cols(h)], xt_lo[:, k, cols(h)], k == 0, k == KT - 1)
                m.then_inc(s_mm, 1)
            for i in range(TILES):
                if i < 4:
                    pe.wait_ge(s_hi, UNITS - 3 + i)
                else:
                    pe.wait_ge(s_v, i - 3)
                t = slice(P * i, P * i + P)
                c = slice(2 * DIM, QKV)
                for k in range(KT):
                    m = three_products(pe, bank[4 + i % 4][:, 0:DIM], xt_hi[:, k, t], xt_lo[:, k, t], w_hi[:, k, c],
                                       w_lo[:, k, c], k == 0, k == KT - 1)
                m.then_inc(s_mm, 1)
            pe.wait_ge(s_const, 3)
            pe.wait_ge(s_lo, UNITS)
            for s in range(STACKS):
                which, pair, h = stack_unit(s)
                if s < 4:
                    pe.wait_ge(s_v, TILES - 3 + s)
                else:
                    pe.wait_ge((s_q, s_k)[which], s // 2 - 1)
                g, r = pair // 4, slice(32 * (pair % 4), 32 * (pair % 4) + 32)
                out = bank[4 + s % 4][:]
                pe.matmul(out, select[r, 1 + 2 * which, :], qk_hi[r, which, g, cols(h)], start=True, stop=False)
                pe.matmul(out, select[r, 2 + 2 * which, :], qk_lo[r, which, g, cols(h)], start=False,
                          stop=True).then_inc(s_stacked, 1)


def attention_heads(nc, G, kit, A):
    x, bank, banks, ident = G["x"], G["bank"], G["banks"], G["ident"]
    q, k, v, w_o_hi, w_o_lo = A["q"], A["k"], A["v"], A["w_o_hi"], A["w_o_lo"]
    UNITS = BATCHES * PAIRS
    SET = 2
    SETS = UNITS // SET
    peaks = kit.sb("minus_peaks", [P, 2, 2, 2])
    peak_rows = kit.sb("peak_rows", [P, 2, 2, 2, ROWS], F16)
    probs = kit.sb("probs", [P, 2, 2, SPAN])
    probs_hi = kit.sb("probs_hi", [P, 2, 2, SPAN], F16)
    probs_lo = kit.sb("probs_lo", [P, 2, 2, SPAN], F16)
    sum_parts = kit.sb("attended_parts_sum", [P, 2, 2, 2 * SET, ATT_DIM])
    inverse = kit.sb("inverse_sums", [P, 2, 2, 2 * SET, 1])
    attended = kit.sb("attended", [P, TILES, DIM])
    at_hi = kit.sb("attended_turned_hi", [P, KT, TOKENS], F16)
    at_lo = kit.sb("attended_turned_lo", [P, KT, TOKENS], F16)
    s_zero = kit.sem("peak_rows_cleared")
    s_s = kit.sem("scores_done")
    s_max = kit.sem("maximum_done")
    s_peak = kit.sem("peak_row_done")
    s_turn = kit.sem("peaks_turned")
    s_aug = kit.sem("q_augmented")
    s_st = kit.sem("turned_scores_done")
    s_hi = kit.sem("probs_hi_done")
    s_lo = kit.sem("probs_lo_done")
    s_pv = kit.sem("attended_done")
    s_part = kit.sem("attended_part_taken")
    s_norm = kit.sem("attended_normed")
    s_at = kit.sem("attended_turned")
    s_at_hi = kit.sem("attended_hi_done")
    s_at_lo = kit.sem("attended_lo_done")
    s_out = kit.sem("attention_projected")
    s_res = kit.sem("attention_residual_added")
    ident_b, mask, mask_t = A["masks"][:, 0, :], A["masks"][:, 1, :], A["masks"][:, 2, :]
    ident16 = A["select"][:, 0, :]

    def head_rows(jj):
        return slice(ROWS * jj, ROWS * jj + ROWS)

    def add_mask(pe, out_bank, m):
        out = banks[:, out_bank, 0:SPAN + P].rearrange("p (c n) -> p c n", n=P)[:, 0:3:2, :]
        return pe.matmul(out, ident_b, bc(m, 1, 2), start=False, stop=True, skip_group_check=True)

    with nc.Block() as block:
        @block.tensor
        def _(pe):
            def scores(n):
                b, pair = n // PAIRS, n % PAIRS
                if n >= 2:
                    pe.wait_ge(s_aug, n - 1)
                for jj in range(2):
                    r, bk = head_rows(jj), 2 * (n % 2) + jj
                    for qt in range(2):
                        queries = q[r, pair, SEQ * b + P * qt:SEQ * b + P * qt + P]
                        keys = k[r, pair, SEQ * b:SEQ * b + P * (qt + 1)]
                        pe.matmul(banks[:, bk, P * qt:P * qt + P * (qt + 1)], queries, keys, start=(qt == 0),
                                  stop=False, skip_group_check=True)
                    m = add_mask(pe, bk, mask)
                m.then_inc(s_s, 1)

            def turn_peaks(n):
                pe.wait_ge(s_peak, n + 1)
                for qt in range(2):
                    m = pe.matmul(banks[:, 2 * (n % 2) + qt, SPAN:SPAN + P],
                                  peak_rows[:, n % 2, qt].rearrange("p j e -> p (j e)"), ident16,
                                  start=True, stop=True, skip_group_check=True)
                m.then_inc(s_turn, 1)

            def turned_scores(n):
                b, pair = n // PAIRS, n % PAIRS
                pe.wait_ge(s_aug, n + 1)
                for jj in range(2):
                    if n >= 1:
                        pe.wait_ge(s_hi, 2 * n - 1 + jj)
                    r = head_rows(jj)
                    for kb in range(2):
                        keys = k[r, pair, SEQ * b + P * kb:SEQ * b + P * kb + P]
                        queries = q[r, pair, SEQ * b + P * kb:SEQ * b + SEQ]
                        pe.matmul(banks[:, 4 + jj, SEQ * kb:SEQ + P * kb], keys, queries, start=(kb == 0),
                                  stop=False, skip_group_check=True)
                    add_mask(pe, 4 + jj, mask_t).then_inc(s_st, 1)

            def attend(n):
                b, pair = n // PAIRS, n % PAIRS
                s, w = n // SET, n % SET
                pe.wait_ge(s_lo, n + 1)
                if w == 0 and s >= 2:
                    pe.wait_ge(s_part, 3 * (s - 1))
                for jj in range(2):
                    for qt in range(2):
                        c = V_COLS * (2 * SET * qt + 2 * w + jj)
                        for kb in range(qt + 1):
                            block_cols = slice(P * (qt + kb), P * (qt + kb) + P)
                            v_head = v[:, 2 * b + kb, 2 * pair + jj, :]
                            out = bank[6 + s % 2][:, c:c + V_COLS]
                            pe.matmul(out, probs_hi[:, n % 2, jj, block_cols], v_head, start=(kb == 0), stop=False)
                            m = pe.matmul(out, probs_lo[:, n % 2, jj, block_cols], v_head, start=False,
                                          stop=(kb == qt))
                m.then_inc(s_pv, 1)

            scores(0)
            for n in range(UNITS + 3):
                if n + 1 < UNITS:
                    scores(n + 1)
                if n < UNITS:
                    turn_peaks(n)
                if 1 <= n <= UNITS:
                    turned_scores(n - 1)
                if n >= 3:
                    attend(n - 3)

        @block.gpsimd
        def _(pool):
            pool.memset(peak_rows[:], 0.0).then_inc(s_zero, 1)
            for n in range(UNITS):
                pool.wait_ge(s_hi, 2 * (n + 1))
                if n >= 2:
                    pool.wait_ge(s_pv, n - 1)
                pool.tensor_tensor(probs_lo[:, n % 2], probs[:, n % 2], probs_hi[:, n % 2],
                                   ALU.subtract).then_inc(s_lo, 1)
            pool.wait_ge(s_lo, UNITS)

        @block.scalar
        def _(act):
            for n in range(UNITS):
                for jj in range(2):
                    act.wait_ge(s_st, 2 * n + jj + 1)
                    if n >= 2:
                        act.wait_ge(s_lo, n - 1)
                    act.activation(probs[:, n % 2, jj], banks[:, 4 + jj, 0:SPAN], ACT.Exp)
                    if n >= 2:
                        act.wait_ge(s_pv, n - 1)
                    act.activation(probs_hi[:, n % 2, jj], banks[:, 4 + jj, 0:SPAN], ACT.Exp).then_inc(s_hi, 1)

        @block.vector
        def _(dve):
            dve.wait_ge(s_zero, 1)

            def peak(n):
                dve.wait_ge(s_s, n + 1)
                if n >= 2:
                    dve.wait_ge(s_peak, n - 1)
                for qt in range(2):
                    dve.tensor_reduce(peaks[:, n % 2, qt, :],
                                      banks[:, 2 * (n % 2):2 * (n % 2) + 2, P * qt:P * (2 * qt + 1)],
                                      AX.X, ALU.max, negate=True).then_inc(s_max, 1)
                dve.wait_ge(s_max, 2 * (n + 1))
                if n >= 2:
                    dve.wait_ge(s_turn, n - 1)
                dve.tensor_scalar(peak_rows[:, n % 2, :, :, PEAK_ROW:PEAK_ROW + 1].squeeze(3), peaks[:, n % 2],
                                  1.0 / PEAK_SCALE, 0.0, ALU.mult, ALU.add).then_inc(s_peak, 1)

            def augment(n):
                b, pair = n // PAIRS, n % PAIRS
                dve.wait_ge(s_turn, n + 1)
                rows = q[:, pair, SEQ * b:SEQ * b + SEQ].rearrange("p (t n) -> p t n", n=P)
                dve.tensor_tensor(rows, rows, banks[:, 2 * (n % 2):2 * (n % 2) + 2, SPAN:SPAN + P],
                                  ALU.add).then_inc(s_aug, 1)

            def normalize(s):
                b, pair = s * SET // PAIRS, s * SET % PAIRS
                dve.wait_ge(s_pv, SET * (s + 1))
                out = bank[6 + s % 2][:, 0:4 * SET * V_COLS].rearrange("p (t h d) -> p t h d", t=2, d=V_COLS)
                dve.reciprocal(inverse[:, s % 2], out[:, :, :, 2 * ATT_DIM:V_COLS]).then_inc(s_part, 1)
                dve.tensor_copy(sum_parts[:, s % 2], out[:, :, :, 0:ATT_DIM]).then_inc(s_part, 1)
                dve.wait_ge(s_part, 3 * s + 2)
                dve.tensor_tensor(sum_parts[:, s % 2], sum_parts[:, s % 2], out[:, :, :, ATT_DIM:2 * ATT_DIM],
                                  ALU.add).then_inc(s_part, 1)
                dve.wait_ge(s_part, 3 * s + 3)
                c = 2 * ATT_DIM * pair
                dst = attended[:, 2 * b:2 * b + 2, c:c + 2 * ATT_DIM * SET].rearrange("p t (h d) -> p t h d", d=ATT_DIM)
                dve.tensor_tensor(dst, sum_parts[:, s % 2],
                                  inverse[:, s % 2].broadcast_to([P, 2, 2 * SET, ATT_DIM]),
                                  ALU.mult).then_inc(s_norm, 1)

            for n in range(UNITS):
                peak(n)
                augment(n)
                if n >= 5 and n % 2:
                    normalize((n - 5) // 2)
            normalize(SETS - 2)
            normalize(SETS - 1)
            dve.wait_ge(s_norm, SETS)

    with nc.Block() as block:
        def turned_bank(g):
            return bank[g % 4]

        @block.tensor
        def _(pe):
            for g in range(HALVES * KT):
                for i in range(4):
                    m = pe.transpose(turned_bank(g)[:, P * i:P * i + P],
                                     attended[:, 4 * (g // KT) + i, P * (g % KT):P * (g % KT) + P], ident)
                m.then_inc(s_at, 1)
            for i in range(TILES):
                pe.wait_ge(s_at_lo, KT * (i // 4 + 1))
                if i >= 4:
                    pe.wait_ge(s_res, i - 3)
                t = slice(P * i, P * i + P)
                for kt in range(KT):
                    m = three_products(pe, bank[4 + i % 4][:, 0:DIM], at_hi[:, kt, t], at_lo[:, kt, t],
                                       w_o_hi[:, kt, :], w_o_lo[:, kt, :], kt == 0, kt == KT - 1)
                m.then_inc(s_out, 1)

        @block.scalar
        def _(act):
            for g in range(HALVES * KT):
                act.wait_ge(s_at, g + 1)
                act.activation(at_hi[:, g % KT, HALF * (g // KT):HALF * (g // KT) + HALF], turned_bank(g)[:],
                               ACT.Copy).then_inc(s_at_hi, 1)

        @block.vector
        def _(dve):
            for g in range(HALVES * KT):
                t = slice(HALF * (g // KT), HALF * (g // KT) + HALF)
                dve.wait_ge(s_at_hi, g + 1)
                dve.tensor_tensor(at_lo[:, g % KT, t], turned_bank(g)[:], at_hi[:, g % KT, t],
                                  ALU.subtract).then_inc(s_at_lo, 1)
            for i in range(TILES):
                dve.wait_ge(s_out, i + 1)
                dve.tensor_tensor(x[:, i, :], x[:, i, :], bank[4 + i % 4][:, 0:DIM], ALU.add).then_inc(s_res, 1)
            dve.wait_ge(s_res, TILES)


def run_stages(nc, G):
    mamba(nc, G)
    moe(nc, G, 0)
    attention(nc, G)
    moe(nc, G, 1)


def more_layout(i, a):
    moe_layout(i, a)
    attention_layout(i, a)


def store(nc, G):
    with ExitStack() as stack:
        s_stored = Kit(nc, stack, []).sem("output_stored")
        with nc.Block() as block:
            @block.sync
            def _(sp):
                sp.dma_start(G["out"].rearrange("(t p) d -> p t d", p=P), G["x"][:]).then_inc(s_stored, 16)
                sp.wait_ge(s_stored, 16)


def build(nc, inputs, out):
    with ExitStack() as stack:
        kit = Kit(nc, stack, [])
        G = dict(inputs)
        G["x_in"] = inputs["x"]
        G["ident_in"] = inputs["ident"]
        G["out"] = out
        G["x"] = kit.sb("residual", [P, TILES, DIM])
        G["ident"] = kit.sb("identity", [P, P])[:]
        G["banks"] = stack.enter_context(nc.psum_tensor("banks", [P, 8, 512], F32))
        G["bank"] = [G["banks"][:, b, :] for b in range(8)]
        G["s_ident"] = kit.sem("identity_loaded")
        run_stages(nc, G)
        store(nc, G)


def level_masks():
    import numpy as np
    t = np.arange(P)
    cum = np.zeros((2, LEVELS + 1, P, P), np.float32)
    pair = np.zeros((LEVELS, P, P), np.float32)
    for k in range(LEVELS):
        half = 1 << k
        second = (t // half) % 2 == 1
        block = t // (2 * half)
        ref = block * 2 * half + half - 1
        r = t[:, None]
        cum[0, k] = (~second)[None] & (r > t[None]) & (r <= ref[None])
        cum[1, k] = second[None] & (r > ref[None]) & (r <= t[None])
        pair[k] = (~second)[:, None] & second[None] & (block[:, None] == block[None])
    cum[0, LEVELS] = t[:, None] > t[None]
    cum[1, LEVELS] = t[:, None] <= t[None]
    return cum.reshape(-1, P, P).transpose(1, 0, 2), pair.transpose(1, 0, 2)


def layout(i):
    import numpy as np
    cum, pair = level_masks()
    a = {
        "x": i["L0_attn_x"].reshape(TOKENS, DIM),
        "ident": np.eye(P, dtype=np.float32),
        "w_in": i["L0_attn_in_proj_w"].T,
        "conv_w": i["L0_attn_conv_w"],
        "dt_bias": i["L0_attn_dt_bias"],
        "A_log": i["L0_attn_A_log"],
        "D": i["L0_attn_D"],
        "norm_w": i["L0_attn_norm_w"].reshape(-1, P).T,
        "w_out": i["L0_attn_out_proj_w"].T,
        "cum_masks": cum,
        "pair_masks": pair,
    }
    more_layout(i, a)
    return a


def kernel(**inputs):
    import numpy as np
    import concourse.bacc as bacc
    from concourse.bass_utils import run_bass_kernel_spmd

    nc = bacc.Bacc("TRN2", target_bir_lowering=False, num_devices=1)
    arrays = {k + "_dram": np.ascontiguousarray(v) for k, v in layout({k: np.asarray(v) for k, v in inputs.items()}).items()}
    aps = {k[:-5]: nc.dram_tensor(k, v.shape, mybir.dt.from_np(v.dtype), kind="ExternalInput").ap()
           for k, v in arrays.items()}
    out = nc.dram_tensor("out_dram", (TOKENS, DIM), F32, kind="ExternalOutput").ap()
    build(nc, aps, out)
    result = run_bass_kernel_spmd(nc, [arrays], core_ids=[0])
    return result.results[0]["out_dram"].reshape(4, SEQ, DIM)


def moe_blocks(gate, up, down):
    import numpy as np
    n = -(-gate.shape[0] // (2 * P)) * 2 * P
    pad = lambda w: np.concatenate([w, np.zeros((n - w.shape[0], DIM), w.dtype)])
    gu = np.stack([pad(gate), pad(up)]).reshape(2, n // P, P, KT, P)
    return gu.transpose(1, 4, 0, 3, 2).reshape(n, 2 * KT * P), pad(down)


def moe_layout(i, a):
    import numpy as np
    cat = np.concatenate
    a["moe0_gate_up"], a["moe0_down"] = moe_blocks(
        cat([i["L0_ffn_expert_gate"].reshape(-1, DIM), i["L0_ffn_shared_gate"]]),
        cat([i["L0_ffn_expert_up"].reshape(-1, DIM), i["L0_ffn_shared_up"]]),
        cat([i["L0_ffn_expert_down"].transpose(0, 2, 1).reshape(-1, DIM), i["L0_ffn_shared_down"].T]))
    a["moe0_router"] = i["L0_ffn_gate_w"].T
    a["moe0_lower_expert"] = np.tril(np.ones((L0_EXPERTS, L0_EXPERTS), np.float32), -1)
    w = i["L1_ffn_gate_up_proj"]
    a["moe1_gate_up"], a["moe1_down"] = moe_blocks(
        w[:, :, 0::2].transpose(0, 2, 1).reshape(-1, DIM), w[:, :, 1::2].transpose(0, 2, 1).reshape(-1, DIM),
        i["L1_ffn_down_proj"].reshape(-1, DIM))
    a["moe1_router"] = i["L1_ffn_router_weight"].T
    a["moe1_lower_expert"] = np.tril(np.ones((L1_EXPERTS, L1_EXPERTS), np.float32), -1)
    a["moe1_router_bias"] = i["L1_ffn_router_bias"]
    a["moe1_biases"] = i["L1_ffn_gate_up_proj_bias"].reshape(-1, P, 2).transpose(1, 2, 0)
    a["moe1_down_bias"] = i["L1_ffn_down_proj_bias"]


def attention_layout(i, a):
    import numpy as np

    a["w_qkv"] = np.concatenate([i["L1_attn_Wq"], i["L1_attn_Wk"], i["L1_attn_Wv"]]).T
    a["qk_bias"] = np.stack([i["L1_attn_bq"].reshape(KT, P), i["L1_attn_bk"].reshape(KT, P)]).transpose(2, 0, 1)
    a["bv"] = i["L1_attn_bv"]
    a["bo"] = i["L1_attn_bo"]
    a["w_o"] = i["L1_attn_Wo"].T
    t = np.arange(P)
    above = np.where(t[None] > t[:, None], -1e30, 0.0)
    same_head = (t[:, None] // ATT_DIM) % 2 == t[None] // ROWS
    same_dim = t[:, None] % ATT_DIM == t[None] % ATT_DIM
    part = (t[None] % ROWS) // ATT_DIM
    hits = same_head & same_dim
    q_hi, q_lo = hits & (part < 2), hits & (part == 2)
    k_hi, k_lo = hits & (part % 2 == 0) & (part < 3), hits & (part == 1)
    a["attention_consts"] = np.stack([np.eye(P), above, above.T, q_hi, q_lo, k_hi, k_lo]).transpose(1, 0, 2).astype(
        np.float32)
    a["k_stack_bias"] = np.where(t % ROWS == PEAK_ROW, PEAK_SCALE, 0.0).astype(np.float32)[:, None]
```

```python
from contextlib import ExitStack

import concourse.bass as bass
from concourse import mybir

F32 = mybir.dt.float32
F16 = mybir.dt.float16
ALU = mybir.AluOpType
ACT = mybir.ActivationFunctionType
AX = mybir.AxisListType

P = 128
TOKENS = 1024
DIM = 256
TILES = TOKENS // P
KT = DIM // P
HALF = 512
HALVES = TOKENS // HALF
EPS = 1e-5

HID = 512
HEADS = 64
HEAD_DIM = HID // HEADS
CONV_BLOCKS = 6
XB = HID // P
TAPS = 4
SEQ = 256
LEVELS = 7
SIDES = LEVELS + 1
Z0, X0, DT0 = 0, HID, HID + 768


class Kit:

    def __init__(self, nc, stack, taken):
        self.nc, self.stack, self.taken = nc, stack, taken

    def part(self, stack):
        return Kit(self.nc, stack, self.taken)

    def sb(self, name, shape, dtype=F32):
        return self.stack.enter_context(self.nc.sbuf_tensor(name, shape, dtype))

    def sem(self, name):
        self.taken.append(self.nc.alloc_semaphore(name))
        return self.taken[-1]

    def retire_semaphores(self):
        def clear(eng, part):
            for sem in self.taken[part::4]:
                eng.sem_clear(sem)

        with self.nc.Block() as block:
            @block.sync
            def _(sp):
                clear(sp, 0)

            @block.scalar
            def _(act):
                clear(act, 1)

            @block.vector
            def _(dve):
                clear(dve, 2)

            @block.tensor
            def _(pe):
                clear(pe, 3)
        for sem in self.taken:
            self.nc.release_semaphore(sem)
        self.taken.clear()


def bc(ap, axis, n):
    ap = ap.unsqueeze(axis)
    shape = list(ap.shape)
    shape[axis] = n
    return ap.broadcast_to(shape)


class Norm:

    def __init__(self, kit, name, G):
        self.x = G["x"]
        self.stats, self.mv, self.var, self.half_power, self.rstd, self.xn = G["norm"]
        self.s_stats = kit.sem(name + "_stats_done")
        self.s_mv = kit.sem(name + "_mean_var_done")
        self.s_var = kit.sem(name + "_var_eps_done")
        self.s_rstd = kit.sem(name + "_rstd_done")
        self.s_xn = kit.sem(name + "_xn_done")
        self.vars_done = 0

    def vector_stats(self, dve, i):
        dve.bn_stats(self.stats[:, i, :], self.x[:, i, :]).then_inc(self.s_stats, 1)

    def vector_mean_var(self, dve, i):
        dve.wait_ge(self.s_stats, i + 1)
        dve.bn_aggr(self.mv[:, i, :], self.stats[:, i, :]).then_inc(self.s_mv, 1)

    def pool_rstd(self, pool, i, n):
        pool.wait_ge(self.s_mv, i + n)
        pool.tensor_scalar(self.var[:, i:i + n], self.mv[:, i:i + n, 1], EPS, 1.0, ALU.add,
                           ALU.mult).then_inc(self.s_var, 1)
        self.vars_done += 1
        pool.wait_ge(self.s_var, self.vars_done)
        pool.tensor_tensor(self.rstd[:, i:i + n], self.var[:, i:i + n], self.half_power[:, i:i + n],
                           ALU.pow).then_inc(self.s_rstd, 1)

    def vector_normalize(self, dve, i, rstds):
        dve.wait_ge(self.s_rstd, rstds)
        dve.tensor_scalar(self.xn[:, i, :], self.x[:, i, :], self.mv[:, i, 0:1], self.rstd[:, i:i + 1],
                          ALU.subtract, ALU.mult).then_inc(self.s_xn, 1)


class TurnedNorm:

    def __init__(self, kit, name, G, norm=None):
        self.bank, self.ident, self.xn, self.norm = G["bank"], G["ident"], G["norm"][-1], norm
        self.s_turned = kit.sem(name + "_turned")
        self.s_hi = kit.sem(name + "_hi_done")
        self.s_lo = kit.sem(name + "_lo_done")

    def tensor(self, pe):
        for h in range(HALVES):
            for i in range(4 * h, 4 * h + 4):
                if self.norm is not None:
                    pe.wait_ge(self.norm.s_xn, i + 1)
                for k in range(KT):
                    m = pe.transpose(self.bank[2 * h + k][:, P * (i % 4):P * (i % 4) + P],
                                     self.xn[:, i, P * k:P * k + P], self.ident)
            m.then_inc(self.s_turned, 1)

    def scalar_hi(self, act, hi, banks=range(4)):
        for b in banks:
            act.wait_ge(self.s_turned, b // 2 + 1)
            act.activation(hi[:, b % 2, HALF * (b // 2):HALF * (b // 2) + HALF], self.bank[b][:],
                           ACT.Copy).then_inc(self.s_hi, 1)

    def vector_lo(self, dve, hi, lo, banks=range(4)):
        for b in banks:
            dve.wait_ge(self.s_hi, b + 1)
            sl = slice(HALF * (b // 2), HALF * (b // 2) + HALF)
            dve.tensor_tensor(lo[:, b % 2, sl], self.bank[b][:], hi[:, b % 2, sl],
                              ALU.subtract).then_inc(self.s_lo, 1)


def three_products(pe, out, w_hi, w_lo, x_hi, x_lo, start, stop, **kw):
    pe.matmul(out, w_hi, x_hi, start=start, stop=False, **kw)
    pe.matmul(out, w_hi, x_lo, start=False, stop=False, **kw)
    return pe.matmul(out, w_lo, x_hi, start=False, stop=stop, **kw)


def mamba(nc, G):
    x, bank, ident = G["x"], G["bank"], G["ident"]
    with ExitStack() as stack:
        kit = Kit(nc, stack, G["semaphores"])
        xbc = kit.sb("xbc", [P, CONV_BLOCKS, TOKENS])
        zs = kit.sb("silu_z", [P, TILES, HID])
        dt = kit.sb("dt", [P, TILES, HEADS])
        fs = kit.sb("source_factors", [P, SIDES, TILES, HEADS])
        fl = kit.sb("target_factors", [P, SIDES, TILES, HEADS])
        d_skip = kit.sb("D_rows", [P, HEADS])
        norm_w = kit.sb("norm_w", [P, XB])
        w_out = kit.sb("w_out", [P, XB, DIM])
        pair_masks = kit.sb("pair_masks", [P, LEVELS, P])
        s_ssd_consts = kit.sem("ssd_consts_loaded")
        with ExitStack() as inner:
            mamba_projections(nc, G, kit.part(inner), x, bank, ident, xbc, zs, dt, fs, fl, d_skip, norm_w, w_out,
                              pair_masks, s_ssd_consts)
        with ExitStack() as inner:
            mamba_scan(nc, G, kit.part(inner), x, bank, ident, xbc, zs, dt, fs, fl, d_skip, norm_w, w_out,
                       pair_masks, s_ssd_consts)


def mamba_projections(nc, G, kit, x, bank, ident, xbc, zs, dt, fs, fl, d_skip, norm_w, w_out, pair_masks,
                      s_ssd_consts):
    D_IN = 2 * HID + 256 + HEADS
    w_raw = kit.sb("w_in_raw", [P, KT, D_IN])
    w_hi = kit.sb("w_in_hi", [P, KT, D_IN], F16)
    w_lo = kit.sb("w_in_lo", [P, KT, D_IN], F16)
    xt_hi = kit.sb("xt_hi", [P, KT, TOKENS], F16)
    xt_lo = kit.sb("xt_lo", [P, KT, TOKENS], F16)
    conv_w = kit.sb("conv_w", [P, CONV_BLOCKS, TAPS])
    dt_bias = kit.sb("dt_bias_rows", [P, HEADS])
    a_log = kit.sb("A_log_rows", [P, HEADS])
    a_exp = kit.sb("A_exp_rows", [P, HEADS])
    d_a = kit.sb("dt_times_A", [P, TILES, HEADS])
    cum_masks = kit.sb("cum_masks", [P, 2 * SIDES, P])
    dt_v = kit.sb("dt_shifted", [P, TILES, HEADS])
    dt_e = kit.sb("dt_exp", [P, TILES, HEADS])
    dt_l = kit.sb("dt_log", [P, TILES, HEADS])
    norm = Norm(kit, "mamba_norm", G)
    ln = TurnedNorm(kit, "mamba_norm", G, norm)
    s_half = kit.sem("minus_half_done")
    s_x = [kit.sem(f"x_tiles{i}_loaded") for i in range(TILES // 2)]
    s_w = [kit.sem(f"w_in{k}_loaded") for k in range(KT)]
    s_small = kit.sem("small_loaded")
    s_w_hi = kit.sem("w_in_hi_done")
    s_w_lo = [kit.sem(f"w_in_lo{k}_done") for k in range(KT)]
    s_mm = kit.sem("projected")
    s_z_mm = kit.sem("z_projected")
    s_dt_mm = kit.sem("dt_projected")
    s_tap0 = kit.sem("first_tap_done")
    s_taps = kit.sem("tap_done")
    s_silu = kit.sem("silu_x_done")
    s_z = kit.sem("silu_z_done")
    s_dt = kit.sem("dt_step")
    s_cum_masks = kit.sem("cum_masks_loaded")
    s_cum = kit.sem("cum_done")
    s_fac = kit.sem("factor_exp_done")
    s_fs = kit.sem("source_factor_done")
    UNITS = CONV_BLOCKS * HALVES
    SMALL = 5

    def mm_bank(u):
        return bank[4 + u % 3]

    def z_bank(i):
        return bank[1 + i % 3]

    with nc.Block() as block:
        @block.sync
        def _(sp):
            for j in range(TILES // 2):
                sp.dma_start(x[:, 2 * j:2 * j + 2, :],
                             G["x_in"][2 * P * j:2 * P * j + 2 * P, :].rearrange("(t p) d -> p t d", p=P)
                             ).then_inc(s_x[j], 16)
                if j == 0:
                    sp.dma_start(ident, G["ident_in"]).then_inc(G["s_ident"], 16)
            for k in range(KT):
                sp.dma_start(w_raw[:, k, :], G["w_in"][P * k:P * k + P, :]).then_inc(s_w[k], 16)
            sp.dma_start(conv_w[:], G["conv_w"].rearrange("(j p) t -> p j t", p=P)).then_inc(s_small, 16)
            sp.dma_start(dt_bias[:], G["dt_bias"].partition_broadcast(P)).then_inc(s_small, 16)
            sp.dma_start(a_log[:], G["A_log"].partition_broadcast(P)).then_inc(s_small, 16)
            sp.dma_start(d_skip[:], G["D"].partition_broadcast(P)).then_inc(s_small, 16)
            sp.dma_start(norm_w[:], G["norm_w"]).then_inc(s_small, 16)
            sp.dma_start(cum_masks[:], G["cum_masks"]).then_inc(s_cum_masks, 16)
            sp.dma_start(pair_masks[:], G["pair_masks"]).then_inc(s_ssd_consts, 16)
            sp.dma_start(w_out[:], G["w_out"].rearrange("(j p) n -> p j n", p=P)).then_inc(s_ssd_consts, 16)

        def split_lo(eng, k):
            eng.wait_ge(s_w_hi, k + 1)
            return eng.tensor_tensor(w_lo[:, k, :], w_raw[:, k, :], w_hi[:, k, :], ALU.subtract)

        @block.gpsimd
        def _(pool):
            pool.memset(norm.half_power[:], -0.5).then_inc(s_half, 1)
            pool.wait_ge(s_half, 1)
            norm.pool_rstd(pool, 0, TILES)
            split_lo(pool, 0).then_inc(s_w_lo[0], 1)
            pool.wait_ge(s_w_lo[0], 1)

        @block.scalar
        def _(act):
            for k in range(KT):
                act.wait_ge(s_w[k], 16)
                act.activation(w_hi[:, k, :], w_raw[:, k, :], ACT.Copy).then_inc(s_w_hi, 1)
            act.wait_ge(s_small, 16 * SMALL)
            act.activation(a_exp[:], a_log[:], ACT.Exp).then_inc(s_dt, 1)
            ln.scalar_hi(act, xt_hi)

            def first_tap(u):
                fb, h = u % CONV_BLOCKS, u // CONV_BLOCKS
                act.wait_ge(s_mm, u + 1)
                act.activation(xbc[:, fb, HALF * h:HALF * h + HALF], mm_bank(u)[:], ACT.Copy,
                               scale=conv_w[:, fb, TAPS - 1:TAPS]).then_inc(s_tap0, 1)

            def silu_x(u):
                fb, h = u % CONV_BLOCKS, u // CONV_BLOCKS
                act.wait_ge(s_taps, 3 * (u + 1))
                act.activation(xbc[:, fb, HALF * h:HALF * h + HALF], xbc[:, fb, HALF * h:HALF * h + HALF],
                               ACT.Silu).then_inc(s_silu, 1)

            def silu_z(i):
                act.wait_ge(s_z_mm, i + 1)
                act.activation(zs[:, i, :], z_bank(i)[:], ACT.Silu).then_inc(s_z, 1)

            first_tap(0)
            act.wait_ge(s_dt, 2)
            act.activation(dt_e[:], dt_v[:], ACT.Abs).then_inc(s_dt, 1)
            act.wait_ge(s_dt, 3)
            act.activation(dt_e[:], dt_e[:], ACT.Exp, scale=-1.0).then_inc(s_dt, 1)
            first_tap(1)
            act.wait_ge(s_dt, 4)
            act.activation(dt_l[:], dt_e[:], ACT.Ln, bias=1.0).then_inc(s_dt, 1)
            for u in range(2, UNITS):
                first_tap(u)
                silu_x(u - 2)
                if 1 <= u - 2 <= TILES:
                    silu_z(u - 3)

            def factor(m):
                act.wait_ge(s_cum, m + 1)
                dst = (fs, fl)[m // SIDES]
                act.activation(dst[:, m % SIDES, :, :].rearrange("p t h -> p (t h)"), bank[m % 4][:],
                               ACT.Exp).then_inc(s_fac, 1)

            for m in range(SIDES):
                factor(m)
            silu_x(UNITS - 2)
            silu_x(UNITS - 1)
            for m in range(SIDES, 2 * SIDES):
                factor(m)

        @block.tensor
        def _(pe):
            pe.wait_ge(G["s_ident"], 16)
            ln.tensor(pe)
            for k in range(KT):
                pe.wait_ge(s_w_lo[k], 1)
            for i in range(TILES):
                pe.wait_ge(ln.s_lo, 2 * (i // 4 + 1))
                t = slice(P * i, P * i + P)
                for k in range(KT):
                    m = three_products(pe, bank[7][:, HEADS * i:HEADS * i + HEADS], xt_hi[:, k, t], xt_lo[:, k, t],
                                       w_hi[:, k, DT0:D_IN], w_lo[:, k, DT0:D_IN], k == 0, k == KT - 1)
            m.then_inc(s_dt_mm, 1)

            def project_xbc(u):
                fb, h = u % CONV_BLOCKS, u // CONV_BLOCKS
                if u >= 3:
                    pe.wait_ge(s_taps, 3 * (u - 2))
                for k in range(KT):
                    c = slice(X0 + P * fb, X0 + P * fb + P)
                    t = slice(HALF * h, HALF * h + HALF)
                    m = three_products(pe, mm_bank(u)[:], w_hi[:, k, c], w_lo[:, k, c], xt_hi[:, k, t],
                                       xt_lo[:, k, t], k == 0, k == KT - 1)
                m.then_inc(s_mm, 1)

            def project_z(i):
                if i >= 3:
                    pe.wait_ge(s_z, i - 2)
                t = slice(P * i, P * i + P)
                for k in range(KT):
                    m = three_products(pe, z_bank(i)[:], xt_hi[:, k, t], xt_lo[:, k, t], w_hi[:, k, Z0:Z0 + HID],
                                       w_lo[:, k, Z0:Z0 + HID], k == 0, k == KT - 1)
                m.then_inc(s_z_mm, 1)

            for u in range(UNITS):
                project_xbc(u)
                if 1 <= u <= TILES:
                    project_z(u - 1)
            pe.wait_ge(s_cum_masks, 16)
            pe.wait_ge(s_dt, 7)
            pe.wait_ge(s_z, TILES)
            for m in range(2 * SIDES):
                if m >= 4:
                    pe.wait_ge(s_fac, m - 3)
                pe.matmul(bank[m % 4][:], cum_masks[:, m, :], d_a[:].rearrange("p t h -> p (t h)"),
                          start=True, stop=True).then_inc(s_cum, 1)

        @block.vector
        def _(dve):
            for i in range(TILES):
                dve.wait_ge(s_x[i // 2], 16)
                norm.vector_stats(dve, i)
            for i in range(TILES):
                norm.vector_mean_var(dve, i)
            for i in range(TILES):
                norm.vector_normalize(dve, i, 1)
            split_lo(dve, 1).then_inc(s_w_lo[1], 1)
            ln.vector_lo(dve, xt_hi, xt_lo)
            dve.wait_ge(s_dt_mm, 1)
            dve.wait_ge(s_dt, 1)
            dve.tensor_tensor(dt_v[:], bank[7][:].rearrange("p (t h) -> p t h", h=HEADS),
                              bc(dt_bias[:], 1, TILES), ALU.add).then_inc(s_dt, 1)
            for u in range(UNITS):
                fb, h = u % CONV_BLOCKS, u // CONV_BLOCKS
                dve.wait_ge(s_tap0, u + 1)
                src = mm_bank(u)[:].rearrange("p (b s) -> p b s", s=SEQ)
                acc = xbc[:, fb, HALF * h:HALF * h + HALF].rearrange("p (b s) -> p b s", s=SEQ)
                for tap in range(1, TAPS):
                    if tap > 1:
                        dve.wait_ge(s_taps, 3 * u + tap - 1)
                    dve.scalar_tensor_tensor(acc[:, :, tap:], src[:, :, :SEQ - tap],
                                             conv_w[:, fb, TAPS - 1 - tap:TAPS - tap], acc[:, :, tap:],
                                             ALU.mult, ALU.add).then_inc(s_taps, 1)
                if u == 1:
                    dve.wait_ge(s_dt, 5)
                    dve.scalar_tensor_tensor(dt[:], dt_v[:], 0.0, dt_l[:], ALU.max, ALU.add).then_inc(s_dt, 1)
                if u == 2:
                    dve.wait_ge(s_dt, 6)
                    dve.scalar_tensor_tensor(d_a[:], dt[:], -1.0, bc(a_exp[:], 1, TILES), ALU.mult,
                                             ALU.mult).then_inc(s_dt, 1)
            dve.wait_ge(s_dt, 7)
            dtf = dt[:].rearrange("p t h -> p (t h)")
            for k in range(SIDES):
                dve.wait_ge(s_fac, k + 1)
                f = fs[:, k, :, :].rearrange("p t h -> p (t h)")
                dve.tensor_tensor(f, f, dtf, ALU.mult).then_inc(s_fs, 1)
            dve.wait_ge(s_fs, SIDES)

def mamba_scan(nc, G, kit, x, bank, ident, xbc, zs, dt, fs, fl, d_skip, norm_w, w_out, pair_masks,
               s_ssd_consts):
    BUFS = 6
    ADD_LAG = 3
    x_tok = kit.sb("x_tok", [P, 2, HID])
    scaled = kit.sb("scaled_x", [P, 2, SIDES, HID])
    g_all = kit.sb("g_scores", [P, 3, SEQ])
    g_masked = kit.sb("g_masked", [P, 2, LEVELS, P])
    g_diag = kit.sb("g_diag", [P, TILES])
    junk = kit.sb("diag_products", [P, 2, P])
    coef = kit.sb("diag_coef", [P, 2, HEADS])
    terms = kit.sb("terms", [P, BUFS, HID])
    y = kit.sb("y", [P, TILES, HID])
    square = kit.sb("squares", [P, 2, HID])
    mean_sq = kit.sb("sum_squares", [P, TILES])
    mean_eps = kit.sb("mean_squares_eps", [P, TILES])
    half_power = G["norm"][3]
    rstd = kit.sb("rms_rstd", [P, TILES])
    yt = kit.sb("y_turned", [P, 2, XB, P])
    s_xt = kit.sem("x_turned")
    s_xtok = kit.sem("x_tok_done")
    s_g = kit.sem("g_done")
    s_gs = kit.sem("g_saved")
    s_gm = kit.sem("g_masked_done")
    s_gd = kit.sem("g_diag_done")
    s_coef = kit.sem("coef_done")
    s_scaled = kit.sem("x_scaled")
    s_lvl = kit.sem("level_product_done")
    s_term = kit.sem("term_done")
    s_y = kit.sem("y_added")
    s_acc = kit.sem("term_accumulated")
    s_sum = kit.sem("y_summed")
    s_gate = kit.sem("y_gated")
    s_sq = kit.sem("squares_done")
    norm = Norm(kit, "moe0_norm", G)
    s_wout = kit.sem("w_out_scaled")
    s_mean = kit.sem("mean_squares_done")
    s_rms = kit.sem("rms_rstd_done")
    s_yt = kit.sem("y_turned_done")
    s_yts = kit.sem("y_turned_saved")
    s_out = kit.sem("out_projected")
    s_res = kit.sem("residual_added")

    products = []
    for i in range(TILES):
        levels = ([LEVELS] if i % 2 else []) + list(range(LEVELS))
        products += [(i, k, place) for place, k in enumerate(levels)]
    ON_PE = (2, 3, 4)
    last = {i: n for n, (i, k, place) in enumerate(products)}
    y_count, acc_count = {}, {}
    start_count = {}
    ys = accs = 0
    for n, (i, k, place) in enumerate(products):
        if place == 0:
            ys += 1
            start_count[i] = ys
        if place in ON_PE:
            accs += 1
        else:
            ys += 1
        y_count[n], acc_count[n] = ys, accs

    def scaled_count(i, k):
        return 8 * i - i // 2 + k + 1

    def wait_consumed(eng, n):
        if products[n][2] in ON_PE:
            eng.wait_ge(s_acc, acc_count[n])
        else:
            eng.wait_ge(s_y, y_count[n])

    def by_head(ap):
        return ap.rearrange("p (h e) -> p h e", e=HEAD_DIM)

    with nc.Block() as block:
        @block.sync
        def _(sp):
            G["next_loads"].start(sp)

        @block.tensor
        def _(pe):
            
            def turn(i):
                if i >= 1:
                    pe.wait_ge(s_xtok, i)
                for j in range(XB):
                    m = pe.transpose(bank[4][:, P * j:P * j + P], xbc[:, j, P * i:P * i + P], ident)
                m.then_inc(s_xt, 1)
                if i >= 1:
                    pe.wait_ge(s_gs, i)
                n = SEQ if i % 2 == 0 else P
                pe.matmul(bank[5][:, 0:n], xbc[:, XB, P * i:P * i + P], xbc[:, XB + 1, P * i:P * i + n],
                          start=True, stop=True).then_inc(s_g, 1)

            def accumulate(n):
                i, k, place = products[n]
                if place == ON_PE[0] and i >= 1:
                    pe.wait_ge(s_sum, i)
                pe.wait_ge(s_term, n + 1)
                pe.matmul(bank[6][:], ident, terms[:, n % BUFS, :], start=(place == ON_PE[0]),
                          stop=(place == ON_PE[-1])).then_inc(s_acc, 1)

            def turn_y(i):
                pe.wait_ge(s_gate, i + 1)
                if i >= 1:
                    pe.wait_ge(s_yts, i)
                for j in range(XB):
                    m = pe.transpose(bank[3][:, P * j:P * j + P], y[:, i, P * j:P * j + P], ident)
                m.then_inc(s_yt, 1)

            def project(i):
                pe.wait_ge(s_yts, i + 1)
                if i == 0:
                    pe.wait_ge(s_wout, 1)
                else:
                    pe.wait_ge(s_res, i)
                for j in range(XB):
                    m = pe.matmul(bank[7][:, 0:DIM], yt[:, i % 2, j, :], w_out[:, j, :], start=(j == 0),
                                  stop=(j == XB - 1))
                m.then_inc(s_out, 1)

            turn(0)
            turn(1)
            for n, (i, k, place) in enumerate(products):
                if n >= 3:
                    pe.wait_ge(s_term, n - 2)
                if k < LEVELS:
                    if k == 0:
                        pe.wait_ge(s_gm, 2 * i + 1)
                    if k == 4:
                        pe.wait_ge(s_gm, 2 * i + 2)
                    pe.wait_ge(s_scaled, scaled_count(i, k))
                    weights, moving = g_masked[:, i % 2, k, :], scaled[:, i % 2, k, :]
                else:
                    pe.wait_ge(s_scaled, scaled_count(i - 1, k))
                    pe.wait_ge(s_gs, i)
                    weights, moving = g_all[:, (i - 1) % 3, P:SEQ], scaled[:, 0, LEVELS, :]
                pe.matmul(bank[n % 3][:], weights, moving, start=True, stop=True).then_inc(s_lvl, 1)
                if n >= ADD_LAG and products[n - ADD_LAG][2] in ON_PE:
                    accumulate(n - ADD_LAG)
                if place == 4 and i + 2 < TILES:
                    turn(i + 2)
                if place == 6 and i >= 1:
                    turn_y(i - 1)
                if place == 2 and i >= 2:
                    project(i - 2)
            turn_y(TILES - 1)
            project(TILES - 2)
            project(TILES - 1)

        @block.scalar
        def _(act):

            def save_turned(i):
                act.wait_ge(s_xt, i + 1)
                if i >= 2:
                    act.wait_ge(s_scaled, scaled_count(i - 2, LEVELS - 1 if i % 2 else LEVELS))
                    act.wait_ge(s_y, start_count[i - 2])
                act.activation(x_tok[:, i % 2, :], bank[4][:], ACT.Copy).then_inc(s_xtok, 1)
                n = SEQ if i % 2 == 0 else P
                act.wait_ge(s_g, i + 1)
                if i >= 3:
                    act.wait_ge(s_gm, 2 * (i - 2))
                    act.wait_ge(s_gd, i - 2)
                    act.wait_ge(s_lvl, last[i - 3] + 2)
                act.activation(g_all[:, i % 3, 0:n], bank[5][:, 0:n], ACT.Copy).then_inc(s_gs, 1)

            def squares(i):
                act.wait_ge(s_gate, i + 1)
                if i >= 2:
                    act.wait_ge(s_sq, i - 1)
                act.activation(square[:, i % 2, :], y[:, i, :], ACT.Square,
                               accum_out=mean_sq[:, i:i + 1]).then_inc(s_sq, 1)

            def save_y(i):
                act.wait_ge(s_yt, i + 1)
                if i >= 2:
                    act.wait_ge(s_out, i - 1)
                act.activation(yt[:, i % 2].rearrange("p j t -> p (j t)"), bank[3][:], ACT.Copy).then_inc(s_yts, 1)

            save_turned(0)
            save_turned(1)
            for i in range(TILES + 1):
                if i >= 1:
                    squares(i - 1)
                if i + 2 < TILES:
                    save_turned(i + 2)
                if i >= 1:
                    save_y(i - 1)

        @block.vector
        def _(dve):

            def scale(i, k):
                if k == 0:
                    dve.wait_ge(s_xtok, i + 1)
                dve.tensor_tensor(by_head(scaled[:, i % 2, k, :]), by_head(x_tok[:, i % 2, :]),
                                  bc(fs[:, k, i, :], 2, HEAD_DIM), ALU.mult).then_inc(s_scaled, 1)

            def diag(i):
                dve.wait_ge(s_gs, i + 1)
                if i >= 2:
                    dve.wait_ge(s_gd, i - 1)
                dve.tensor_tensor_reduce(junk[:, i % 2, :], g_all[:, i % 3, 0:P], ident, 1.0, 0.0, ALU.mult,
                                         ALU.add, g_diag[:, i:i + 1]).then_inc(s_gd, 1)
                dve.wait_ge(s_gd, i + 1)
                if i >= 2:
                    dve.wait_ge(s_y, start_count[i - 2])
                dve.scalar_tensor_tensor(coef[:, i % 2, :], dt[:, i, :], g_diag[:, i:i + 1], d_skip[:], ALU.mult,
                                         ALU.add).then_inc(s_coef, 1)

            def add_accumulated(i):
                dve.wait_ge(s_acc, acc_count[last[i]])
                dve.wait_ge(s_y, y_count[last[i]])
                dve.tensor_tensor(y[:, i, :], y[:, i, :], bank[6][:], ALU.add).then_inc(s_sum, 1)

            def residual(i):
                dve.wait_ge(s_out, i + 1)
                dve.wait_ge(s_rms, i + 1)
                dve.scalar_tensor_tensor(x[:, i, :], bank[7][:, 0:DIM], rstd[:, i:i + 1], x[:, i, :], ALU.mult,
                                         ALU.add).then_inc(s_res, 1)
                dve.wait_ge(s_res, i + 1)
                norm.vector_stats(dve, i)
                norm.vector_mean_var(dve, i)

            for k in range(SIDES):
                scale(0, k)
            diag(0)
            for n, (i, k, place) in enumerate(products):
                dve.wait_ge(s_lvl, n + 1)
                if n >= BUFS:
                    wait_consumed(dve, n - BUFS)
                dve.tensor_tensor(by_head(terms[:, n % BUFS, :]), by_head(bank[n % 3][:]),
                                  bc(fl[:, k, i, :], 2, HEAD_DIM), ALU.mult).then_inc(s_term, 1)
                if i + 1 < TILES:
                    scale(i + 1, place)
                    if place == 1:
                        diag(i + 1)
                if place == 3 and i >= 1:
                    add_accumulated(i - 1)
                if place == 5 and i >= 2:
                    residual(i - 2)
                if place == 1 and i >= 3:
                    norm.vector_normalize(dve, i - 3, i - 2)
            add_accumulated(TILES - 1)
            residual(TILES - 2)
            norm.vector_normalize(dve, TILES - 3, TILES - 2)
            residual(TILES - 1)
            norm.vector_normalize(dve, TILES - 2, TILES - 1)
            norm.vector_normalize(dve, TILES - 1, TILES)
            dve.wait_ge(norm.s_xn, TILES)

        @block.gpsimd
        def _(pool):
            def mask(i, part):
                lo, hi = ((0, 4), (4, LEVELS))[part]
                pool.wait_ge(s_gs, i + 1)
                if i >= 2:
                    pool.wait_ge(s_lvl, last[i - 2] + 1)
                pool.tensor_tensor(g_masked[:, i % 2, lo:hi, :], pair_masks[:, lo:hi, :],
                                   bc(g_all[:, i % 3, 0:P], 1, hi - lo), ALU.mult).then_inc(s_gm, 1)

            def gate(i):
                pool.wait_ge(s_sum, i + 1)
                pool.tensor_tensor(y[:, i, :], y[:, i, :], zs[:, i, :], ALU.mult).then_inc(s_gate, 1)

            def rms(i):
                pool.wait_ge(s_sq, i + 1)
                pool.tensor_scalar(mean_eps[:, i:i + 1], mean_sq[:, i:i + 1], 1.0 / HID, EPS, ALU.mult,
                                   ALU.add).then_inc(s_mean, 1)
                pool.wait_ge(s_mean, i + 1)
                pool.tensor_tensor(rstd[:, i:i + 1], mean_eps[:, i:i + 1], half_power[:, i:i + 1],
                                   ALU.pow).then_inc(s_rms, 1)

            pool.wait_ge(s_ssd_consts, 32)
            mask(0, 0)
            mask(0, 1)
            pool.tensor_tensor(w_out[:], w_out[:], bc(norm_w[:], 2, DIM), ALU.mult).then_inc(s_wout, 1)
            for n, (i, k, place) in enumerate(products):
                if place == 0:
                    pool.wait_ge(s_coef, i + 1)
                    pool.tensor_tensor(by_head(y[:, i, :]), by_head(x_tok[:, i % 2, :]),
                                       bc(coef[:, i % 2, :], 2, HEAD_DIM), ALU.mult).then_inc(s_y, 1)
                if place in (2, 4) and i + 1 < TILES:
                    mask(i + 1, place // 2 - 1)
                if place not in ON_PE:
                    pool.wait_ge(s_term, n + 1)
                    pool.wait_ge(s_y, y_count[n] - 1)
                    pool.tensor_tensor(y[:, i, :], y[:, i, :], terms[:, n % BUFS, :], ALU.add).then_inc(s_y, 1)
                if place == 4 and i >= 1:
                    gate(i - 1)
                if place == 6 and i >= 1:
                    rms(i - 1)
                    if i >= 2:
                        norm.pool_rstd(pool, i - 2, 1)
            gate(TILES - 1)
            rms(TILES - 1)
            norm.pool_rstd(pool, TILES - 2, 1)
            norm.pool_rstd(pool, TILES - 1, 1)


L0_FEATURES, L0_EXPERTS, L0_TOP = 176, 8, 2
L0_BLOCKS, L0_SCORED = 14, 11
L1_FEATURES, L1_EXPERTS, L1_TOP = 256, 16, 4
L1_BLOCKS = L1_EXPERTS * L1_FEATURES // P
ALPHA, LIMIT = 1.702, 7.0


class MoeLoads:

    def __init__(self, G, kit, layer):
        self.G, self.layer, self.name = G, layer, f"moe{layer}"
        E = L1_EXPERTS if layer else L0_EXPERTS
        self.r_raw = kit.sb(self.name + "_router", [P, KT, E])
        self.raw_gu = kit.sb(self.name + "_raw_gate_up", [P, 2, 512])
        self.raw_d = kit.sb(self.name + "_raw_down", [P, 2, DIM])
        if layer:
            self.r_bias = kit.sb("moe1_router_bias", [P, E])
            self.biases = kit.sb("moe1_biases", [P, 2, L1_BLOCKS])
            self.down_bias = kit.sb("moe1_down_bias", [E, DIM])
        self.s_small = kit.sem(self.name + "_small_loaded")
        self.s_raw_gu = [kit.sem(self.name + f"_raw_gate_up{p}_loaded") for p in range(2)]
        self.s_raw_d = [kit.sem(self.name + f"_raw_down{p}_loaded") for p in range(2)]

    def block(self, sp, b, par):
        return lambda: sp.dma_start(self.raw_gu[:, par, :], self.G[self.name + "_gate_up"][bass.ds(b * P, P), :]
                                    ).then_inc(self.s_raw_gu[par], 16), \
            lambda: sp.dma_start(self.raw_d[:, par, :], self.G[self.name + "_down"][bass.ds(b * P, P), :]
                                 ).then_inc(self.s_raw_d[par], 16)

    def start(self, sp):
        G = self.G
        sp.dma_start(self.r_raw[:], G[self.name + "_router"].rearrange("(k p) e -> p k e", p=P)
                     ).then_inc(self.s_small, 16)
        for b in range(2):
            for load in self.block(sp, b, b):
                load()
        if self.layer:
            sp.dma_start(self.r_bias[:], G["moe1_router_bias"].partition_broadcast(P)).then_inc(self.s_small, 16)
            sp.dma_start(self.biases[:], G["moe1_biases"]).then_inc(self.s_small, 16)
            sp.dma_start(self.down_bias[:], G["moe1_down_bias"]).then_inc(self.s_small, 16)


def moe(nc, G, layer, loads):
    clamped = layer == 1
    name = f"moe{layer}"
    E, TOP = (L1_EXPERTS, L1_TOP) if clamped else (L0_EXPERTS, L0_TOP)
    BLOCKS = L1_BLOCKS if clamped else L0_BLOCKS
    FEATURES = L1_FEATURES if clamped else L0_FEATURES
    x, bank, ident = G["x"], G["bank"], G["ident"]
    r_raw, raw_gu, raw_d = loads.r_raw, loads.raw_gu, loads.raw_d
    s_small, s_raw_gu, s_raw_d = loads.s_small, loads.s_raw_gu, loads.s_raw_d
    score_dram = nc.dram_tensor(name + "_scores_dram", (E, TOKENS), F32, kind="Internal").ap()
    with ExitStack() as stack:
        kit = Kit(nc, stack, G["semaphores"])
        xt_hi = kit.sb(name + "_xt_hi", [P, KT, TOKENS], F16)
        xt_lo = kit.sb(name + "_xt_lo", [P, KT, TOKENS], F16)
        gu_hi = kit.sb(name + "_gate_up_hi", [P, 2, 2, KT, P], F16)
        gu_lo = kit.sb(name + "_gate_up_lo", [P, 2, 2, KT, P], F16)
        d_hi = kit.sb(name + "_down_hi", [P, 2, DIM], F16)
        d_lo = kit.sb(name + "_down_lo", [P, 2, DIM], F16)
        scores = kit.sb(name + "_scores_spread", [P, BLOCKS if not clamped else E, TOKENS])
        r_hi = kit.sb(name + "_router_hi", [P, KT, E], F16)
        r_lo = kit.sb(name + "_router_lo", [P, KT, E], F16)
        logits = kit.sb(name + "_logits", [P, TILES, E])
        peak = kit.sb(name + "_peak", [P, TILES])
        weight = kit.sb(name + "_weight", [P, TILES, E])
        best = kit.sb(name + "_best_eight", [P, TILES, 8])
        above = kit.sb(name + "_above_bar", [P, TILES, E])
        count = kit.sb(name + "_above_count", [P, TILES])
        equal = kit.sb(name + "_at_bar", [P, 1, TILES, 2 * E])
        sums = kit.sb(name + "_at_bar_sums", [P, 2, TILES, 2 * E])
        total = kit.sb(name + "_total", [P, TILES])
        score_t = kit.sb(name + "_scores_turned", [E, TOKENS])
        gate = kit.sb(name + "_gate", [P, 2, HALF])
        hid = kit.sb(name + "_hidden", [P, 2, HALF])
        h_hi = kit.sb(name + "_hidden_hi", [P, 2, HALF], F16)
        h_lo = kit.sb(name + "_hidden_lo", [P, 2, HALF], F16)
        out_t = kit.sb(name + "_out_turned", [P, 2, TOKENS])
        if not clamped:
            act_out = kit.sb(name + "_activated", [P, 2, HALF])
        if clamped:
            sig = kit.sb(name + "_sigmoid", [P, 2, HALF])
            up = kit.sb(name + "_up", [P, 2, HALF])
            up_clipped = kit.sb(name + "_up_clipped", [P, 2, HALF])
            up_scored = kit.sb(name + "_up_scored", [P, 2, HALF])
            glu = kit.sb(name + "_glu", [P, 2, HALF])
            r_bias, biases, down_bias = loads.r_bias, loads.biases, loads.down_bias
        ln = TurnedNorm(kit, name + "_norm", G)
        norm = None if clamped else Norm(kit, "attention_norm", G)
        s_gu_hi = kit.sem(name + "_gate_up_hi_done")
        s_gu_lo = kit.sem(name + "_gate_up_lo_done")
        s_d_hi = kit.sem(name + "_down_hi_done")
        s_d_lo = kit.sem(name + "_down_lo_done")
        s_r_hi = kit.sem(name + "_router_hi_done")
        s_r_lo = kit.sem(name + "_router_lo_done")
        s_logits = kit.sem(name + "_logits_done")
        s_route = kit.sem(name + "_routing_step")
        s_zero = kit.sem(name + "_sums_cleared")
        s_exp = kit.sem(name + "_routing_exp_done")
        s_routed = kit.sem(name + "_routed")
        s_score_t = kit.sem(name + "_scores_turned_done")
        s_score_s = kit.sem(name + "_scores_saved")
        s_score_w = kit.sem(name + "_scores_written")
        s_spread = [kit.sem(name + f"_scores_spread_part{j}_done") for j in range(3)]
        s_gu_mm = kit.sem(name + "_gate_up_product_done")
        s_gate = kit.sem(name + "_gate_done")
        if clamped:
            s_up = kit.sem(name + "_up_done")
            s_clip = kit.sem(name + "_up_clipped_done")
            s_scored = kit.sem(name + "_up_scored_done")
            s_sig = kit.sem(name + "_sigmoid_done")
            s_glu = kit.sem(name + "_glu_done")
            s_turns = kit.sem(name + "_score_turn")
            s_act_turns = kit.sem(name + "_bias_turn")
            s_stored = kit.sem(name + "_output_stored")
        else:
            s_ones = kit.sem(name + "_ones_done")
            s_acted = kit.sem(name + "_activated_done")
        s_hid = kit.sem(name + "_hidden_done")
        s_h_hi = kit.sem(name + "_hidden_hi_done")
        s_h_lo = kit.sem(name + "_hidden_lo_done")
        s_down = kit.sem(name + "_down_product_done")
        s_out_s = kit.sem(name + "_out_saved")
        s_out_d = kit.sem(name + "_out_last_saved")
        s_out_t = kit.sem(name + "_out_turned_done")
        s_res = kit.sem(name + "_residual_added")
        SMALL = 4 if clamped else 1
        pieces = []
        if not clamped:
            for b in range(L0_SCORED):
                a = 0
                while a < P:
                    e = (P * b + a) // FEATURES
                    end = min(P, (e + 1) * FEATURES - P * b)
                    pieces.append((b, a, end, e))
                    a = end

        part_starts = (0, 2, 3)

        def part_of(b):
            return sum(b >= s for s in part_starts) - 1

        part_sizes = [sum(part_of(b) == j for b, _, _, _ in pieces) for j in range(3)]

        def block_stages(eng, stage, peeled=()):
            stage(0, 0, True, False)
            stage(1, 1, True, False)
            for b, step in enumerate(peeled, 2):
                step()
                stage(b, b % 2, False, False)
            with eng.Fori(2 if peeled else 1, BLOCKS // 2 - 1, 1) as i:
                stage(2 * i, 0, False, False)
                stage(2 * i + 1, 1, False, False)
            stage(BLOCKS - 2, 0, False, False)
            stage(BLOCKS - 1, 1, False, True)

        with nc.Block() as block:
            @block.sync
            def _(sp):
                def stage(b, par, first, last):
                    if first:
                        return
                    gate_up, down = loads.block(sp, b, par)
                    sp.wait_ge(s_gu_lo, b - 1)
                    gate_up()
                    sp.wait_ge(s_d_lo, b - 1)
                    down()

                def spread(parts):
                    for b, a, end, e in pieces:
                        if part_of(b) in parts:
                            sp.dma_start(scores[a:end, b, :], score_dram[e:e + 1, :].partition_broadcast(end - a)
                                         ).then_inc(s_spread[part_of(b)], 16)

                def spread_first():
                    sp.wait_ge(s_score_s, HALVES)
                    sp.dma_start(score_dram, score_t[:]).then_inc(s_score_w, 16)
                    sp.wait_ge(s_score_w, 16)
                    spread((0,))

                block_stages(sp, stage, (spread_first, lambda: spread((1, 2))))
                if not clamped:
                    G["next_loads"].start(sp)
                else:
                    for j in range(TILES // 2):
                        sp.wait_ge(s_res, j + 1)
                        sp.dma_start(G["out"][2 * P * j:2 * P * j + 2 * P, :].rearrange("(t p) d -> p t d", p=P),
                                     x[:, 2 * j:2 * j + 2, :]).then_inc(s_stored, 16)
                    sp.wait_ge(s_stored, 16 * (TILES // 2))

            @block.gpsimd
            def _(pool):
                pool.memset(equal[:], 0.0).then_inc(s_zero, 1)
                pool.memset(sums[:], 0.0).then_inc(s_zero, 1)
                if not clamped:
                    pool.memset(scores[:, L0_SCORED:BLOCKS, :], 1.0).then_inc(s_ones, 1)
                    pool.wait_ge(s_ones, 1)
                    pool.wait_ge(s_spread[0], 16 * part_sizes[0])

                def stage(b, par, first, last):
                    for h in range(HALVES):
                        u = 2 * b + h
                        later = not (first and par == 0)
                        pool.wait_ge(s_acted, u + 1)
                        if later:
                            pool.wait_ge(s_h_lo, u - 1)
                        row = scores[:, bass.ds(b, 1), HALF * h:HALF * h + HALF].squeeze(1)
                        pool.tensor_tensor(hid[:, h, :], act_out[:, h, :], row, ALU.mult).then_inc(s_hid, 1)

                if clamped:
                    def spread_expert(e):
                        pool.dma_start(scores[:, bass.ds(e, 1), :].squeeze(1),
                                       score_dram[bass.ds(e, 1), :].partition_broadcast(P)
                                       ).then_inc(s_spread[0], 16)

                    def pair(i, last=False):
                        pool.wait_ge(s_spread[0], 16 * (i + 1))
                        if not last:
                            spread_expert(i + 1)
                        for par in range(2):
                            for h in range(HALVES):
                                u = 4 * i + 2 * par + h
                                later = not (isinstance(i, int) and i == 0 and par == 0)
                                pool.wait_ge(s_clip, u + 1)
                                if later:
                                    pool.wait_ge(s_hid, u - 1)
                                pool.sem_inc(s_turns, 1)
                                row = scores[:, bass.ds(i, 1), HALF * h:HALF * h + HALF].squeeze(1)
                                pool.tensor_tensor(up_scored[:, h, :], up_clipped[:, h, :], row,
                                                   ALU.mult).then_inc(s_scored, 1)
                                pool.wait_ge(s_sig, u + 1)
                                pool.tensor_tensor(glu[:, h, :], gate[:, h, :], sig[:, h, :],
                                                   ALU.mult).then_inc(s_glu, 1)
                    pool.wait_ge(s_score_w, 16)
                    spread_expert(0)
                    pair(0)
                    with pool.Fori(1, E - 1, 1) as i:
                        pair(i)
                    pair(E - 1, last=True)
                else:
                    block_stages(pool, stage, (lambda: pool.wait_ge(s_spread[1], 16 * part_sizes[1]),
                                               lambda: pool.wait_ge(s_spread[2], 16 * part_sizes[2])))
                    for j in range(TILES // 2):
                        norm.pool_rstd(pool, 2 * j, 2)

            @block.scalar
            def _(act):
                act.wait_ge(s_small, 16 * SMALL)
                act.activation(r_hi[:], r_raw[:], ACT.Copy).then_inc(s_r_hi, 1)
                act.wait_ge(s_raw_gu[0], 16)
                act.activation(gu_hi[:, 0].rearrange("p g k f -> p (g k f)"), raw_gu[:, 0, :],
                               ACT.Copy).then_inc(s_gu_hi, 1)
                ln.scalar_hi(act, xt_hi)
                act.wait_ge(s_route, 2)
                act.activation(weight[:], weight[:], ACT.Exp).then_inc(s_exp, 1)
                for h in range(HALVES):
                    act.wait_ge(s_score_t, h + 1)
                    act.activation(score_t[:, HALF * h:HALF * h + HALF], bank[4 + h][0:E, :],
                                   ACT.Copy).then_inc(s_score_s, 1)

                def hidden_hi(u, h, later):
                    act.wait_ge(s_hid, u + 1)
                    if later:
                        act.wait_ge(s_down, u - 1)
                    act.activation(h_hi[:, h, :], hid[:, h, :], ACT.Copy).then_inc(s_h_hi, 1)

                def stage(b, par, first, last):
                    for h in range(HALVES):
                        u = 2 * b + h
                        later = not (first and par == 0)
                        if clamped:
                            act.wait_ge(s_gu_mm, u + 1)
                            if later:
                                act.wait_ge(s_clip, u - 1)
                            act.sem_inc(s_act_turns, 1)
                            act.activation(up[:, h, :], bank[2 * h + 1][:], ACT.Identity,
                                           bias=biases[:, 1, bass.ds(b, 1)]).then_inc(s_up, 1)
                            act.wait_ge(s_gate, u + 1)
                            if later:
                                act.wait_ge(s_glu, u - 1)
                            act.activation(sig[:, h, :], gate[:, h, :], ACT.Sigmoid, scale=ALPHA).then_inc(s_sig, 1)
                        if not (first and par == 0 and h == 0):
                            hidden_hi(u - 1, 1 - h, not (first and (par == 0 or h == 0)))
                        if not clamped:
                            act.wait_ge(s_gu_mm, u + 1)
                            if later:
                                act.wait_ge(s_acted, u - 1)
                            act.activation(gate[:, h, :], bank[2 * h][:], ACT.Silu).then_inc(s_gate, 1)
                        if h == 0 and not last:
                            act.wait_ge(s_raw_gu[1 - par], raw_loaded(b + 1, 1 - par))
                            act.wait_ge(s_gu_mm, 2 * b if not (first and par == 0) else 1)
                            act.activation(gu_hi[:, 1 - par].rearrange("p g k f -> p (g k f)"), raw_gu[:, 1 - par, :],
                                           ACT.Copy).then_inc(s_gu_hi, 1)
                        if h == 0:
                            act.wait_ge(s_raw_d[par], raw_loaded(b, par))
                            if not first:
                                act.wait_ge(s_down, 2 * b - 2)
                            act.activation(d_hi[:, par, :], raw_d[:, par, :], ACT.Copy).then_inc(s_d_hi, 1)

                def raw_loaded(b, par):
                    return 8 * (b - par) + 16

                block_stages(act, stage)
                hidden_hi(2 * BLOCKS - 1, 1, True)
                act.wait_ge(s_down, 2 * BLOCKS - 1)
                for o in range(2):
                    act.activation(out_t[:, o, 0:HALF], bank[4 + 2 * o][:], ACT.Copy).then_inc(s_out_s, 1)
                act.wait_ge(s_down, 2 * BLOCKS)
                act.activation(out_t[:, 0, HALF:TOKENS], bank[5][:], ACT.Copy).then_inc(s_out_s, 1)

            @block.vector
            def _(dve):
                dve.wait_ge(s_r_hi, 1)
                dve.tensor_tensor(r_lo[:], r_raw[:], r_hi[:], ALU.subtract).then_inc(s_r_lo, 1)
                if clamped:
                    dve.tensor_scalar(biases[:, 1, :], biases[:, 1, :], 1.0, None, ALU.add).then_inc(s_r_lo, 1)
                ln.vector_lo(dve, xt_hi, xt_lo)
                dve.wait_ge(s_gu_hi, 1)
                dve.tensor_tensor(gu_lo[:, 0].rearrange("p g k f -> p (g k f)"), raw_gu[:, 0, :],
                                  gu_hi[:, 0].rearrange("p g k f -> p (g k f)"), ALU.subtract).then_inc(s_gu_lo, 1)
                n = 0

                def step(ins):
                    nonlocal n
                    n += 1
                    ins.then_inc(s_route, 1)
                    dve.wait_ge(s_route, n)

                dve.wait_ge(s_zero, 2)
                dve.wait_ge(s_logits, 1)
                lg = bank[4][:, 0:TILES * E].rearrange("p (t e) -> p t e", e=E)
                if clamped:
                    dve.tensor_tensor(logits[:], lg, bc(r_bias[:], 1, TILES), ALU.add).then_inc(s_routed, 1)
                else:
                    dve.tensor_copy(logits[:], lg).then_inc(s_routed, 1)
                dve.wait_ge(s_routed, 1)
                step(dve.tensor_reduce(peak[:], logits[:], AX.X, ALU.max))
                step(dve.tensor_tensor(weight[:], logits[:], bc(peak[:], 2, E), ALU.subtract))
                dve.wait_ge(s_exp, 1)
                ranked = logits
                if not clamped:
                    step(dve.tensor_reduce(total[:], weight[:], AX.X, ALU.add))
                    step(dve.reciprocal(total[:], total[:]))
                    step(dve.tensor_tensor(weight[:], weight[:], bc(total[:], 2, E), ALU.mult))
                    ranked = weight
                for i in range(TILES):
                    n += 1
                    dve.max(best[:, i, :], ranked[:, i, :]).then_inc(s_route, 1)
                dve.wait_ge(s_route, n)
                bar = best[:, :, TOP - 1:TOP].broadcast_to([P, TILES, E])
                step(dve.tensor_tensor(above[:], ranked[:], bar, ALU.is_gt))
                step(dve.tensor_reduce(count[:], above[:], AX.X, ALU.add))
                step(dve.tensor_tensor(equal[:, 0, :, E:], ranked[:], bar, ALU.is_equal))
                shift, side = 1, 0
                while shift < E:
                    src, dst = sums[:, side], sums[:, 1 - side]
                    if shift == 1:
                        src = equal[:, 0]
                    step(dve.tensor_tensor(dst[:, :, E:], src[:, :, E:], src[:, :, E - shift:2 * E - shift], ALU.add))
                    shift, side = 2 * shift, 1 - side
                taken = sums[:, 1 - side, :, E:]
                step(dve.tensor_tensor(taken, sums[:, side, :, E:], bc(count[:], 2, E), ALU.add))
                step(dve.scalar_tensor_tensor(taken, taken, float(TOP), equal[:, 0, :, E:], ALU.is_le, ALU.mult))
                step(dve.tensor_tensor(above[:], above[:], taken, ALU.add))
                step(dve.tensor_tensor(weight[:], above[:], weight[:], ALU.mult))
                step(dve.tensor_reduce(total[:], weight[:], AX.X, ALU.add))
                if not clamped:
                    step(dve.tensor_scalar(total[:], total[:], 1e-20, None, ALU.add))
                step(dve.reciprocal(total[:], total[:]))
                dve.tensor_tensor(weight[:], weight[:], bc(total[:], 2, E), ALU.mult).then_inc(s_routed, 1)

                def norm_pair(j):
                    dve.wait_ge(s_res, j + 1)
                    norm.vector_stats(dve, 2 * j)
                    norm.vector_stats(dve, 2 * j + 1)
                    norm.vector_mean_var(dve, 2 * j)
                    norm.vector_mean_var(dve, 2 * j + 1)

                def hidden(u, h, later):
                    dve.wait_ge(s_glu, u + 1)
                    dve.wait_ge(s_scored, u + 1)
                    if later:
                        dve.wait_ge(s_h_lo, u - 1)
                    dve.tensor_tensor(hid[:, h, :], up_scored[:, h, :], glu[:, h, :], ALU.mult).then_inc(s_hid, 1)

                def hidden_lo(u, h):
                    dve.wait_ge(s_h_hi, u + 1)
                    dve.tensor_tensor(h_lo[:, h, :], hid[:, h, :], h_hi[:, h, :], ALU.subtract).then_inc(s_h_lo, 1)

                def stage(b, par, first, last):
                    for h in range(HALVES):
                        u = 2 * b + h
                        later = not (first and par == 0)
                        if clamped:
                            dve.wait_ge(s_gu_mm, u + 1)
                            if later:
                                dve.wait_ge(s_glu, u - 1)
                            dve.tensor_scalar(gate[:, h, :], bank[2 * h][:], biases[:, 0, bass.ds(b, 1)], LIMIT, ALU.add,
                                              ALU.min).then_inc(s_gate, 1)
                            dve.wait_ge(s_up, u + 1)
                            if later:
                                dve.wait_ge(s_scored, u - 1)
                            dve.tensor_scalar(up_clipped[:, h, :], up[:, h, :], LIMIT + 1.0, 1.0 - LIMIT, ALU.min,
                                              ALU.max).then_inc(s_clip, 1)
                        some_before = not (first and par == 0 and h == 0)
                        before_is_later = not (first and (par == 0 or h == 0))
                        if clamped and some_before:
                            hidden(u - 1, 1 - h, before_is_later)
                        if some_before:
                            hidden_lo(u - 1, 1 - h)
                        if h == 0 and not last:
                            dve.wait_ge(s_gu_hi, b + 2)
                            dve.tensor_tensor(gu_lo[:, 1 - par].rearrange("p g k f -> p (g k f)"), raw_gu[:, 1 - par, :],
                                              gu_hi[:, 1 - par].rearrange("p g k f -> p (g k f)"),
                                              ALU.subtract).then_inc(s_gu_lo, 1)
                        if not clamped:
                            dve.wait_ge(s_gate, u + 1)
                            if later:
                                dve.wait_ge(s_hid, u - 1)
                            dve.tensor_tensor(act_out[:, h, :], gate[:, h, :], bank[2 * h + 1][:],
                                              ALU.mult).then_inc(s_acted, 1)
                        if h == 0:
                            dve.wait_ge(s_d_hi, b + 1)
                            dve.tensor_tensor(d_lo[:, par, :], raw_d[:, par, :], d_hi[:, par, :],
                                              ALU.subtract).then_inc(s_d_lo, 1)

                block_stages(dve, stage)
                if clamped:
                    hidden(2 * BLOCKS - 1, 1, True)
                hidden_lo(2 * BLOCKS - 1, 1)
                dve.wait_ge(s_down, 2 * BLOCKS)
                dve.tensor_copy(out_t[:, 1, HALF:TOKENS], bank[7][:]).then_inc(s_out_d, 1)
                for j in range(TILES // 2):
                    if norm is not None and j >= 1:
                        norm_pair(j - 1)
                    dve.wait_ge(s_out_t, j + 1)
                    dve.tensor_tensor(x[:, 2 * j:2 * j + 2, :], x[:, 2 * j:2 * j + 2, :],
                                      bank[j][:].rearrange("p (t d) -> p t d", d=DIM), ALU.add).then_inc(s_res, 1)
                if norm is not None:
                    norm_pair(TILES // 2 - 1)
                    for i in range(TILES):
                        norm.vector_normalize(dve, i, i // 2 + 1)
                    dve.wait_ge(norm.s_xn, TILES)
                dve.wait_ge(s_res, TILES // 2)

            @block.tensor
            def _(pe):
                ln.tensor(pe)
                pe.wait_ge(s_r_lo, 2 if clamped else 1)
                for i in range(TILES):
                    pe.wait_ge(ln.s_lo, 2 * (i // 4 + 1))
                    t = slice(P * i, P * i + P)
                    for k in range(KT):
                        m = three_products(pe, bank[4][:, E * i:E * i + E], xt_hi[:, k, t], xt_lo[:, k, t],
                                           r_hi[:, k, :], r_lo[:, k, :], k == 0, k == KT - 1)
                m.then_inc(s_logits, 1)

                def gate_up(b, par, h, later):
                    u = 2 * b + h
                    pe.wait_ge(s_gu_lo, b + 1)
                    if later:
                        pe.wait_ge(s_gate if clamped else s_acted, u - 1)
                        if clamped:
                            pe.wait_ge(s_up, u - 1)
                    for g in range(2):
                        for k in range(KT):
                            t = slice(HALF * h, HALF * h + HALF)
                            m = three_products(pe, bank[2 * h + g][:], gu_hi[:, par, g, k, :], gu_lo[:, par, g, k, :],
                                               xt_hi[:, k, t], xt_lo[:, k, t], k == 0, k == KT - 1)
                    m.then_inc(s_gu_mm, 1)

                def down(b, par, h, first, last):
                    pe.wait_ge(s_h_lo, 2 * b + h + 1)
                    pe.wait_ge(s_d_lo, b + 1)
                    for o in range(2):
                        m = three_products(pe, bank[4 + 2 * o + h][:], d_hi[:, par, P * o:P * o + P],
                                           d_lo[:, par, P * o:P * o + P], h_hi[:, h, :], h_lo[:, h, :],
                                           first and not clamped, last, skip_group_check=True)
                    m.then_inc(s_down, 1)

                gate_up(0, 0, 0, False)
                gate_up(0, 0, 1, False)
                pe.wait_ge(s_routed, 2)
                for h in range(HALVES):
                    for i in range(4 * h, 4 * h + 4):
                        m = pe.transpose(bank[4 + h][0:E, P * (i % 4):P * (i % 4) + P], weight[:, i, :], ident)
                    m.then_inc(s_score_t, 1)
                pe.wait_ge(s_score_s, HALVES)
                if clamped:
                    for o in range(2):
                        for h in range(HALVES):
                            pe.matmul(bank[4 + 2 * o + h][:], down_bias[:, P * o:P * o + P],
                                      score_t[:, HALF * h:HALF * h + HALF], start=True, stop=False,
                                      skip_group_check=True)

                def turn(b, par, first):
                    for h in range(HALVES):
                        gate_up(b + 1, 1 - par, h, True)
                        down(b, par, h, first, False)

                turn(0, 0, True)
                with pe.Fori(1, BLOCKS // 2, 1) as i:
                    turn(2 * i - 1, 1, False)
                    turn(2 * i, 0, False)
                for h in range(HALVES):
                    down(BLOCKS - 1, 1, h, False, True)
                for i in range(TILES):
                    if i % 4 == 0:
                        pe.wait_ge(s_out_s, (2, 3)[i // 4])
                    if i == 4:
                        pe.wait_ge(s_out_d, 1)
                    for o in range(2):
                        c = DIM * (i % 2) + P * o
                        m = pe.transpose(bank[i // 2][:, c:c + P], out_t[:, o, P * i:P * i + P], ident)
                    if i % 2:
                        m.then_inc(s_out_t, 1)


BF16 = mybir.dt.bfloat16
ATT_HEADS, ATT_DIM = 16, 16
PAIRS = ATT_HEADS // 2
ROWS = 64
PEAK_ROW = 3 * ATT_DIM
PEAK_SCALE = 64.0
V_COLS = 2 * ATT_DIM + 1
SCALE_ROOT = ATT_DIM ** -0.25
SPAN = 3 * P
BATCHES = TOKENS // SEQ
QKV = 3 * DIM


class AttentionLoads:

    def __init__(self, G, kit):
        self.G = G
        self.raw = kit.sb("w_qkv_raw", [P, KT, QKV])
        self.biases = kit.sb("qk_biases", [P, 2, KT])
        self.stack_bias = kit.sb("k_stack_bias", [P, 1])
        self.bv = kit.sb("bv_rows", [P, DIM])
        self.bo = kit.sb("bo_rows", [P, DIM])
        self.consts = kit.sb("attention_consts", [P, 7, P])
        self.w_o = kit.sb("w_o", [P, KT, DIM])
        self.s_w = kit.sem("w_qkv_loaded")
        self.s_small = kit.sem("attention_small_loaded")

    def start(self, sp):
        G, small = self.G, self.s_small
        sp.dma_start(self.raw[:], G["w_qkv"].rearrange("(k p) n -> p k n", p=P)).then_inc(self.s_w, 16)
        sp.dma_start(self.biases[:], G["qk_bias"]).then_inc(small, 16)
        sp.dma_start(self.stack_bias[:], G["k_stack_bias"]).then_inc(small, 16)
        sp.dma_start(self.bv[:], G["bv"].partition_broadcast(P)).then_inc(small, 16)
        sp.dma_start(self.bo[:], G["bo"].partition_broadcast(P)).then_inc(small, 16)
        sp.dma_start(self.consts[:], G["attention_consts"]).then_inc(small, 16)
        sp.dma_start(self.w_o[:], G["w_o"].rearrange("(k p) n -> p k n", p=P)).then_inc(small, 16)


def attention(nc, G, loads):
    with ExitStack() as stack:
        kit = Kit(nc, stack, G["semaphores"])
        A = {
            "q": kit.sb("q_stacks", [P, PAIRS, TOKENS], F16),
            "k": kit.sb("k_stacks", [P, ATT_HEADS, TOKENS], F16),
            "v": kit.sb("v_parts_and_ones", [P, TILES, ATT_HEADS, V_COLS], F16),
            "w_o_hi": kit.sb("w_o_hi", [P, KT, DIM], F16),
            "w_o_lo": kit.sb("w_o_lo", [P, KT, DIM], F16),
            "masks": kit.sb("attention_masks", [P, 3, P], BF16),
            "ident16": kit.sb("attention_identity16", [P, P], F16),
        }
        with ExitStack() as inner:
            attention_projections(nc, G, kit.part(inner), A, loads)
        with ExitStack() as inner:
            attention_heads(nc, G, kit.part(inner), A, loads)


def attention_projections(nc, G, kit, A, loads):
    x, bank, ident = G["x"], G["bank"], G["ident"]
    v, w_o_hi, w_o_lo, masks = A["v"], A["w_o_hi"], A["w_o_lo"], A["masks"]
    select = kit.sb("attention_selections", [P, 4, 4, P], F16)
    raw, biases, stack_bias, bv = loads.raw, loads.biases, loads.stack_bias, loads.bv
    consts, w_o, s_w, s_small = loads.consts, loads.w_o, loads.s_w, loads.s_small
    w_hi = kit.sb("w_qkv_hi", [P, KT, QKV], F16)
    w_lo = kit.sb("w_qkv_lo", [P, KT, QKV], F16)
    xt_hi = kit.sb("attention_xt_hi", [P, KT, TOKENS], F16)
    xt_lo = kit.sb("attention_xt_lo", [P, KT, TOKENS], F16)
    root_biases = kit.sb("qk_biases_scaled", [P, 2, KT])
    v_exact = kit.sb("v_float32", [P, TILES, ATT_HEADS, ATT_DIM])
    exact = kit.sb("qk_float32", [P, 2, HALF])
    qk_hi = kit.sb("qk_hi", [P, 2, KT, TOKENS], F16)
    qk_lo = kit.sb("qk_lo", [P, 2, KT, TOKENS], F16)
    ln = TurnedNorm(kit, "attention_norm", G)
    s_w_hi = kit.sem("w_qkv_hi_done")
    s_w_lo = kit.sem("w_qkv_lo_done")
    s_bias = kit.sem("qk_biases_done")
    s_const = kit.sem("attention_consts16_done")
    s_wo = kit.sem("w_o_split")
    s_mm = kit.sem("qkv_projected")
    s_exact = kit.sem("qk_float32_done")
    s_hi = kit.sem("qk_hi_done")
    s_lo = kit.sem("qk_lo_done")
    s_v = kit.sem("v_done")
    s_ones = kit.sem("v_ones_done")
    s_v_hi = kit.sem("v_hi_done")
    s_v_lo = kit.sem("v_lo_done")
    s_stacked = kit.sem("stack_selected")
    s_q = kit.sem("q_stack_saved")
    s_k = kit.sem("k_stack_saved")
    s_k_act = kit.sem("k_stack_saved_by_scalar")
    s_rest = kit.sem("k_stack_rest_cleared")
    s_zero = kit.sem("selections_cleared")
    UNITS = 2 * KT * HALVES
    STACKS = 2 * PAIRS * HALVES

    def unit(u):
        return u % 2, (u // 2) % KT, u // (2 * KT)

    def stack_unit(s):
        return s % 2, (s // 2) % PAIRS, s // (2 * PAIRS)

    def stack_bank(s):
        return bank[(4 + s) % 8]

    def by_scalar(m):
        return m % 8 in (1, 4, 7)

    def k_saved(m):
        mine = [j for j in range(m + 1) if by_scalar(j) == by_scalar(m)]
        return (s_k_act if by_scalar(m) else s_k), 2 * len(mine)

    def cols(h):
        return slice(HALF * h, HALF * h + HALF)

    with nc.Block() as block:
        @block.gpsimd
        def _(pool):
            def clear_rest(jj):
                r = slice(ROWS * (1 - jj), ROWS * (1 - jj) + ROWS)
                pool.memset(A["k"][r].rearrange("p (g j) t -> p g j t", j=2)[:, :, jj, :], 0.0).then_inc(s_rest, 1)

            pool.memset(v[:, :, :, 2 * ATT_DIM:V_COLS], 1.0).then_inc(s_ones, 1)
            pool.memset(select[:], 0.0).then_inc(s_zero, 1)
            pool.wait_ge(s_zero, 1)
            pool.wait_ge(s_small, 96)
            for j in range(4):
                r = slice(32 * j, 32 * j + 32)
                pool.tensor_copy(select[r, j], consts[r, 3:7, :]).then_inc(s_const, 1)
            pool.wait_ge(s_const, 4)
            pool.tensor_copy(A["ident16"][:], consts[:, 0, :]).then_inc(s_const, 1)
            pool.tensor_copy(masks[:], consts[:, 0:3, :]).then_inc(s_const, 1)
            pool.tensor_copy(w_o_hi[:], w_o[:]).then_inc(s_wo, 1)
            pool.wait_ge(s_wo, 1)
            pool.tensor_tensor(w_o_lo[:], w_o[:], w_o_hi[:], ALU.subtract).then_inc(s_wo, 1)
            pool.wait_ge(s_const, 6)
            pool.wait_ge(s_wo, 2)
            clear_rest(0)
            pool.wait_ge(s_rest, 1)
            for i in range(TILES):
                pool.wait_ge(s_v_hi, i + 1)
                pool.tensor_tensor(v[:, i, :, ATT_DIM:2 * ATT_DIM], v_exact[:, i], v[:, i, :, 0:ATT_DIM],
                                   ALU.subtract).then_inc(s_v_lo, 1)
            pool.wait_ge(s_v_lo, TILES)
            clear_rest(1)
            pool.wait_ge(s_rest, 2)

        @block.scalar
        def _(act):
            act.wait_ge(s_w, 16)
            for k in range(KT):
                act.activation(w_hi[:, k, :], raw[:, k, :], ACT.Copy).then_inc(s_w_hi, 1)
            act.wait_ge(s_small, 96)
            act.activation(root_biases[:], biases[:], ACT.Copy, scale=SCALE_ROOT).then_inc(s_bias, 1)
            ln.scalar_hi(act, xt_hi)
            act.wait_ge(s_bias, 1)
            for u in range(UNITS):
                which, g, h = unit(u)
                act.wait_ge(s_mm, u + 1)
                if u >= 2:
                    act.wait_ge(s_lo, u - 1)
                bias = root_biases[:, which, g:g + 1]
                act.activation(exact[:, u % 2, :], bank[4 + u % 4][:], ACT.Identity, bias=bias,
                               scale=SCALE_ROOT).then_inc(s_exact, 1)
                act.activation(qk_hi[:, which, g, cols(h)], bank[4 + u % 4][:], ACT.Identity, bias=bias,
                               scale=SCALE_ROOT).then_inc(s_hi, 1)
            for i in range(TILES):
                act.wait_ge(s_v, i + 1)
                act.activation(v[:, i, :, 0:ATT_DIM], v_exact[:, i], ACT.Copy).then_inc(s_v_hi, 1)
            for s in range(STACKS):
                which, pair, h = stack_unit(s)
                if which == 0:
                    act.wait_ge(s_stacked, s + 1)
                    act.activation(A["q"][:, pair, cols(h)], stack_bank(s)[:], ACT.Copy).then_inc(s_q, 1)
                elif by_scalar(s // 2):
                    act.wait_ge(s_stacked, s + 1)
                    for jj in range(2):
                        r = slice(ROWS * jj, ROWS * jj + ROWS)
                        act.activation(A["k"][r, 2 * pair + jj, cols(h)], stack_bank(s)[r], ACT.Identity,
                                       bias=stack_bias[r]).then_inc(s_k_act, 1)

        @block.vector
        def _(dve):
            for k in range(KT):
                dve.wait_ge(s_w_hi, k + 1)
                dve.tensor_tensor(w_lo[:, k, :], raw[:, k, :], w_hi[:, k, :], ALU.subtract).then_inc(s_w_lo, 1)
            ln.vector_lo(dve, xt_hi, xt_lo)
            for u in range(UNITS):
                which, g, h = unit(u)
                dve.wait_ge(s_exact, u + 1)
                dve.wait_ge(s_hi, u + 1)
                dve.tensor_tensor(qk_lo[:, which, g, cols(h)], exact[:, u % 2, :], qk_hi[:, which, g, cols(h)],
                                  ALU.subtract).then_inc(s_lo, 1)
            dve.wait_ge(s_small, 96)
            for i in range(TILES):
                dve.wait_ge(s_mm, UNITS + i + 1)
                dve.tensor_tensor(v_exact[:, i],
                                  bank[4 + i % 4][:, 0:DIM].rearrange("p (h d) -> p h d", d=ATT_DIM),
                                  bv[:].rearrange("p (h d) -> p h d", d=ATT_DIM), ALU.add).then_inc(s_v, 1)
            for s in range(1, STACKS, 2):
                _, pair, h = stack_unit(s)
                if by_scalar(s // 2):
                    continue
                dve.wait_ge(s_stacked, s + 1)
                for jj in range(2):
                    r = slice(ROWS * jj, ROWS * jj + ROWS)
                    dve.tensor_scalar(A["k"][r, 2 * pair + jj, cols(h)], stack_bank(s)[r], stack_bias[r], 1.0,
                                      ALU.add, ALU.mult).then_inc(s_k, 1)

        @block.tensor
        def _(pe):
            ln.tensor(pe)
            pe.wait_ge(s_w_lo, KT)
            for u in range(UNITS):
                which, g, h = unit(u)
                pe.wait_ge(ln.s_lo, 2 * (h + 1))
                if u >= 4:
                    pe.wait_ge(s_hi, u - 3)
                c = slice(DIM * which + P * g, DIM * which + P * g + P)
                for k in range(KT):
                    m = three_products(pe, bank[4 + u % 4][:], w_hi[:, k, c], w_lo[:, k, c],
                                       xt_hi[:, k, cols(h)], xt_lo[:, k, cols(h)], k == 0, k == KT - 1)
                m.then_inc(s_mm, 1)
            for i in range(TILES):
                if i < 4:
                    pe.wait_ge(s_hi, UNITS - 3 + i)
                else:
                    pe.wait_ge(s_v, i - 3)
                t = slice(P * i, P * i + P)
                c = slice(2 * DIM, QKV)
                for k in range(KT):
                    m = three_products(pe, bank[4 + i % 4][:, 0:DIM], xt_hi[:, k, t], xt_lo[:, k, t], w_hi[:, k, c],
                                       w_lo[:, k, c], k == 0, k == KT - 1)
                m.then_inc(s_mm, 1)
            pe.wait_ge(s_const, 6)
            pe.wait_ge(s_lo, UNITS)
            for s in range(STACKS):
                which, pair, h = stack_unit(s)
                if s < 4:
                    pe.wait_ge(s_v, TILES - 3 + s)
                elif s >= 8:
                    pe.wait_ge(*((s_q, s // 2 - 3) if which == 0 else k_saved(s // 2 - 4)))
                g, j = pair // 4, pair % 4
                out = stack_bank(s)[:]
                pe.matmul(out, select[:, j, 2 * which, :], qk_hi[:, which, g, cols(h)], start=True, stop=False)
                pe.matmul(out, select[:, j, 2 * which + 1, :], qk_lo[:, which, g, cols(h)], start=False,
                          stop=True).then_inc(s_stacked, 1)


def attention_heads(nc, G, kit, A, loads):
    x, bank, banks, ident = G["x"], G["bank"], G["banks"], G["ident"]
    q, k, v, w_o_hi, w_o_lo = A["q"], A["k"], A["v"], A["w_o_hi"], A["w_o_lo"]
    UNITS = BATCHES * PAIRS
    SET = 2
    SETS = UNITS // SET
    peaks = kit.sb("minus_peaks", [P, 2, 2, 2])
    peak_rows = kit.sb("peak_rows", [P, 2, 2, 2, ROWS], F16)
    probs = kit.sb("probs", [P, 2, 2, SPAN])
    probs_hi = kit.sb("probs_hi", [P, 3, 2, SPAN], F16)
    probs_lo = kit.sb("probs_lo", [P, 3, 2, SPAN], F16)
    sums = kit.sb("attended_and_sums", [P, 2, 2, 2 * SET, V_COLS])
    sum_parts = kit.sb("attended_parts_sum", [P, 2, 2, 2 * SET, ATT_DIM])
    inverse = kit.sb("inverse_sums", [P, 2, 2, 2 * SET, 1])
    attended = kit.sb("attended", [P, TILES, DIM])
    at_hi = kit.sb("attended_turned_hi", [P, KT, TOKENS], F16)
    at_lo = kit.sb("attended_turned_lo", [P, KT, TOKENS], F16)
    s_zero = kit.sem("peak_rows_cleared")
    s_bo = kit.sem("bo_added")
    s_s = kit.sem("scores_done")
    s_max = kit.sem("maximum_done")
    s_peak = kit.sem("peak_row_done")
    s_turn = kit.sem("peaks_turned")
    s_aug = kit.sem("q_augmented")
    s_st = kit.sem("turned_scores_done")
    s_hi = kit.sem("probs_hi_done")
    s_lo = kit.sem("probs_lo_done")
    s_pv = kit.sem("attended_done")
    s_copied = kit.sem("attended_copied")
    s_part = kit.sem("attended_part_taken")
    s_norm = kit.sem("attended_normed")
    s_at = kit.sem("attended_turned")
    s_at_hi = kit.sem("attended_hi_done")
    s_at_lo = kit.sem("attended_lo_done")
    s_out = kit.sem("attention_projected")
    s_res = kit.sem("attention_residual_added")
    norm = Norm(kit, "moe1_norm", G)
    ident_b, mask, mask_t = A["masks"][:, 0, :], A["masks"][:, 1, :], A["masks"][:, 2, :]
    ident16 = A["ident16"][:]

    def add_mask(pe, out_bank, m):
        out = banks[:, out_bank, 0:SPAN + P].rearrange("p (c n) -> p c n", n=P)[:, 0:3:2, :]
        return pe.matmul(out, ident_b, bc(m, 1, 2), start=False, stop=True, skip_group_check=True)

    with nc.Block() as block:
        @block.sync
        def _(sp):
            G["next_loads"].start(sp)

        @block.tensor
        def _(pe):
            def scores(n):
                b, pair = n // PAIRS, n % PAIRS
                if n >= 2:
                    pe.wait_ge(s_peak, n - 1)
                for jj in range(2):
                    bk = 2 * (n % 2) + jj
                    for qt in range(2):
                        queries = q[:, pair, SEQ * b + P * qt:SEQ * b + P * qt + P]
                        keys = k[:, 2 * pair + jj, SEQ * b:SEQ * b + P * (qt + 1)]
                        pe.matmul(banks[:, bk, P * qt:P * qt + P * (qt + 1)], queries, keys, start=(qt == 0),
                                  stop=False, skip_group_check=True)
                    m = add_mask(pe, bk, mask)
                m.then_inc(s_s, 1)

            def turn_peaks(n):
                pe.wait_ge(s_peak, n + 1)
                if n >= 1:
                    pe.wait_ge(s_aug, n)
                for qt in range(2):
                    m = pe.matmul(bank[7][:, P * qt:P * qt + P],
                                  peak_rows[:, n % 2, qt].rearrange("p j e -> p (j e)"), ident16,
                                  start=True, stop=True, skip_group_check=True)
                m.then_inc(s_turn, 1)

            def turned_scores(n):
                b, pair = n // PAIRS, n % PAIRS
                pe.wait_ge(s_aug, n + 1)
                for jj in range(2):
                    if n >= 1:
                        pe.wait_ge(s_hi, 2 * n - 1 + jj)
                    for kb in range(2):
                        keys = k[:, 2 * pair + jj, SEQ * b + P * kb:SEQ * b + P * kb + P]
                        queries = q[:, pair, SEQ * b + P * kb:SEQ * b + SEQ]
                        pe.matmul(banks[:, 4 + jj, SEQ * kb:SEQ + P * kb], keys, queries, start=(kb == 0),
                                  stop=False, skip_group_check=True)
                    add_mask(pe, 4 + jj, mask_t).then_inc(s_st, 1)

            def attend(n):
                b, pair = n // PAIRS, n % PAIRS
                s, w = n // SET, n % SET
                pe.wait_ge(s_lo, n + 1)
                if w == 0 and s >= 1:
                    pe.wait_ge(s_copied, s)
                for jj in range(2):
                    for qt in range(2):
                        c = V_COLS * (2 * SET * qt + 2 * w + jj)
                        for kb in range(qt + 1):
                            block_cols = slice(P * (qt + kb), P * (qt + kb) + P)
                            v_head = v[:, 2 * b + kb, 2 * pair + jj, :]
                            out = bank[6][:, c:c + V_COLS]
                            pe.matmul(out, probs_hi[:, n % 3, jj, block_cols], v_head, start=(kb == 0), stop=False)
                            m = pe.matmul(out, probs_lo[:, n % 3, jj, block_cols], v_head, start=False,
                                          stop=(kb == qt))
                m.then_inc(s_pv, 1)

            scores(0)
            scores(1)
            for n in range(UNITS + 3):
                if n < UNITS:
                    turn_peaks(n)
                if 1 <= n <= UNITS:
                    turned_scores(n - 1)
                if n + 2 < UNITS:
                    scores(n + 2)
                if n >= 3:
                    attend(n - 3)

        @block.gpsimd
        def _(pool):
            pool.memset(peak_rows[:], 0.0).then_inc(s_zero, 1)
            for n in range(UNITS):
                pool.wait_ge(s_hi, 2 * (n + 1))
                if n >= 3:
                    pool.wait_ge(s_pv, n - 2)
                pool.tensor_tensor(probs_lo[:, n % 3], probs[:, n % 2], probs_hi[:, n % 3],
                                   ALU.subtract).then_inc(s_lo, 1)
                if n % 3 == 2 and n // 3 < TILES:
                    pool.tensor_tensor(x[:, n // 3, :], x[:, n // 3, :], loads.bo[:], ALU.add).then_inc(s_bo, 1)
            pool.wait_ge(s_lo, UNITS)
            pool.wait_ge(s_bo, TILES)

        @block.scalar
        def _(act):
            def copy_outputs(s):
                act.wait_ge(s_pv, SET * (s + 1))
                if s >= 2:
                    act.wait_ge(s_part, 2 * (s - 1))
                act.activation(sums[:, s % 2].rearrange("p t h d -> p (t h d)"),
                               bank[6][:, 0:4 * SET * V_COLS], ACT.Copy).then_inc(s_copied, 1)

            for n in range(UNITS):
                if n >= 4 and n % 2 == 0:
                    copy_outputs((n - 4) // 2)
                for jj in range(2):
                    act.wait_ge(s_st, 2 * n + jj + 1)
                    if n >= 2:
                        act.wait_ge(s_lo, n - 1)
                    act.activation(probs[:, n % 2, jj], banks[:, 4 + jj, 0:SPAN], ACT.Exp)
                    if n >= 3:
                        act.wait_ge(s_pv, n - 2)
                    act.activation(probs_hi[:, n % 3, jj], banks[:, 4 + jj, 0:SPAN], ACT.Exp).then_inc(s_hi, 1)
            copy_outputs(SETS - 2)
            copy_outputs(SETS - 1)

        @block.vector
        def _(dve):
            dve.wait_ge(s_zero, 1)

            def peak(n):
                dve.wait_ge(s_s, n + 1)
                if n >= 2:
                    dve.wait_ge(s_peak, n - 1)
                for qt in range(2):
                    dve.tensor_reduce(peaks[:, n % 2, qt, :],
                                      banks[:, 2 * (n % 2):2 * (n % 2) + 2, P * qt:P * (2 * qt + 1)],
                                      AX.X, ALU.max, negate=True).then_inc(s_max, 1)
                dve.wait_ge(s_max, 2 * (n + 1))
                if n >= 2:
                    dve.wait_ge(s_turn, n - 1)
                dve.tensor_scalar(peak_rows[:, n % 2, :, :, PEAK_ROW:PEAK_ROW + 1].squeeze(3), peaks[:, n % 2],
                                  1.0 / PEAK_SCALE, 0.0, ALU.mult, ALU.add).then_inc(s_peak, 1)

            def augment(n):
                b, pair = n // PAIRS, n % PAIRS
                dve.wait_ge(s_turn, n + 1)
                rows = q[:, pair, SEQ * b:SEQ * b + SEQ].rearrange("p (t n) -> p t n", n=P)
                dve.tensor_tensor(rows, rows, bank[7][:, 0:SEQ].rearrange("p (t n) -> p t n", n=P),
                                  ALU.add).then_inc(s_aug, 1)

            def normalize(s):
                b, pair = s * SET // PAIRS, s * SET % PAIRS
                dve.wait_ge(s_copied, s + 1)
                out = sums[:, s % 2]
                dve.reciprocal(inverse[:, s % 2], out[:, :, :, 2 * ATT_DIM:V_COLS]).then_inc(s_part, 1)
                dve.tensor_tensor(sum_parts[:, s % 2], out[:, :, :, 0:ATT_DIM], out[:, :, :, ATT_DIM:2 * ATT_DIM],
                                  ALU.add).then_inc(s_part, 1)
                dve.wait_ge(s_part, 2 * (s + 1))
                c = 2 * ATT_DIM * pair
                dst = attended[:, 2 * b:2 * b + 2, c:c + 2 * ATT_DIM * SET].rearrange("p t (h d) -> p t h d", d=ATT_DIM)
                dve.tensor_tensor(dst, sum_parts[:, s % 2],
                                  inverse[:, s % 2].broadcast_to([P, 2, 2 * SET, ATT_DIM]),
                                  ALU.mult).then_inc(s_norm, 1)

            peak(0)
            for n in range(UNITS):
                if n + 1 < UNITS:
                    peak(n + 1)
                augment(n)
                if n >= 6 and n % 2 == 0:
                    normalize((n - 6) // 2)
            for s in range(SETS - 3, SETS):
                normalize(s)
            dve.wait_ge(s_norm, SETS)

    with nc.Block() as block:
        def turned_bank(g):
            return bank[g % 4]

        @block.tensor
        def _(pe):
            for g in range(HALVES * KT):
                for i in range(4):
                    m = pe.transpose(turned_bank(g)[:, P * i:P * i + P],
                                     attended[:, 4 * (g // KT) + i, P * (g % KT):P * (g % KT) + P], ident)
                m.then_inc(s_at, 1)
            for i in range(TILES):
                pe.wait_ge(s_at_lo, KT * (i // 4 + 1))
                if i >= 4:
                    pe.wait_ge(s_res, i - 3)
                t = slice(P * i, P * i + P)
                for kt in range(KT):
                    m = three_products(pe, bank[4 + i % 4][:, 0:DIM], at_hi[:, kt, t], at_lo[:, kt, t],
                                       w_o_hi[:, kt, :], w_o_lo[:, kt, :], kt == 0, kt == KT - 1)
                m.then_inc(s_out, 1)

        @block.scalar
        def _(act):
            for g in range(HALVES * KT):
                act.wait_ge(s_at, g + 1)
                act.activation(at_hi[:, g % KT, HALF * (g // KT):HALF * (g // KT) + HALF], turned_bank(g)[:],
                               ACT.Copy).then_inc(s_at_hi, 1)

        @block.vector
        def _(dve):
            for g in range(HALVES * KT):
                t = slice(HALF * (g // KT), HALF * (g // KT) + HALF)
                dve.wait_ge(s_at_hi, g + 1)
                dve.tensor_tensor(at_lo[:, g % KT, t], turned_bank(g)[:], at_hi[:, g % KT, t],
                                  ALU.subtract).then_inc(s_at_lo, 1)
            for i in range(TILES + 2):
                if i < TILES:
                    dve.wait_ge(s_out, i + 1)
                    dve.tensor_tensor(x[:, i, :], x[:, i, :], bank[4 + i % 4][:, 0:DIM], ALU.add).then_inc(s_res, 1)
                if 1 <= i <= TILES:
                    dve.wait_ge(s_res, i)
                    norm.vector_stats(dve, i - 1)
                if i >= 2:
                    norm.vector_mean_var(dve, i - 2)
                if i % 2 == 0 and i >= 6:
                    for j in (i - 6, i - 5):
                        norm.vector_normalize(dve, j, i // 2 - 2)
            for j in range(TILES - 4, TILES):
                norm.vector_normalize(dve, j, j // 2 + 1)
            dve.wait_ge(norm.s_xn, TILES)

        @block.gpsimd
        def _(pool):
            for j in range(TILES // 2):
                norm.pool_rstd(pool, 2 * j, 2)


def more_layout(i, a):
    moe_layout(i, a)
    attention_layout(i, a)


def run_stages(nc, G):
    with ExitStack() as stack:
        kit = Kit(nc, stack, [])
        moe0_loads = MoeLoads(G, kit, 0)
        stage_kit = Kit(nc, stack, G["semaphores"])
        G["next_loads"] = moe0_loads
        mamba(nc, G)
        attention_loads, moe1_loads = AttentionLoads(G, kit), MoeLoads(G, kit, 1)
        G["next_loads"] = attention_loads
        moe(nc, G, 0, moe0_loads)
        stage_kit.retire_semaphores()
        G["next_loads"] = moe1_loads
        attention(nc, G, attention_loads)
        moe(nc, G, 1, moe1_loads)


def build(nc, inputs, out):
    with ExitStack() as stack:
        kit = Kit(nc, stack, [])
        G = dict(inputs)
        G["x_in"] = inputs["x"]
        G["ident_in"] = inputs["ident"]
        G["out"] = out
        G["x"] = kit.sb("residual", [P, TILES, DIM])
        G["ident"] = kit.sb("identity", [P, P])[:]
        G["banks"] = stack.enter_context(nc.psum_tensor("banks", [P, 8, 512], F32))
        G["bank"] = [G["banks"][:, b, :] for b in range(8)]
        G["norm"] = [kit.sb("norm_stats", [P, TILES, 6]), kit.sb("norm_mean_var", [P, TILES, 2]),
                     kit.sb("norm_var_eps", [P, TILES]), kit.sb("minus_half", [P, TILES]),
                     kit.sb("norm_rstd", [P, TILES]), kit.sb("normed_x", [P, TILES, DIM])]
        G["semaphores"] = []
        G["s_ident"] = kit.sem("identity_loaded")
        run_stages(nc, G)


def level_masks():
    import numpy as np
    t = np.arange(P)
    cum = np.zeros((2, LEVELS + 1, P, P), np.float32)
    pair = np.zeros((LEVELS, P, P), np.float32)
    for k in range(LEVELS):
        half = 1 << k
        second = (t // half) % 2 == 1
        block = t // (2 * half)
        ref = block * 2 * half + half - 1
        r = t[:, None]
        cum[0, k] = (~second)[None] & (r > t[None]) & (r <= ref[None])
        cum[1, k] = second[None] & (r > ref[None]) & (r <= t[None])
        pair[k] = (~second)[:, None] & second[None] & (block[:, None] == block[None])
    cum[0, LEVELS] = t[:, None] > t[None]
    cum[1, LEVELS] = t[:, None] <= t[None]
    return cum.reshape(-1, P, P).transpose(1, 0, 2), pair.transpose(1, 0, 2)


def layout(i):
    import numpy as np
    cum, pair = level_masks()
    a = {
        "x": i["L0_attn_x"].reshape(TOKENS, DIM),
        "ident": np.eye(P, dtype=np.float32),
        "w_in": i["L0_attn_in_proj_w"].T,
        "conv_w": i["L0_attn_conv_w"],
        "dt_bias": i["L0_attn_dt_bias"],
        "A_log": i["L0_attn_A_log"],
        "D": i["L0_attn_D"],
        "norm_w": i["L0_attn_norm_w"].reshape(-1, P).T,
        "w_out": i["L0_attn_out_proj_w"].T,
        "cum_masks": cum,
        "pair_masks": pair,
    }
    more_layout(i, a)
    return a


def kernel(**inputs):
    import numpy as np
    import concourse.bacc as bacc
    from concourse.bass_utils import run_bass_kernel_spmd

    nc = bacc.Bacc("TRN2", target_bir_lowering=False, num_devices=1)
    arrays = {k + "_dram": np.ascontiguousarray(v) for k, v in layout({k: np.asarray(v) for k, v in inputs.items()}).items()}
    aps = {k[:-5]: nc.dram_tensor(k, v.shape, mybir.dt.from_np(v.dtype), kind="ExternalInput").ap()
           for k, v in arrays.items()}
    out = nc.dram_tensor("out_dram", (TOKENS, DIM), F32, kind="ExternalOutput").ap()
    build(nc, aps, out)
    result = run_bass_kernel_spmd(nc, [arrays], core_ids=[0])
    return result.results[0]["out_dram"].reshape(4, SEQ, DIM)


def moe_blocks(gate, up, down):
    import numpy as np
    n = -(-gate.shape[0] // (2 * P)) * 2 * P
    pad = lambda w: np.concatenate([w, np.zeros((n - w.shape[0], DIM), w.dtype)])
    gu = np.stack([pad(gate), pad(up)]).reshape(2, n // P, P, KT, P)
    return gu.transpose(1, 4, 0, 3, 2).reshape(n, 2 * KT * P), pad(down)


def moe_layout(i, a):
    import numpy as np
    cat = np.concatenate
    a["moe0_gate_up"], a["moe0_down"] = moe_blocks(
        cat([i["L0_ffn_expert_gate"].reshape(-1, DIM), i["L0_ffn_shared_gate"]]),
        cat([i["L0_ffn_expert_up"].reshape(-1, DIM), i["L0_ffn_shared_up"]]),
        cat([i["L0_ffn_expert_down"].transpose(0, 2, 1).reshape(-1, DIM), i["L0_ffn_shared_down"].T]))
    a["moe0_router"] = i["L0_ffn_gate_w"].T
    w = i["L1_ffn_gate_up_proj"]
    a["moe1_gate_up"], a["moe1_down"] = moe_blocks(
        w[:, :, 0::2].transpose(0, 2, 1).reshape(-1, DIM), w[:, :, 1::2].transpose(0, 2, 1).reshape(-1, DIM),
        i["L1_ffn_down_proj"].reshape(-1, DIM))
    a["moe1_router"] = i["L1_ffn_router_weight"].T
    a["moe1_router_bias"] = i["L1_ffn_router_bias"]
    a["moe1_biases"] = i["L1_ffn_gate_up_proj_bias"].reshape(-1, P, 2).transpose(1, 2, 0)
    a["moe1_down_bias"] = i["L1_ffn_down_proj_bias"]


def attention_layout(i, a):
    import numpy as np

    a["w_qkv"] = np.concatenate([i["L1_attn_Wq"], i["L1_attn_Wk"], i["L1_attn_Wv"]]).T
    a["qk_bias"] = np.stack([i["L1_attn_bq"].reshape(KT, P), i["L1_attn_bk"].reshape(KT, P)]).transpose(2, 0, 1)
    a["bv"] = i["L1_attn_bv"]
    a["bo"] = i["L1_attn_bo"]
    a["w_o"] = i["L1_attn_Wo"].T
    t = np.arange(P)
    above = np.where(t[None] > t[:, None], -1e30, 0.0)
    same_head = (t[:, None] // ATT_DIM) % 2 == t[None] // ROWS
    same_dim = t[:, None] % ATT_DIM == t[None] % ATT_DIM
    part = (t[None] % ROWS) // ATT_DIM
    hits = same_head & same_dim
    q_hi, q_lo = hits & (part < 2), hits & (part == 2)
    k_hi, k_lo = hits & (part % 2 == 0) & (part < 3), hits & (part == 1)
    a["attention_consts"] = np.stack([np.eye(P), above, above.T, q_hi, q_lo, k_hi, k_lo]).transpose(1, 0, 2).astype(
        np.float32)
    a["k_stack_bias"] = np.where(t % ROWS == PEAK_ROW, PEAK_SCALE, 0.0).astype(np.float32)[:, None]
```
